# Optimizing a Trainium2 kernel written in Bass

```python
import numpy as np
import jax
import jax.numpy as jnp

def _softmax(x, axis=-1):
    return jax.nn.softmax(x, axis=axis)

def _gelu(x):
    return jax.nn.gelu(x, approximate=True)

def _silu(x):
    return jax.nn.silu(x)

def _sigmoid(x):
    return jax.nn.sigmoid(x)

def _layernorm(x, axis=-1, eps=1e-05):
    m = jnp.mean(x, axis=axis, keepdims=True)
    v = jnp.var(x, axis=axis, keepdims=True)
    return (x - m) / jnp.sqrt(v + eps)

def _scatter_add(tgt, idx, src, axis=0):
    return tgt.at[idx].add(src)

def _segment_sum(src, seg, n):
    return jax.ops.segment_sum(src, seg, n)
kernel_name = 'mk_vit_tower_cls_d2_tok_img256_r4_d49b25'

def setup_inputs(seed: int=0):
    np.random.seed(seed)
    _w = jnp.asarray

    def _rec_inputs():
        import jax
        import jax.numpy as jnp
        _rk = jax.random.key(seed)
        x = -0.000222058 + 0.999998 * jax.random.normal(jax.random.fold_in(_rk, 1), (32, 3, 64, 64), jnp.float32)
        cls_tok = 0.02 * jax.random.normal(jax.random.fold_in(_rk, 5), (1, 1, 64), jnp.float32)
        return (x, cls_tok)
    x, cls_tok = _rec_inputs()

    def _L0_tok_setup():
        import jax, jax.numpy as jnp
        import numpy as np
        IMAGE_SIZE = 64
        PATCH = 16
        EMBED_DIM = 64
        IN_CH = 3
        BATCH = 128
        IN_DIM = IN_CH * PATCH * PATCH

        def _patchify(x, p):
            B, C, H, Wd = x.shape
            x = x.reshape(B, C, H // p, p, Wd // p, p)
            x = x.transpose(0, 2, 4, 1, 3, 5)
            return x.reshape(B, H // p * (Wd // p), C * p * p)
        key = jax.random.key(seed)
        kx, kw, kb = jax.random.split(key, 3)
        x = jax.random.normal(kx, (BATCH, IN_CH, IMAGE_SIZE, IMAGE_SIZE), dtype=jnp.float32)
        W = jax.random.normal(kw, (EMBED_DIM, IN_DIM), dtype=jnp.float32) * (1.0 / np.sqrt(IN_DIM))
        b = jax.random.normal(kb, (EMBED_DIM,), dtype=jnp.float32) * 0.01
        return {'x': x, 'W': W, 'b': b}
    _L0_tok_all = _L0_tok_setup()
    _L0_tok_in = {k: v for k, v in _L0_tok_all.items() if k in ('W', 'b')}
    del _L0_tok_all

    def _L0_attn_setup():
        import jax, jax.numpy as jnp
        import numpy as np
        BN_EPS = 1e-05
        key = jax.random.key(seed)
        ks = jax.random.split(key, 4)
        B, N, D = (8, 2048, 64)
        outD = 64
        s = 1.0 / np.sqrt(D)
        return {'feature': jax.random.normal(ks[0], (B, N, D), dtype=jnp.float32), 'W_qk': jax.random.normal(ks[1], (2, D, D), dtype=jnp.float32) * s, 'b_qk': jnp.zeros((2, D), dtype=jnp.float32), 'W_v': jax.random.normal(ks[2], (D, outD), dtype=jnp.float32) * s, 'b_v': jnp.zeros((outD,), dtype=jnp.float32), 'gamma': jnp.ones((D,), dtype=jnp.float32), 'beta': jnp.zeros((D,), dtype=jnp.float32)}
    _L0_attn_all = _L0_attn_setup()
    _L0_attn_in = {k: v for k, v in _L0_attn_all.items() if k in ('W_qk', 'b_qk', 'W_v', 'b_v', 'gamma', 'beta')}
    del _L0_attn_all

    def _L0_ffn_setup():
        import jax, jax.numpy as jnp
        import numpy as np
        DIM = 64
        H = 8
        D = 64
        G = 64
        INNER = H * D
        SCALE = D ** (-0.5)
        key = jax.random.key(seed)
        ks = jax.random.split(key, 12)
        B, N = (4, 4096)
        x = jax.random.normal(ks[0], (B, N, DIM), dtype=jnp.float32)
        s = lambda fan_in: 1.0 / np.sqrt(fan_in)
        W_fx = jax.random.normal(ks[1], (DIM, INNER), dtype=jnp.float32) * s(DIM)
        b_fx = jnp.zeros((INNER,), dtype=jnp.float32)
        W_x = jax.random.normal(ks[2], (DIM, INNER), dtype=jnp.float32) * s(DIM)
        b_x = jnp.zeros((INNER,), dtype=jnp.float32)
        A = jax.random.normal(ks[3], (G, D), dtype=jnp.float32)
        Q, _ = jnp.linalg.qr(A.T)
        W_slice = Q[:, :G].astype(jnp.float32)
        b_slice = jnp.zeros((G,), dtype=jnp.float32)
        W_q = jax.random.normal(ks[4], (D, D), dtype=jnp.float32) * s(D)
        W_k = jax.random.normal(ks[5], (D, D), dtype=jnp.float32) * s(D)
        W_v = jax.random.normal(ks[6], (D, D), dtype=jnp.float32) * s(D)
        W_out = jax.random.normal(ks[7], (INNER, DIM), dtype=jnp.float32) * s(INNER)
        b_out = jnp.zeros((DIM,), dtype=jnp.float32)
        temperature = jnp.ones((1, H, 1, 1), dtype=jnp.float32) * 0.5
        return {'x': x, 'W_fx': W_fx, 'b_fx': b_fx, 'W_x': W_x, 'b_x': b_x, 'W_slice': W_slice, 'b_slice': b_slice, 'W_q': W_q, 'W_k': W_k, 'W_v': W_v, 'W_out': W_out, 'b_out': b_out, 'temperature': temperature}
    _L0_ffn_all = _L0_ffn_setup()
    _L0_ffn_in = {k: v for k, v in _L0_ffn_all.items() if k in ('W_fx', 'b_fx', 'W_x', 'b_x', 'W_slice', 'b_slice', 'W_q', 'W_k', 'W_v', 'W_out', 'b_out', 'temperature')}
    del _L0_ffn_all

    def _L1_attn_setup():
        import jax, jax.numpy as jnp
        import numpy as np
        B, L, D = (4, 1024, 64)
        key = jax.random.key(seed)
        kx, kq, kk, kv, ko = jax.random.split(key, 5)
        std = 0.02
        return {'x': jax.random.normal(kx, (B, L, D), dtype=jnp.float32), 'Wq': std * jax.random.normal(kq, (D, D), dtype=jnp.float32), 'Wk': std * jax.random.normal(kk, (D, D), dtype=jnp.float32), 'Wv': std * jax.random.normal(kv, (D, D), dtype=jnp.float32), 'Wo': std * jax.random.normal(ko, (D, D), dtype=jnp.float32)}
    _L1_attn_all = _L1_attn_setup()
    _L1_attn_in = {k: v for k, v in _L1_attn_all.items() if k in ('Wq', 'Wk', 'Wv', 'Wo')}
    del _L1_attn_all

    def _L1_ffn_setup():
        import jax, jax.numpy as jnp
        import numpy as np
        D_MODEL = 64
        N_EXPERTS = 16
        HIDDEN = 128
        SCALE = 0.02
        key = jax.random.key(seed)
        ks = jax.random.split(key, 5)
        x = jax.random.normal(ks[0], (4, 2048, D_MODEL), dtype=jnp.float32)
        gate_w = jax.random.normal(ks[1], (D_MODEL, N_EXPERTS), dtype=jnp.float32) * SCALE
        gate_b = jnp.zeros((N_EXPERTS,), dtype=jnp.float32)
        w1 = jax.random.normal(ks[2], (N_EXPERTS, D_MODEL, HIDDEN), dtype=jnp.float32) * SCALE
        w2 = jax.random.normal(ks[3], (N_EXPERTS, D_MODEL, HIDDEN), dtype=jnp.float32) * SCALE
        w3 = jax.random.normal(ks[4], (N_EXPERTS, HIDDEN, D_MODEL), dtype=jnp.float32) * SCALE
        return {'x': x, 'gate_w': gate_w, 'gate_b': gate_b, 'w1': w1, 'w2': w2, 'w3': w3}
    _L1_ffn_all = _L1_ffn_setup()
    _L1_ffn_in = {k: v for k, v in _L1_ffn_all.items() if k in ('gate_w', 'gate_b', 'w1', 'w2', 'w3')}
    del _L1_ffn_all
    return {'x': x, 'cls_tok': cls_tok, 'L0_tok_W': _L0_tok_in['W'], 'L0_tok_b': _L0_tok_in['b'], 'L0_attn_W_qk': _L0_attn_in['W_qk'], 'L0_attn_b_qk': _L0_attn_in['b_qk'], 'L0_attn_W_v': _L0_attn_in['W_v'], 'L0_attn_b_v': _L0_attn_in['b_v'], 'L0_attn_gamma': _L0_attn_in['gamma'], 'L0_attn_beta': _L0_attn_in['beta'], 'L0_ffn_W_fx': _L0_ffn_in['W_fx'], 'L0_ffn_b_fx': _L0_ffn_in['b_fx'], 'L0_ffn_W_x': _L0_ffn_in['W_x'], 'L0_ffn_b_x': _L0_ffn_in['b_x'], 'L0_ffn_W_slice': _L0_ffn_in['W_slice'], 'L0_ffn_b_slice': _L0_ffn_in['b_slice'], 'L0_ffn_W_q': _L0_ffn_in['W_q'], 'L0_ffn_W_k': _L0_ffn_in['W_k'], 'L0_ffn_W_v': _L0_ffn_in['W_v'], 'L0_ffn_W_out': _L0_ffn_in['W_out'], 'L0_ffn_b_out': _L0_ffn_in['b_out'], 'L0_ffn_temperature': _L0_ffn_in['temperature'], 'L1_attn_Wq': _L1_attn_in['Wq'], 'L1_attn_Wk': _L1_attn_in['Wk'], 'L1_attn_Wv': _L1_attn_in['Wv'], 'L1_attn_Wo': _L1_attn_in['Wo'], 'L1_ffn_gate_w': _L1_ffn_in['gate_w'], 'L1_ffn_gate_b': _L1_ffn_in['gate_b'], 'L1_ffn_w1': _L1_ffn_in['w1'], 'L1_ffn_w2': _L1_ffn_in['w2'], 'L1_ffn_w3': _L1_ffn_in['w3']}

def reference(x, cls_tok, L0_tok_W, L0_tok_b, L0_attn_W_qk, L0_attn_b_qk, L0_attn_W_v, L0_attn_b_v, L0_attn_gamma, L0_attn_beta, L0_ffn_W_fx, L0_ffn_b_fx, L0_ffn_W_x, L0_ffn_b_x, L0_ffn_W_slice, L0_ffn_b_slice, L0_ffn_W_q, L0_ffn_W_k, L0_ffn_W_v, L0_ffn_W_out, L0_ffn_b_out, L0_ffn_temperature, L1_attn_Wq, L1_attn_Wk, L1_attn_Wv, L1_attn_Wo, L1_ffn_gate_w, L1_ffn_gate_b, L1_ffn_w1, L1_ffn_w2, L1_ffn_w3):
    import jax
    import jax.numpy as jnp

    def _L0_tok_ref(x, W, b):
        import jax, jax.numpy as jnp
        import numpy as np
        IMAGE_SIZE = 64
        PATCH = 16
        EMBED_DIM = 64
        IN_CH = 3
        BATCH = 128
        IN_DIM = IN_CH * PATCH * PATCH

        def _patchify(x, p):
            B, C, H, Wd = x.shape
            x = x.reshape(B, C, H // p, p, Wd // p, p)
            x = x.transpose(0, 2, 4, 1, 3, 5)
            return x.reshape(B, H // p * (Wd // p), C * p * p)
        patches = _patchify(x, PATCH)
        return jnp.einsum('bnk,ek->bne', patches, W) + b

    def _L0_attn_ref(feature, W_qk, b_qk, W_v, b_v, gamma, beta):
        import jax, jax.numpy as jnp
        import numpy as np
        BN_EPS = 1e-05
        QK = jnp.einsum('bnd,kde->bkne', feature, W_qk) + b_qk[None, :, None, :]
        value = jnp.einsum('bnd,de->bne', feature, W_v) + b_v
        query = QK[:, 0]
        key = QK[:, 1]
        sm = jax.nn.softmax(key, axis=1)
        lam = jnp.einsum('bnd,bne->bde', sm, value)
        mean = jnp.mean(lam, axis=(0, 2), keepdims=True)
        var = jnp.var(lam, axis=(0, 2), keepdims=True)
        bn = (lam - mean) * jax.lax.rsqrt(var + BN_EPS)
        bn = bn * gamma[None, :, None] + beta[None, :, None]
        return jnp.einsum('bnd,bde->bne', query, bn)

    def _L0_ffn_ref(x, W_fx, b_fx, W_x, b_x, W_slice, b_slice, W_q, W_k, W_v, W_out, b_out, temperature):
        import jax, jax.numpy as jnp
        import numpy as np
        DIM = 64
        H = 8
        D = 64
        G = 64
        INNER = H * D
        SCALE = D ** (-0.5)
        B, N, _ = x.shape
        fx_mid = (x @ W_fx + b_fx).reshape(B, N, H, D).transpose(0, 2, 1, 3)
        x_mid = (x @ W_x + b_x).reshape(B, N, H, D).transpose(0, 2, 1, 3)
        temp = jnp.clip(temperature, 0.1, 5.0)
        slice_weights = jax.nn.softmax((x_mid @ W_slice + b_slice) / temp, axis=-1)
        slice_norm = slice_weights.sum(axis=2)
        slice_token = jnp.einsum('bhnc,bhng->bhgc', fx_mid, slice_weights)
        slice_token = slice_token / (slice_norm[..., None] + 1e-05)
        q = slice_token @ W_q
        k = slice_token @ W_k
        v = slice_token @ W_v
        attn = jax.nn.softmax(jnp.einsum('bhgc,bhkc->bhgk', q, k) * SCALE, axis=-1)
        out_slice = jnp.einsum('bhgk,bhkc->bhgc', attn, v)
        out_x = jnp.einsum('bhgc,bhng->bhnc', out_slice, slice_weights)
        out_x = out_x.transpose(0, 2, 1, 3).reshape(B, N, INNER)
        return out_x @ W_out + b_out

    def _L1_attn_ref(x, Wq, Wk, Wv, Wo):
        import jax, jax.numpy as jnp
        import numpy as np
        B, L, D = (4, 1024, 64)
        q = x @ Wq.T
        k = x @ Wk.T
        v = x @ Wv.T
        logits = jnp.einsum('bld,bmd->blm', q, k)
        Lq = x.shape[1]
        causal_mask = jnp.triu(jnp.ones((Lq, Lq), dtype=bool), k=1)
        logits = jnp.where(causal_mask[None], jnp.asarray(0.0, logits.dtype), logits)
        attn = jax.nn.relu(logits)
        row_counts = jnp.maximum(jnp.arange(Lq, dtype=attn.dtype), 1.0)
        attn = attn / row_counts[None, :, None]
        ctx = jnp.einsum('blm,bmd->bld', attn, v)
        return ctx @ Wo.T

    def _L1_ffn_ref(x, gate_w, gate_b, w1, w2, w3):
        import jax, jax.numpy as jnp
        import numpy as np
        D_MODEL = 64
        N_EXPERTS = 16
        HIDDEN = 128
        SCALE = 0.02
        n_experts = w1.shape[0]
        logits = jnp.einsum('bsd,de->bse', x, gate_w) + gate_b
        probs = jax.nn.softmax(logits, axis=-1)
        top_probs, top_idx = jax.lax.top_k(probs, 2)
        top_probs = top_probs / jnp.sum(top_probs, axis=-1, keepdims=True)
        dispatch = jnp.sum(jax.nn.one_hot(top_idx, n_experts, dtype=x.dtype) * top_probs[..., None], axis=-2)
        h1 = jnp.einsum('bsd,edh->bseh', x, w1)
        h2 = jnp.einsum('bsd,edh->bseh', x, w2)
        hidden = jax.nn.silu(h1) * h2
        expert_out = jnp.einsum('bseh,eho->bseo', hidden, w3)
        return jnp.einsum('bseo,bse->bso', expert_out, dispatch)
    h = _L0_tok_ref(x, L0_tok_W, L0_tok_b)
    h = jnp.concatenate([jnp.broadcast_to(cls_tok, (h.shape[0], 1, h.shape[2])), h], axis=1)
    h = h + _L0_attn_ref(_layernorm(h, axis=-1), L0_attn_W_qk, L0_attn_b_qk, L0_attn_W_v, L0_attn_b_v, L0_attn_gamma, L0_attn_beta)
    h = h + _L0_ffn_ref(_layernorm(h, axis=-1), L0_ffn_W_fx, L0_ffn_b_fx, L0_ffn_W_x, L0_ffn_b_x, L0_ffn_W_slice, L0_ffn_b_slice, L0_ffn_W_q, L0_ffn_W_k, L0_ffn_W_v, L0_ffn_W_out, L0_ffn_b_out, L0_ffn_temperature)
    h = h + _L1_attn_ref(_layernorm(h, axis=-1), L1_attn_Wq, L1_attn_Wk, L1_attn_Wv, L1_attn_Wo)
    h = h + _L1_ffn_ref(_layernorm(h, axis=-1), L1_ffn_gate_w, L1_ffn_gate_b, L1_ffn_w1, L1_ffn_w2, L1_ffn_w3)
    return h

_drawn_inputs = setup_inputs


def setup_inputs(seed=0):
    import zlib

    import numpy as np

    out = dict(_drawn_inputs(seed))
    spreads = {'L0_attn_b_qk': (0.0, 0.1),
     'L0_attn_b_v': (0.0, 0.1),
     'L0_attn_gamma': (1.0, 0.2),
     'L0_attn_beta': (0.0, 0.1),
     'L0_ffn_b_fx': (0.0, 0.529),
     'L0_ffn_b_x': (0.0, 0.8),
     'L0_ffn_b_slice': (0.0, 2.0),
     'L0_ffn_b_out': (0.0, 0.654),
     'L0_ffn_temperature': (0.5, 0.6),
     'L1_ffn_gate_b': (0.0, 0.8)}
    factors = {'L0_tok_b': 2.677,
     'L0_ffn_W_x': 6.29,
     'L0_ffn_W_slice': 6.662,
     'L0_ffn_W_q': 4.107,
     'L0_ffn_W_k': 4.089,
     'L1_attn_Wq': 8.0,
     'L1_attn_Wk': 8.0,
     'L1_attn_Wv': 8.0,
     'L1_attn_Wo': 8.0,
     'L1_ffn_gate_w': 8.0,
     'L1_ffn_w1': 8.0,
     'L1_ffn_w2': 8.0,
     'L1_ffn_w3': 8.0}
    for name, (base, spread) in spreads.items():
        noise = np.random.default_rng([zlib.crc32(name.encode()), seed]).standard_normal(out[name].shape)
        drawn = base * np.exp(spread * noise) if base else spread * noise
        out[name] = jnp.asarray(drawn.astype(out[name].dtype))
    for name, factor in factors.items():
        out[name] = (out[name] * factor).astype(out[name].dtype)
    return out
```

```python
from contextlib import ExitStack

import concourse.bass as bass
from concourse import mybir

F32 = mybir.dt.float32
F32R = mybir.dt.float32r
ALU = mybir.AluOpType
ACT = mybir.ActivationFunctionType
AX_X = mybir.AxisListType.X

EPS = 1e-5


def vit_tower_kernel(nc, x, cls_tok, tok_W, tok_b, a0_W_qk, a0_b_qk, a0_W_v, a0_b_v, a0_gamma, a0_beta,
                     f0_W_fx, f0_b_fx, f0_W_x, f0_b_x, f0_W_slice, f0_b_slice, f0_W_q, f0_W_k, f0_W_v,
                     f0_W_out, f0_b_out, f0_temperature, a1_Wq, a1_Wk, a1_Wv, a1_Wo,
                     f1_gate_w, f1_gate_b, f1_w1, f1_w2, f1_w3, out):
    B, C, IMG, _ = x.shape
    D = cls_tok.shape[2]
    PATCH = 16
    HP = IMG // PATCH
    N = HP * HP + 1
    G = 6
    R = G * N
    NT = -(-B // G)
    TP = NT * R
    T = B * N
    H = f0_temperature.shape[1]
    HH = H // 2
    S = f0_W_slice.shape[1]
    E, _, HID = f1_w1.shape
    A = D + 1
    HALF = T // 2
    XC = HALF // N
    FIRST = (512 // R) * R
    IH = 8
    NCH = C * PATCH // IH
    assert D == 64 and S == 64 and B * HP == 128 and R <= 128 and HID == 128 and C == 3
    LOW = 32
    rows = [min(G, B - t * G) * N for t in range(NT)]
    imgs = [min(G, B - t * G) for t in range(NT)]
    pairs = [n // 2 for n in imgs]

    with ExitStack() as ctx:
        def sb(name, shape, dt=F32):
            return ctx.enter_context(nc.sbuf_tensor(name, shape, dt))

        def sem(name):
            return ctx.enter_context(nc.semaphore(name))

        bank = [ctx.enter_context(nc.psum_tensor(f"bank{i}", [128, 512], F32)) for i in range(8)]

        region = sb("region", [128, 2 * G * H * S])
        XIN, PIX = C * PATCH * IMG, 2 * 512
        CH = HP * 128
        xin = region[:, 0:XIN].rearrange("p (c n) -> p c n", c=C)
        pixT = region[:, XIN:XIN + PIX].rearrange("p (k n) -> p k n", k=2)
        tokw = region[0:D, XIN + PIX:XIN + PIX + C * PATCH * PATCH]
        silu, hid, hidw = (region[0:HID, i * 2 * HALF:(i + 1) * 2 * HALF].rearrange("p (a n) -> p a n", a=2) for i in range(3))
        xre = sb("xre", [128, 2, CH])
        zx = region[0:R, :].rearrange("p (a i n) -> p a i n", a=2, i=G)
        tokb = sb("tokb", [D, 1])
        cls = sb("cls", [D, 1])
        wk_a = sb("wk_a", [A, D])
        wq_a = sb("wq_a", [A, D])
        wv_a = sb("wv_a", [A, D])
        gamma = sb("gamma", [D, 1])
        beta = sb("beta", [D, 1])
        wfx_a = sb("wfx_a", [A, H * D])
        wx_a = sb("wx_a", [A, H * D])
        wslice = sb("wslice", [128, S])
        bslice = sb("bslice", [D + 1, S])
        wq2 = sb("wq2", [128, D])
        wk2 = sb("wk2", [128, D])
        wv2 = sb("wv2", [D, 2, D])
        wout = sb("wout", [128, HH, D])
        bout = sb("bout", [D, 1])
        temp = sb("temp", [A, H])
        l1q = sb("l1q", [D, D])
        l1k = sb("l1k", [D, D])
        l1v = sb("l1v", [D, D])
        l1o = sb("l1o", [D, D])
        gate_a = sb("gate_a", [A, E])
        w3 = sb("w3", [HID, E, D])

        ident = sb("ident", [128, 128])
        EPSC = sb("eps_col", [128, 1])
        imgmask = sb("imgmask", [R, G])
        same = sb("same", [R, R])
        causal = sb("causal", [R, R])
        e64 = sb("e64", [A, A])
        rev = sb("rev", [R, E])
        pick = sb("pick", [LOW + E, E], F32R)

        tokwT = sb("tokwT", [128, NCH, D])
        wfxT = sb("wfxT", [128, HH, A])
        wxT = sb("wxT", [128, HH, A])
        wvT = sb("wvT", [128, D])
        rtemp = sb("rtemp", [A, H])
        ws = sb("ws", [A, H * S])
        qT = sb("qT", [128, HH, A])
        kT = sb("kT", [128, HH, A])
        gram = sb("gram", [A, H, A])
        wvo = sb("wvo", [128, HH, D])
        vo = sb("vo", [A, H * D])
        g1 = sb("g1", [D, D])
        l1oT = sb("l1oT", [D, D])
        vo1 = sb("vo1", [D, D])

        hT0 = sb("hT0", [D, TP])
        h = sb("h", [R, NT, D])
        musum = sb("musum", [R, NT])
        xc = sb("xc", [R, NT, D])
        sq = sb("sq", [R, NT, D])
        vsum = sb("vsum", [R, NT])
        std = sb("std", [R, NT])
        spare = sb("spare", [1, 16])
        rstd = sb("rstd", [R, NT])
        xn = sb("xn", [R, NT, D])
        xT = sb("xT", [A, TP])

        kmax = sb("kmax", [D, B])
        ksum = sb("ksum", [D, B])
        krec = sb("krec", [D, B])
        kexp = sb("kexp", [D, T])
        smT = sb("smT", [D, TP])
        q0T = sb("q0T", [D, TP])
        qsT = sb("qsT", [D, TP])
        v0 = sb("v0", [R, NT, D])
        sm = sb("sm", [R, NT, D])
        vexp = sb("vexp", [R, 2, G, D])
        stats = sb("stats", [D, NT, 6])
        mv = sb("mv", [D, 2])
        bnl = sb("bnl", [D, 1])
        bnr = sb("bnr", [D, 1])
        bna = sb("bna", [D, 1])
        bnm = sb("bnm", [D, 1])
        bnc = sb("bnc", [D, 1])
        att = sb("att", [R, NT, R])
        vt1 = sb("vt1", [R, NT, D])

        smax = sb("smax", [R, NT, H])
        ssum = sb("ssum", [R, NT, H])
        srec = sb("srec", [R, NT, H])
        sexp = sb("sexp", [R, 2, H, S])
        sw = sb("sw", [R, 4, H, S])
        neps = sb("neps", [R, 2, H, S])
        nrec = sb("nrec", [R, 2, H, S])
        sn = sb("sn", [R, 4, H, S])
        mm = sb("mm", [R, 2, H, R])
        lg = sb("lg", [128, 2, H, S])
        fe = sb("fe", [128, 2, G // 2, H, S])
        umax = sb("umax", [128, NT, G // 2, H])
        usum = sb("usum", [128, 2, G // 2, H])
        urec = sb("urec", [128, 2, H, G // 2])
        etx = sb("etx", [128, 2, H, R])
        snT = sb("snT", [128, 2, HH, R])
        rT = sb("rT", [128, 2, HH, R])
        pT = sb("pT", [R, 2, H, R])
        vox = sb("vox", [R, 2, H, D])

        gmax = sb("gmax", [R, NT])
        gd = sb("gd", [R, NT, E])
        ge = sb("ge", [R, NT, E])
        gc = sb("gc", [R, NT, E])
        gr = sb("gr", [R, NT])
        gs1 = sb("gs1", [R, NT, E])
        gd2 = sb("gd2", [R, NT, E])
        gs2 = sb("gs2", [R, NT, E])
        gw = sb("gw", [R, NT, E])
        dispT = sb("dispT", [LOW + E, TP], F32R)

        with ExitStack() as early:
            w1, w2 = (early.enter_context(nc.sbuf_tensor(n, [2 * D, E, HID], F32)) for n in ("w1", "w2"))
            t1 = early.enter_context(nc.sbuf_tensor("t1", [A, H, TP], F32))
        w1l, w2l, w1h, w2h = (sb(n, [2 * D, E, HID], F32R) for n in ("w1l", "w2l", "w1h", "w2h"))
        xS = sb("xS", [2 * D, TP], F32R)

        names = """x_in0 x_in1 x_in2 tokw_in a0_in f0_in l1_in moe_in small_in const
            tokwT_ps tokwT_sb re_even re_odd pix_ps pix_even pix_odd tok_ps tok_sb htm_ps h_upd
            wT_ps wT_sb ab_ps ab_sb gram_ps gram_sb ws_ps ws_sb rt wvo_ps wvo_sb vo_ps vo_sb l1_ps l1_sb l1b_ps l1b_sb
            ln_sum ln_cen ln_sq ln_var ln_std ln_rstd ln_xn ln_ps ln_xT
            k_ps q_ps v_ps k_max k_sub k_exp k_sum k_rec k_sm q_sb v_sb sm_ps sm_sb vexp_d vexp_p lam_ps bn_st bn_mv bn_std
            bn_rstd bn_a bn_m bn_c q_scaled at_ps at_sb ao_ps
            t1_ps t1_even t1_odd s_ps s_max s_sub s_exp s_sum s_rec s_w n_ps n_eps n_rec s_n m_ps m_sb z_ps z_sb snT_ps snT_sb
            l_ps u_max u_sub u_exp u_sum u_rec et_ps et_sb r_ps r_sb p_ps p_sb vo_ps2 vo_sb2 o_ps o_sb ot_ps
            t_ps t_sb
            w_hi w_lo x_hi x_hi_last x_lo g_ps g_max g_sub g_exp g_step g_disp d_zero d_ps d_sb d_lo e1_ps e2_ps db_ps e_silu e_hid e_w e_out e_outT e_fin
            e_res stored""".split()
        s = {n: sem(n) for n in names}

        CONSTS = 19 + N + E

        block = ctx.enter_context(nc.Block())

        @block.sync
        def _(sp):
            xv = x.rearrange("b c (hp i) w -> c b hp (i w)", hp=HP)
            sp.dma_start(tokw[:, :], tok_W).then_inc(s["tokw_in"], 16)
            for c in range(C):
                for b0 in range(0, B, B // 4):
                    sp.dma_start(xin[b0 * HP:(b0 + B // 4) * HP, c, :], xv[c, b0:b0 + B // 4]).then_inc(s[f"x_in{c}"], 16)
            for half in (slice(0, D), slice(D, 2 * D)):
                sp.dma_start(w1[half, :, :], f1_w1.rearrange("e d f -> d e f")).then_inc(s["moe_in"], 16)
                sp.dma_start(w2[half, :, :], f1_w2.rearrange("e d f -> d e f")).then_inc(s["moe_in"], 16)
            sp.dma_start(w3[:, :, :], f1_w3.rearrange("e f d -> f e d")).then_inc(s["moe_in"], 16)
            sp.wait_ge(s["e_res"], 1)
            ov = out.rearrange("b n d -> (b n) d")
            full = NT - 1
            sp.dma_start(ov[0:full * R, :].rearrange("(t p) d -> p t d", p=R), xn[:, 0:full, :]).then_inc(s["stored"], 16)
            sp.dma_start(ov[full * R:T, :], xn[0:rows[full], full, :]).then_inc(s["stored"], 16)
            sp.wait_ge(s["stored"], 32)

        def row(v, n=1):
            return v.rearrange("(a n) -> a n", a=n)

        def col(v):
            return v.rearrange("(n a) -> n a", a=1)

        def reorder(k, engine, copy, done):
            c, ih = divmod(k, PATCH // IH)
            engine.wait_ge(s[f"x_in{c}"], 4 * 16)
            if k >= 2:
                engine.wait_ge(s["pix_ps"], k - 1)
            v = xin[:, c, :].rearrange("p (i w j) -> p w i j", i=PATCH, w=HP)
            copy(xre[:, k % 2, :].rearrange("p (w i j) -> p w i j", w=HP, i=IH),
                 v[:, :, ih * IH:(ih + 1) * IH, :]).then_inc(done, 1)

        @block.scalar
        def _(act):
            for dst, src in ((wfx_a[0:D, :], f0_W_fx), (wfx_a[D:A, :], row(f0_b_fx)),
                             (wx_a[0:D, :], f0_W_x), (wx_a[D:A, :], row(f0_b_x)),
                             (wslice[0:D, :], f0_W_slice), (wslice[D:128, :], f0_W_slice), (bslice[0:1, :], row(f0_b_slice)), (bslice[D:D + 1, :], row(f0_b_slice)),
                             (wq2[0:D, :], f0_W_q), (wq2[D:128, :], f0_W_q), (wk2[0:D, :], f0_W_k), (wk2[D:128, :], f0_W_k),
                             (wv2[:, 0, :], f0_W_v), (wv2[:, 1, :], f0_W_v),
                             (wout[:, :, :], f0_W_out.rearrange("(a p) d -> p a d", p=128)),
                             (temp[:, :], f0_temperature.rearrange("a h b c -> a (h b c)").to_broadcast([A, H]))):
                act.dma_start(dst, src).then_inc(s["f0_in"], 16)

            def evac(dst, src):
                return nc.scalar.activation(dst, src, ACT.Copy)

            act.wait_ge(s["tokwT_ps"], 1)
            evac(tokwT[:, :, :], bank[0][:, 0:NCH * D].rearrange("p (k d) -> p k d", k=NCH)).then_inc(s["tokwT_sb"], 1)
            act.wait_ge(s["wT_ps"], 1)
            evac(wfxT[:, :, :], bank[1][:, 0:HH * A].rearrange("p (k d) -> p k d", k=HH)).then_inc(s["wT_sb"], 1)
            act.wait_ge(s["wT_ps"], 2)
            evac(wxT[:, :, :], bank[2][:, 0:HH * A].rearrange("p (k d) -> p k d", k=HH)).then_inc(s["wT_sb"], 1)
            act.wait_ge(s["wT_ps"], 3)
            evac(wvT[:, :], bank[3][:, 0:D]).then_inc(s["wT_sb"], 1)
            act.wait_ge(s["ab_ps"], 1)
            nc.scalar.activation(qT[:, :, :], bank[4][:, 0:HH * A].rearrange("p (k d) -> p k d", k=HH), ACT.Copy,
                                 scale=float(D) ** -0.5).then_inc(s["ab_sb"], 1)
            act.wait_ge(s["ab_ps"], 2)
            evac(kT[:, :, :], bank[5][:, 0:HH * A].rearrange("p (k d) -> p k d", k=HH)).then_inc(s["ab_sb"], 1)
            act.wait_ge(s["wvo_ps"], 1)
            evac(wvo[:, :, :], bank[6][:, 0:HH * D].rearrange("p (k d) -> p k d", k=HH)).then_inc(s["wvo_sb"], 1)
            act.wait_ge(s["gram_ps"], 1)
            for i in range(2):
                evac(gram[:, i::2, :],
                     bank[i][0:A, 0:HH * A].rearrange("p (k d) -> p k d", k=HH)).then_inc(s["gram_sb"], 1)
            act.wait_ge(s["vo_ps"], 1)
            for i in range(2):
                evac(vo[:, :].rearrange("p (h d) -> p h d", h=H)[:, i::2, :],
                     bank[6 + i][0:A, 0:HH * D].rearrange("p (k d) -> p k d", k=HH)).then_inc(s["vo_sb"], 1)
            act.wait_ge(s["l1_ps"], 1)
            evac(g1[:, :], bank[4][0:D, 0:D]).then_inc(s["l1_sb"], 1)
            evac(l1oT[:, :], bank[4][0:D, D:2 * D]).then_inc(s["l1_sb"], 1)
            act.wait_ge(s["l1b_ps"], 1)
            evac(vo1[:, :], bank[5][0:D, 0:D]).then_inc(s["l1b_sb"], 1)

            for k in range(0, NCH, 2):
                reorder(k, act, evac, s["re_even"])
                act.wait_ge(s["pix_ps"], k + 1)
                if k >= 2:
                    act.wait_ge(s["tok_ps"], k - 1)
                evac(pixT[:, 0, :], bank[0][:, :]).then_inc(s["pix_even"], 1)
            act.wait_ge(s["tok_ps"], NCH)
            for j in range(HP):
                nc.scalar.activation(
                    hT0[:, 0:T].rearrange("p (b n) -> p b n", n=N)[:, :, 1 + j::HP],
                    bank[2][0:D, j * B * HP:(j + 1) * B * HP].rearrange("p (b a) -> p b a", a=HP),
                    ACT.Identity, bias=tokb[:, 0:1]).then_inc(s["tok_sb"], 1)

            loads = [0]

            def tables(function):
                nc.scalar.activation(spare[:, loads[0]:loads[0] + 1], EPSC[0:1, 0:1], function)
                loads[0] += 1

            def layernorm(k):
                tables(ACT.Sqrt)
                act.wait_ge(s["ln_cen"], k + 1)
                nc.scalar.activation(sq[:, :, :], xc[:, :, :], ACT.Square).then_inc(s["ln_sq"], 1)
                act.wait_ge(s["ln_var"], k + 1)
                nc.scalar.activation(std[:, :], vsum[:, :], ACT.Sqrt, bias=EPSC[0:R, 0:1], scale=1.0 / D).then_inc(s["ln_std"], 1)
                tables(ACT.Exp)
                act.wait_ge(s["ln_ps"], k + 1)
                evac(xT[0:D, 0:FIRST], bank[6][0:D, 0:FIRST]).then_inc(s["ln_xT"], 1)

            layernorm(0)

            for i in range(2):
                act.wait_ge(s["q_ps"], i + 1)
                evac(q0T[:, i * HALF:(i + 1) * HALF], bank[2 + i][0:D, 0:HALF]).then_inc(s["q_sb"], 1)
            act.wait_ge(s["v_ps"], 1)
            evac(v0[:, :, :], bank[4][0:R, 0:NT * D].rearrange("p (t d) -> p t d", t=NT)).then_inc(s["v_sb"], 1)
            act.wait_ge(s["k_sub"], 2)
            nc.scalar.activation(kexp[:, :], kexp[:, :], ACT.Exp).then_inc(s["k_exp"], 1)
            act.wait_ge(s["sm_ps"], 1)
            evac(sm[:, :, :], bank[5][0:R, 0:NT * D].rearrange("p (t d) -> p t d", t=NT)).then_inc(s["sm_sb"], 1)
            tables(ACT.Sqrt)
            act.wait_ge(s["bn_mv"], 1)
            nc.scalar.activation(bnl[:, :], mv[:, 1:2], ACT.Sqrt, bias=EPSC[0:D, 0:1]).then_inc(s["bn_std"], 1)

            layernorm(1)

            for hd in range(0, H, 2):
                for i in range(2):
                    n = 2 * hd + i
                    act.wait_ge(s["t1_ps"], n + 1)
                    evac(t1[:, hd, i * HALF:(i + 1) * HALF], bank[n % 4][0:A, 0:HALF]).then_inc(s["t1_even"], 1)

            def slice_exp(t):
                act.wait_ge(s["s_sub"], t + 1)
                if t >= 2:
                    act.wait_ge(s["s_w"], t - 1)
                nc.scalar.activation(sexp[0:rows[t], t % 2], sexp[0:rows[t], t % 2], ACT.Exp).then_inc(s["s_exp"], 1)

            def norm_eps(t):
                act.wait_ge(s["n_ps"], t + 1)
                if t >= 2:
                    act.wait_ge(s["n_rec"], t - 1)
                nc.scalar.activation(neps[0:rows[t], t % 2],
                                     bank[4][0:rows[t], :].rearrange("p (h g) -> p h g", h=H), ACT.Identity,
                                     bias=EPSC[0:rows[t], 0:1]).then_inc(s["n_eps"], 1)

            def spread_z(t):
                act.wait_ge(s["z_ps"], t + 1)
                if t >= 2:
                    act.wait_ge(s["l_ps"], sum(pairs[0:t - 1]))
                for i in range(imgs[t]):
                    nc.scalar.activation(zx[0:rows[t], t % 2, i, :], bank[7][0:rows[t], :], ACT.Copy,
                                         scale=imgmask[0:rows[t], i:i + 1]).then_inc(s["z_sb"], 1)

            def slices_T(t):
                act.wait_ge(s["snT_ps"], t + 1)
                if t >= 2:
                    act.wait_ge(s["p_ps"], t - 1)
                evac(snT[:, t % 2, :, 0:rows[t]],
                     bank[3][:, 0:HH * R].rearrange("p (k r) -> p k r", k=HH)[:, :, 0:rows[t]]).then_inc(s["snT_sb"], 1)

            def values(t):
                act.wait_ge(s["vo_ps2"], t + 1)
                if t >= 2:
                    act.wait_ge(s["o_ps"], t - 1)
                evac(vox[0:rows[t], t % 2], bank[0][0:rows[t], :].rearrange("p (h d) -> p h d", h=H)).then_inc(s["vo_sb2"], 1)

            def slice_attention_exp(t, p):
                if 0 <= t < NT and p < pairs[t]:
                    u = sum(pairs[0:t]) + p
                    act.wait_ge(s["u_sub"], u + 1)
                    if t >= 2:
                        act.wait_ge(s["r_ps"], t - 1)
                    nc.scalar.activation(fe[:, t % 2, p], lg[:, u % 2], ACT.Exp).then_inc(s["u_exp"], 1)

            def r_out(t):
                act.wait_ge(s["r_ps"], t + 1)
                if t >= 2:
                    act.wait_ge(s["p_ps"], t - 1)
                evac(rT[:, t % 2, :, 0:rows[t]],
                     bank[3][:, 0:HH * R].rearrange("p (k r) -> p k r", k=HH)[:, :, 0:rows[t]]).then_inc(s["r_sb"], 1)

            def o_out(t):
                act.wait_ge(s["o_ps"], t + 1)
                nc.scalar.activation(hT0[:, t * R:t * R + rows[t]], bank[4][0:D, 0:rows[t]], ACT.Identity,
                                     bias=bout[:, 0:1]).then_inc(s["o_sb"], 1)

            for i in range(NT + 3):
                if 0 <= i - 1 < NT:
                    norm_eps(i - 1)
                if i >= 3:
                    slices_T(i - 3)
                if i < NT:
                    slice_exp(i)
                if i >= 3:
                    values(i - 3)
                slice_attention_exp(i - 2, 0)
                if i >= 3:
                    r_out(i - 3)
                slice_attention_exp(i - 2, 1)
                if 0 <= i - 1 < NT:
                    spread_z(i - 1)
                slice_attention_exp(i - 2, 2)
                if i >= 3:
                    o_out(i - 3)

            layernorm(2)

            for i in range(2):
                act.wait_ge(s["t_ps"], i + 1)
                evac(qsT[:, i * HALF:(i + 1) * HALF], bank[i][0:D, 0:HALF]).then_inc(s["t_sb"], 1)
            act.wait_ge(s["v_ps"], 2)
            evac(vt1[:, :, :], bank[4][0:R, 0:NT * D].rearrange("p (t d) -> p t d", t=NT)).then_inc(s["v_sb"], 1)

            layernorm(3)

            act.wait_ge(s["w_hi"], 2)
            evac(xS[0:D, 0:FIRST], bank[6][0:D, 0:FIRST]).then_inc(s["x_hi"], 1)
            act.wait_ge(s["g_sub"], 1)
            nc.scalar.activation(ge[:, :, :], gd[:, :, :], ACT.Exp).then_inc(s["g_exp"], 1)
            act.wait_ge(s["d_zero"], 1)
            act.wait_ge(s["d_ps"], 1)
            evac(dispT[0:E, 0:FIRST], bank[4][0:E, 0:FIRST]).then_inc(s["d_sb"], 1)
            evac(dispT[0:E, FIRST:TP], bank[5][0:E, 0:TP - FIRST]).then_inc(s["d_sb"], 1)
            for n in range(2 * E):
                act.wait_ge(s["e1_ps"], n + 1)
                if n >= 2:
                    act.wait_ge(s["e_hid"], n - 1)
                nc.scalar.activation(silu[:, n % 2, :], bank[n % 2][:, 0:HALF], ACT.Silu).then_inc(s["e_silu"], 1)
            act.wait_ge(s["e_out"], 2 * E)
            for i in range(2):
                evac(hT0[:, i * HALF:(i + 1) * HALF], bank[6 + i][0:D, 0:HALF]).then_inc(s["e_outT"], 1)

        @block.gpsimd
        def _(pool):
            for dst, src in ((tokb[:, :], col(tok_b)), (cls[:, :], col(cls_tok.rearrange("a b d -> (a b d)"))),
                             (bout[:, :], col(f0_b_out)), (gamma[:, :], col(a0_gamma)), (beta[:, :], col(a0_beta))):
                pool.dma_start(dst, src).then_inc(s["small_in"], 16)
            for dst, src in ((wk_a[0:D, :], a0_W_qk[1]), (wk_a[D:A, :], a0_b_qk[1:2, :]),
                             (wq_a[0:D, :], a0_W_qk[0]), (wq_a[D:A, :], a0_b_qk[0:1, :]),
                             (wv_a[0:D, :], a0_W_v), (wv_a[D:A, :], row(a0_b_v))):
                pool.dma_start(dst, src).then_inc(s["a0_in"], 16)
            for dst, src in ((l1q[:, :], a1_Wq), (l1k[:, :], a1_Wk), (l1v[:, :], a1_Wv), (l1o[:, :], a1_Wo),
                             (gate_a[0:D, :], f1_gate_w), (gate_a[D:A, :], row(f1_gate_b))):
                pool.dma_start(dst, src).then_inc(s["l1_in"], 16)

            made = [0]

            def link(ins):
                made[0] += 1
                ins.then_inc(s["const"], 1)
                pool.wait_ge(s["const"], made[0])

            def select(t, pattern, base, mult, op, fill):
                link(nc.gpsimd.affine_select(out=t, in_=t, pattern=pattern, base=base, channel_multiplier=mult,
                                             compare_op=op, fill=fill))

            link(nc.gpsimd.memset(ident[:, :], 0.0))
            select(ident[:, :], [[-1, 128]], 0, 1, ALU.not_equal, 1.0)
            link(nc.gpsimd.memset(xT[D:A, :], 1.0))
            link(nc.gpsimd.memset(hT0[:, T:TP], 0.0))
            link(nc.gpsimd.memset(e64[:, 0:D], 0.0))
            link(nc.gpsimd.memset(e64[:, D:A], 1.0))
            link(nc.gpsimd.memset(smT[:, T:TP], 0.0))
            link(nc.gpsimd.memset(q0T[:, T:TP], 0.0))
            link(nc.gpsimd.memset(qsT[:, T:TP], 0.0))
            link(nc.gpsimd.memset(EPSC[:, :], EPS))
            link(nc.gpsimd.memset(imgmask[:, :], 1.0))
            select(imgmask[:, :], [[-N, G]], 0, 1, ALU.is_ge, 0.0)
            select(imgmask[:, :], [[N, G]], N - 1, -1, ALU.is_ge, 0.0)
            same3 = same[:, :].rearrange("p (i n) -> p i n", i=G)
            link(nc.gpsimd.memset(same[:, :], 1.0))
            select(same3, [[-N, G], [0, N]], 0, 1, ALU.is_ge, 0.0)
            select(same3, [[N, G], [0, N]], N - 1, -1, ALU.is_ge, 0.0)
            causal3 = causal[:, :].rearrange("p (i n) -> p i n", i=G)
            for l in range(N):
                link(nc.gpsimd.memset(causal3[:, :, l:l + 1], 1.0 / max(l, 1)))
            select(causal3, [[-N, G], [0, N]], 0, 1, ALU.is_ge, 0.0)
            select(causal3, [[N, G], [1, N]], 0, -1, ALU.is_ge, 0.0)
            for e in range(E):
                link(nc.gpsimd.memset(rev[:, e:e + 1], float(E - e)))
            link(nc.gpsimd.memset(etx[:, :, :, :], 0.0))

            for t in range(0, NT, 2):
                pool.wait_ge(s["v_sb"], 1)
                if t >= 2:
                    pool.wait_ge(s["lam_ps"], t - 1)
                nc.gpsimd.tensor_tensor(vexp[:, 0], v0[:, t:t + 1, :].to_broadcast([R, G, D]),
                                        imgmask[:, :].unsqueeze(2).to_broadcast([R, G, D]), ALU.mult).then_inc(s["vexp_p"], 1)

            def weights(t):
                pool.wait_ge(s["s_rec"], t + 1)
                if t >= 4:
                    pool.wait_ge(s["et_ps"], t - 3)
                    pool.wait_ge(s["s_n"], t - 3)
                rt = rows[t]
                nc.gpsimd.tensor_tensor(sw[0:rt, t % 4], sexp[0:rt, t % 2],
                                        srec[0:rt, t, :].unsqueeze(2).to_broadcast([rt, H, S]), ALU.mult).then_inc(s["s_w"], 1)

            def normed(t):
                pool.wait_ge(s["n_rec"], t + 1)
                pool.wait_ge(s["s_w"], t + 1)
                if t >= 4:
                    pool.wait_ge(s["l_ps"], sum(pairs[0:t - 3]))
                    pool.wait_ge(s["snT_ps"], t - 3)
                rt = rows[t]
                nc.gpsimd.tensor_tensor(sn[0:rt, t % 4], sw[0:rt, t % 4], nrec[0:rt, t % 2], ALU.mult).then_inc(s["s_n"], 1)

            for i in range(NT + 1):
                if i >= 1:
                    normed(i - 1)
                if i < NT:
                    weights(i)

            pool.wait_ge(s["m_ps"], NT)
            pool.wait_ge(s["moe_in"], 5 * 16)
            for wi, hi in ((w1, w1h), (w2, w2h)):
                nc.gpsimd.tensor_copy(hi[:, :, :], wi[:, :, :]).then_inc(s["w_hi"], 1)
            for j, (wi, hi, lo) in enumerate(((w1, w1h, w1l), (w2, w2h, w2l))):
                pool.wait_ge(s["w_hi"], j + 1)
                nc.gpsimd.tensor_tensor(lo[:, :, :], wi[:, :, :], hi[:, :, :].bitcast(F32), ALU.subtract).then_inc(s["w_lo"], 1)

        @block.vector
        def _(dve):
            def cp(dst, src):
                return nc.vector.tensor_copy(dst, src)

            dve.wait_ge(s["f0_in"], 16 * 16)
            nc.vector.tensor_scalar(rtemp[:, :], temp[:, :], 0.1, 5.0, ALU.max, ALU.min).then_inc(s["rt"], 1)
            dve.wait_ge(s["rt"], 1)
            nc.vector.reciprocal(rtemp[:, :], rtemp[:, :]).then_inc(s["rt"], 1)
            dve.wait_ge(s["rt"], 2)
            dve.wait_ge(s["ws_ps"], 1)
            for i in range(2):
                nc.vector.tensor_tensor(ws[:, :].rearrange("p (h g) -> p h g", h=H)[:, i::2, :],
                                        bank[2 + 5 * i][0:A, 0:HH * S].rearrange("p (k g) -> p k g", k=HH),
                                        rtemp[:, i::2].unsqueeze(2).to_broadcast([A, HH, S]), ALU.mult).then_inc(s["ws_sb"], 1)
            dve.wait_ge(s["const"], CONSTS)
            nc.vector.tensor_tensor(pick[:, :], ident[0:LOW + E, 0:E], ident[0:LOW + E, LOW:LOW + E], ALU.add).then_inc(s["rt"], 1)
            nc.vector.tensor_copy(dispT[0:LOW, :], ident[0:LOW, LOW:LOW + 1].to_broadcast([LOW, TP])).then_inc(s["d_zero"], 1)
            for k in range(1, NCH, 2):
                reorder(k, dve, cp, s["re_odd"])
                dve.wait_ge(s["pix_ps"], k + 1)
                if k >= 2:
                    dve.wait_ge(s["tok_ps"], k - 1)
                cp(pixT[:, 1, :], bank[1][:, :]).then_inc(s["pix_odd"], 1)
            dve.wait_ge(s["small_in"], 5 * 16)
            cp(hT0[:, 0:T].rearrange("p (b n) -> p b n", n=N)[:, :, 0:1],
               cls[:, 0:1].unsqueeze(1).to_broadcast([D, B, 1])).then_inc(s["tok_sb"], 1)
            dve.wait_ge(s["htm_ps"], 1)
            cp(h[:, :, :], bank[3][0:R, 0:NT * D].rearrange("p (t d) -> p t d", t=NT)).then_inc(s["h_upd"], 1)

            def layernorm(k):
                dve.wait_ge(s["h_upd"], k + 1)
                nc.vector.tensor_reduce(musum[:, :], h[:, :, :], AX_X, ALU.add).then_inc(s["ln_sum"], 1)
                dve.wait_ge(s["ln_sum"], k + 1)
                nc.vector.scalar_tensor_tensor(out=xc[:, :, :], in0=musum[:, :].unsqueeze(2).to_broadcast([R, NT, D]),
                                               scalar=-1.0 / D, in1=h[:, :, :], op0=ALU.mult, op1=ALU.add).then_inc(s["ln_cen"], 1)
                dve.wait_ge(s["ln_sq"], k + 1)
                nc.vector.tensor_reduce(vsum[:, :], sq[:, :, :], AX_X, ALU.add).then_inc(s["ln_var"], 1)
                dve.wait_ge(s["ln_std"], k + 1)
                nc.vector.reciprocal(rstd[:, :], std[:, :]).then_inc(s["ln_rstd"], 1)
                dve.wait_ge(s["ln_rstd"], k + 1)
                nc.vector.tensor_tensor(xn[:, :, :], xc[:, :, :], rstd[:, :].unsqueeze(2).to_broadcast([R, NT, D]),
                                        ALU.mult).then_inc(s["ln_xn"], 1)
                dve.wait_ge(s["ln_ps"], k + 1)
                cp(xT[0:D, FIRST:TP], bank[7][0:D, 0:TP - FIRST]).then_inc(s["ln_xT"], 1)

            layernorm(0)

            for i in range(2):
                dve.wait_ge(s["k_ps"], i + 1)
                nc.vector.tensor_reduce(kmax[:, i * XC:(i + 1) * XC], bank[i][0:D, 0:HALF].rearrange("p (b n) -> p b n", n=N),
                                        AX_X, ALU.max).then_inc(s["k_max"], 1)
                dve.wait_ge(s["k_max"], i + 1)
                nc.vector.tensor_tensor(kexp[:, i * HALF:(i + 1) * HALF].rearrange("p (b n) -> p b n", n=N),
                                        bank[i][0:D, 0:HALF].rearrange("p (b n) -> p b n", n=N),
                                        kmax[:, i * XC:(i + 1) * XC].unsqueeze(2).to_broadcast([D, XC, N]),
                                        ALU.subtract).then_inc(s["k_sub"], 1)
            dve.wait_ge(s["k_exp"], 1)
            kv = kexp[:, :].rearrange("p (b n) -> p b n", n=N)
            nc.vector.tensor_reduce(ksum[:, :], kv, AX_X, ALU.add).then_inc(s["k_sum"], 1)
            dve.wait_ge(s["k_sum"], 1)
            nc.vector.reciprocal(krec[:, :], ksum[:, :]).then_inc(s["k_rec"], 1)
            dve.wait_ge(s["k_rec"], 1)
            nc.vector.tensor_tensor(smT[:, 0:T].rearrange("p (b n) -> p b n", n=N), kv,
                                    krec[:, :].unsqueeze(2).to_broadcast([D, B, N]), ALU.mult).then_inc(s["k_sm"], 1)
            for t in range(NT + 1):
                if t < NT and t % 2:
                    dve.wait_ge(s["v_sb"], 1)
                    if t >= 2:
                        dve.wait_ge(s["lam_ps"], t - 1)
                    nc.vector.tensor_tensor(vexp[:, 1], v0[:, t:t + 1, :].to_broadcast([R, G, D]),
                                            imgmask[:, :].unsqueeze(2).to_broadcast([R, G, D]), ALU.mult).then_inc(s["vexp_d"], 1)
                if t >= 1:
                    dve.wait_ge(s["lam_ps"], t)
                    nc.vector.bn_stats(stats[:, t - 1, :], bank[(t - 1) % 4][0:D, 0:imgs[t - 1] * D]).then_inc(s["bn_st"], 1)
            dve.wait_ge(s["bn_st"], NT)
            nc.vector.bn_aggr(mv[:, :], stats[:, :, :].rearrange("p t s -> p (t s)")).then_inc(s["bn_mv"], 1)
            dve.wait_ge(s["bn_std"], 1)
            nc.vector.reciprocal(bnr[:, :], bnl[:, :]).then_inc(s["bn_rstd"], 1)
            dve.wait_ge(s["bn_rstd"], 1)
            nc.vector.tensor_tensor(bna[:, :], gamma[:, :], bnr[:, :], ALU.mult).then_inc(s["bn_a"], 1)
            dve.wait_ge(s["bn_a"], 1)
            nc.vector.tensor_tensor(bnm[:, :], mv[:, 0:1], bna[:, :], ALU.mult).then_inc(s["bn_m"], 1)
            dve.wait_ge(s["bn_m"], 1)
            nc.vector.tensor_tensor(bnc[:, :], beta[:, :], bnm[:, :], ALU.subtract).then_inc(s["bn_c"], 1)
            dve.wait_ge(s["q_sb"], 2)
            nc.vector.tensor_scalar(qsT[:, 0:T], q0T[:, 0:T], bna[:, 0:1], None, ALU.mult).then_inc(s["q_scaled"], 1)

            def mask_attention(k, op_scalar):
                dve.wait_ge(s["at_ps"], k + 1)
                for b_, t0, t1_ in ((0, 0, NT - 1), (1, NT - 1, NT)):
                    src = bank[b_][0:R, 0:(t1_ - t0) * R].rearrange("p (t r) -> p t r", r=R)
                    m = (same if k == 0 else causal)[:, :].unsqueeze(1).to_broadcast([R, t1_ - t0, R])
                    if k == 0:
                        i_ = nc.vector.tensor_tensor(att[:, t0:t1_, :], src, m, ALU.mult)
                    else:
                        i_ = nc.vector.scalar_tensor_tensor(out=att[:, t0:t1_, :], in0=src, scalar=0.0, in1=m,
                                                            op0=ALU.max, op1=ALU.mult)
                    i_.then_inc(s["at_sb"], 1)

            def residual(k, ps):
                nc.vector.tensor_tensor(h[:, :, :], h[:, :, :], ps[0:R, 0:NT * D].rearrange("p (t d) -> p t d", t=NT),
                                        ALU.add).then_inc(s["h_upd"], 1)

            mask_attention(0, None)
            dve.wait_ge(s["ao_ps"], 1)
            residual(0, bank[5])
            layernorm(1)

            for hd in range(1, H, 2):
                for i in range(2):
                    n = 2 * hd + i
                    dve.wait_ge(s["t1_ps"], n + 1)
                    cp(t1[:, hd, i * HALF:(i + 1) * HALF], bank[n % 4][0:A, 0:HALF]).then_inc(s["t1_odd"], 1)

            def slice_softmax(t):
                rt = rows[t]
                ps = bank[0][0:rt, :].rearrange("p (h g) -> p h g", h=H)
                dve.wait_ge(s["s_ps"], t + 1)
                nc.vector.tensor_reduce(smax[0:rt, t, :], ps, AX_X, ALU.max).then_inc(s["s_max"], 1)
                dve.wait_ge(s["s_max"], t + 1)
                if t >= 2:
                    dve.wait_ge(s["s_w"], t - 1)
                nc.vector.tensor_tensor(sexp[0:rt, t % 2], ps, smax[0:rt, t, :].unsqueeze(2).to_broadcast([rt, H, S]),
                                        ALU.subtract).then_inc(s["s_sub"], 1)

            def slice_sum(t):
                rt = rows[t]
                dve.wait_ge(s["s_exp"], t + 1)
                nc.vector.tensor_reduce(ssum[0:rt, t, :], sexp[0:rt, t % 2], AX_X, ALU.add).then_inc(s["s_sum"], 1)
                dve.wait_ge(s["s_sum"], t + 1)
                nc.vector.reciprocal(srec[0:rt, t, :], ssum[0:rt, t, :]).then_inc(s["s_rec"], 1)

            def norm_rec(t):
                dve.wait_ge(s["n_eps"], t + 1)
                if t >= 2:
                    dve.wait_ge(s["s_n"], t - 1)
                nc.vector.reciprocal(nrec[0:rows[t], t % 2], neps[0:rows[t], t % 2]).then_inc(s["n_rec"], 1)

            def mask_pairs(ps_sem, dst, sb_sem, t, used):
                rt = rows[t]
                dve.wait_ge(ps_sem, t + 1)
                if t >= 2:
                    dve.wait_ge(used, t - 1)
                for i in range(2):
                    nc.vector.tensor_tensor(
                        dst[0:rt, t % 2, i::2, 0:rt],
                        bank[1 + i][0:rt, 0:HH * R].rearrange("p (k r) -> p k r", k=HH)[:, :, 0:rt],
                        same[0:rt, 0:rt].unsqueeze(1).to_broadcast([rt, HH, rt]), ALU.mult).then_inc(sb_sem, 1)

            def slice_attention_softmax(t, p):
                if 0 <= t < NT and p < pairs[t]:
                    u = sum(pairs[0:t]) + p
                    ps = bank[5 + u % 2][:, :].rearrange("p (h g) -> p h g", h=H)
                    dve.wait_ge(s["l_ps"], u + 1)
                    nc.vector.tensor_reduce(umax[:, t, p, :], ps, AX_X, ALU.max).then_inc(s["u_max"], 1)
                    dve.wait_ge(s["u_max"], u + 1)
                    if u >= 2:
                        dve.wait_ge(s["u_exp"], u - 1)
                    nc.vector.tensor_tensor(lg[:, u % 2], ps, umax[:, t, p, :].unsqueeze(2).to_broadcast([128, H, S]),
                                            ALU.subtract).then_inc(s["u_sub"], 1)

            def slice_attention_sum(t, p):
                if 0 <= t < NT and p < pairs[t]:
                    u = sum(pairs[0:t]) + p
                    dve.wait_ge(s["u_exp"], u + 1)
                    nc.vector.tensor_reduce(usum[:, t % 2, p, :], fe[:, t % 2, p], AX_X, ALU.add).then_inc(s["u_sum"], 1)
                    dve.wait_ge(s["u_sum"], u + 1)
                    nc.vector.reciprocal(urec[:, t % 2, :, p], usum[:, t % 2, p, :]).then_inc(s["u_rec"], 1)

            def scale_weights(t):
                np_ = pairs[t]
                dve.wait_ge(s["et_ps"], t + 1)
                dve.wait_ge(s["u_rec"], sum(pairs[0:t + 1]))
                if t >= 2:
                    dve.wait_ge(s["r_ps"], t - 1)
                for i in range(2):
                    for j in range(2):
                        src, dst = (slice(a * S, (a + 1) * S) for a in (i, j))

                        def view(a):
                            return a.rearrange("p k (q i n) -> p k q i n", q=G // 2, i=2)[:, :, 0:np_, j, :]

                        nc.vector.tensor_tensor(
                            view(etx[dst, t % 2, i::2, :]),
                            view(bank[1][src, 0:HH * R].rearrange("p (k r) -> p k r", k=HH)),
                            urec[dst, t % 2, i::2, 0:np_].unsqueeze(3).to_broadcast([S, HH, np_, N]),
                            ALU.mult).then_inc(s["et_sb"], 1)

            for i in range(NT + 3):
                if i < NT:
                    slice_softmax(i)
                if 0 <= i - 1 < NT:
                    norm_rec(i - 1)
                if i >= 3:
                    scale_weights(i - 3)
                slice_attention_softmax(i - 2, 0)
                if i < NT:
                    slice_sum(i)
                slice_attention_softmax(i - 2, 1)
                slice_attention_sum(i - 2, 0)
                if i >= 3:
                    mask_pairs(s["p_ps"], pT, s["p_sb"], i - 3, s["o_ps"])
                slice_attention_softmax(i - 2, 2)
                slice_attention_sum(i - 2, 1)
                slice_attention_sum(i - 2, 2)
                if i < NT:
                    mask_pairs(s["m_ps"], mm, s["m_sb"], i, s["z_ps"])
            dve.wait_ge(s["ot_ps"], 1)
            residual(1, bank[5])
            layernorm(2)

            mask_attention(1, None)
            dve.wait_ge(s["ao_ps"], 2)
            residual(2, bank[5])
            layernorm(3)

            dve.wait_ge(s["w_hi"], 2)
            cp(xS[0:D, FIRST:TP], bank[7][0:D, 0:TP - FIRST]).then_inc(s["x_hi_last"], 1)
            dve.wait_ge(s["x_hi"], 1)
            nc.vector.tensor_tensor(xS[D:2 * D, 0:FIRST], bank[6][0:D, 0:FIRST], xS[0:D, 0:FIRST].bitcast(F32), ALU.subtract).then_inc(s["x_lo"], 1)
            dve.wait_ge(s["x_hi_last"], 1)
            nc.vector.tensor_tensor(xS[D:2 * D, FIRST:TP], bank[7][0:D, 0:TP - FIRST], xS[0:D, FIRST:TP].bitcast(F32), ALU.subtract).then_inc(s["x_lo"], 1)

            steps = [0]

            def step(ins):
                steps[0] += 1
                ins.then_inc(s["g_step"], 1)
                dve.wait_ge(s["g_step"], steps[0])

            gps = bank[3][0:R, 0:NT * E].rearrange("p (t e) -> p t e", t=NT)

            def over(a):
                return a[:, :].unsqueeze(2).to_broadcast([R, NT, E])

            ranks = rev[:, :].unsqueeze(1).to_broadcast([R, NT, E])
            dve.wait_ge(s["g_ps"], 1)
            step(nc.vector.tensor_reduce(gmax[:, :], gps, AX_X, ALU.max))
            nc.vector.tensor_tensor(gd[:, :, :], gps, over(gmax), ALU.subtract).then_inc(s["g_sub"], 1)
            dve.wait_ge(s["g_sub"], 1)
            step(nc.vector.scalar_tensor_tensor(out=gc[:, :, :], in0=gd[:, :, :], scalar=0.0, in1=ranks, op0=ALU.is_ge, op1=ALU.mult))
            step(nc.vector.tensor_reduce(gr[:, :], gc[:, :, :], AX_X, ALU.max))
            step(nc.vector.tensor_tensor(gs1[:, :, :], gc[:, :, :], over(gr), ALU.is_equal))
            step(nc.vector.scalar_tensor_tensor(out=gd2[:, :, :], in0=gs1[:, :, :], scalar=-1e30, in1=gd[:, :, :], op0=ALU.mult, op1=ALU.add))
            step(nc.vector.tensor_reduce(gr[:, :], gd2[:, :, :], AX_X, ALU.max))
            step(nc.vector.tensor_tensor(gs2[:, :, :], gd2[:, :, :], over(gr), ALU.is_equal))
            step(nc.vector.tensor_tensor(gc[:, :, :], gs2[:, :, :], ranks, ALU.mult))
            step(nc.vector.tensor_reduce(gr[:, :], gc[:, :, :], AX_X, ALU.max))
            step(nc.vector.tensor_tensor(gs2[:, :, :], gc[:, :, :], over(gr), ALU.is_equal))
            step(nc.vector.tensor_tensor(gs2[:, :, :], gs1[:, :, :], gs2[:, :, :], ALU.add))
            dve.wait_ge(s["g_exp"], 1)
            step(nc.vector.tensor_tensor(gw[:, :, :], gs2[:, :, :], ge[:, :, :], ALU.mult))
            step(nc.vector.tensor_reduce(gr[:, :], gw[:, :, :], AX_X, ALU.add))
            step(nc.vector.reciprocal(gr[:, :], gr[:, :]))
            nc.vector.tensor_tensor(gw[:, :, :], gw[:, :, :], over(gr), ALU.mult).then_inc(s["g_disp"], 1)
            dve.wait_ge(s["d_sb"], 2)
            nc.vector.tensor_tensor(dispT[LOW:LOW + E, 0:FIRST], bank[4][0:E, 0:FIRST], dispT[0:E, 0:FIRST].bitcast(F32), ALU.subtract).then_inc(s["d_lo"], 1)
            nc.vector.tensor_tensor(dispT[LOW:LOW + E, FIRST:TP], bank[5][0:E, 0:TP - FIRST], dispT[0:E, FIRST:TP].bitcast(F32), ALU.subtract).then_inc(s["d_lo"], 1)
            for n in range(2 * E):
                dve.wait_ge(s["e_silu"], n + 1)
                dve.wait_ge(s["e2_ps"], n + 1)
                nc.vector.tensor_tensor(hid[:, n % 2, :], silu[:, n % 2, :], bank[2 + n % 2][:, 0:HALF], ALU.mult).then_inc(s["e_hid"], 1)
                dve.wait_ge(s["e_hid"], n + 1)
                dve.wait_ge(s["db_ps"], n + 1)
                if n >= 2:
                    dve.wait_ge(s["e_out"], n - 1)
                nc.vector.tensor_tensor(hidw[:, n % 2, :], hid[:, n % 2, :], bank[4 + n % 2][:, 0:HALF], ALU.mult).then_inc(s["e_w"], 1)
            dve.wait_ge(s["e_fin"], 1)
            nc.vector.tensor_tensor(xn[:, :, :], h[:, :, :], bank[0][0:R, 0:NT * D].rearrange("p (t d) -> p t d", t=NT),
                                    ALU.add).then_inc(s["e_res"], 1)

        @block.tensor
        def _(pe):
            def mm_(o, l, r, start=True, stop=True):
                return nc.tensor.matmul(o, l, r, start=start, stop=stop)

            def tr(o, i, n):
                return nc.tensor.transpose(o, i, ident[0:n, 0:n])

            pe.wait_ge(s["const"], CONSTS)
            pe.wait_ge(s["tokw_in"], 16)
            for k in range(NCH):
                last = tr(bank[0][:, k * D:(k + 1) * D], tokw[:, k * 128:(k + 1) * 128], D)
            last.then_inc(s["tokwT_ps"], 1)
            pe.wait_ge(s["f0_in"], 16 * 16)
            for b_, w in ((1, wfx_a), (2, wx_a)):
                for k in range(HH):
                    last = tr(bank[b_][:, k * A:(k + 1) * A], w[:, k * 128:(k + 1) * 128], A)
                last.then_inc(s["wT_ps"], 1)
            tr(bank[3][:, 0:D], wv2[:, :, :].rearrange("p a d -> p (a d)"), D).then_inc(s["wT_ps"], 1)
            pe.wait_ge(s["wT_sb"], 3)
            heads = [(hd // 2, slice((hd % 2) * D, (hd % 2 + 1) * D)) for hd in range(H)]
            for b_, w in ((4, wq2), (5, wk2)):
                for k, half in heads:
                    last = mm_(bank[b_][half, k * A:(k + 1) * A], w[half, :], wfxT[half, k, :])
                last.then_inc(s["ab_ps"], 1)
            for k, half in heads:
                last = mm_(bank[6][half, k * D:(k + 1) * D], wvT[half, :], wout[half, k, :])
            last.then_inc(s["wvo_ps"], 1)
            for hd, (k, half) in enumerate(heads):
                o = bank[2 + 5 * (hd % 2)][0:A, k * S:(k + 1) * S]
                mm_(o, wxT[half, k, :], wslice[half, :], True, False)
                last = mm_(o, e64[half.start:half.start + 1, :], bslice[half.start:half.start + 1, :], False, True)
            last.then_inc(s["ws_ps"], 1)
            pe.wait_ge(s["ab_sb"], 2)
            pe.wait_ge(s["tokwT_sb"], 1)
            for hd, (k, half) in enumerate(heads):
                last = mm_(bank[hd % 2][0:A, k * A:(k + 1) * A], qT[half, k, :], kT[half, k, :])
            last.then_inc(s["gram_ps"], 1)
            pe.wait_ge(s["wvo_sb"], 1)
            pe.wait_ge(s["ws_sb"], 2)
            for hd, (k, half) in enumerate(heads):
                last = mm_(bank[6 + hd % 2][0:A, k * D:(k + 1) * D], wfxT[half, k, :], wvo[half, k, :])
            last.then_inc(s["vo_ps"], 1)
            pe.wait_ge(s["l1_in"], 6 * 16)
            mm_(bank[4][0:D, 0:D], l1q[:, :], l1k[:, :])
            tr(bank[4][0:D, D:2 * D], l1o[:, :], D).then_inc(s["l1_ps"], 1)
            pe.wait_ge(s["l1_sb"], 2)
            mm_(bank[5][0:D, 0:D], l1v[:, :], l1oT[:, :]).then_inc(s["l1b_ps"], 1)

            pe.wait_ge(s["gram_sb"], 2)
            pe.wait_ge(s["ws_sb"], 2)

            def pixels(k):
                return s["pix_odd"] if k % 2 else s["pix_even"]

            for k in range(NCH + 1):
                if k < NCH:
                    pe.wait_ge(s["re_odd"] if k % 2 else s["re_even"], k // 2 + 1)
                    if k >= 2:
                        pe.wait_ge(pixels(k - 2), (k - 2) // 2 + 1)
                    for w in range(HP):
                        last = tr(bank[k % 2][:, w * 128:(w + 1) * 128], xre[:, k % 2, w * 128:(w + 1) * 128], 128)
                    last.then_inc(s["pix_ps"], 1)
                if k >= 1:
                    pe.wait_ge(pixels(k - 1), (k - 1) // 2 + 1)
                    mm_(bank[2][0:D, :], tokwT[:, k - 1, :], pixT[:, (k - 1) % 2, :], k == 1, k == NCH).then_inc(s["tok_ps"], 1)
            pe.wait_ge(s["tok_sb"], HP + 1)
            pe.wait_ge(s["vo_sb"], 2)
            for t in range(NT):
                last = tr(bank[3][0:R, t * D:(t + 1) * D], hT0[:, t * R:(t + 1) * R], D)
            last.then_inc(s["htm_ps"], 1)

            def layernorm(k):
                pe.wait_ge(s["ln_xn"], k + 1)
                for t in range(NT):
                    b_, c0 = (6, t * R) if t < NT - 1 else (7, 0)
                    last = tr(bank[b_][0:D, c0:c0 + R], xn[:, t, :], R)
                last.then_inc(s["ln_ps"], 1)
                pe.wait_ge(s["ln_xT"], 2 * (k + 1))

            layernorm(0)

            pe.wait_ge(s["a0_in"], 6 * 16)
            for i in range(2):
                mm_(bank[i][0:D, 0:HALF], wk_a[:, :], xT[:, i * HALF:(i + 1) * HALF]).then_inc(s["k_ps"], 1)
            for t in range(NT):
                last = mm_(bank[4][0:R, t * D:(t + 1) * D], xT[:, t * R:(t + 1) * R], wv_a[:, :])
            last.then_inc(s["v_ps"], 1)
            for i in range(2):
                mm_(bank[2 + i][0:D, 0:HALF], wq_a[:, :], xT[:, i * HALF:(i + 1) * HALF]).then_inc(s["q_ps"], 1)
            pe.wait_ge(s["k_sm"], 1)
            pe.wait_ge(s["l1b_sb"], 1)
            for t in range(NT):
                last = tr(bank[5][0:R, t * D:(t + 1) * D], smT[:, t * R:(t + 1) * R], D)
            last.then_inc(s["sm_ps"], 1)
            pe.wait_ge(s["sm_sb"], 1)
            pe.wait_ge(s["q_sb"], 2)
            for t in range(NT):
                if t % 2:
                    pe.wait_ge(s["vexp_d"], t // 2 + 1)
                else:
                    pe.wait_ge(s["vexp_p"], t // 2 + 1)
                if t >= 4:
                    pe.wait_ge(s["bn_st"], t - 3)
                mm_(bank[t % 4][0:D, 0:imgs[t] * D], sm[:, t, :],
                    vexp[:, t % 2, 0:imgs[t], :]).then_inc(s["lam_ps"], 1)
            pe.wait_ge(s["bn_st"], NT)
            pe.wait_ge(s["q_scaled"], 1)

            def attention(left, right, k):
                for t in range(NT):
                    b_, c0 = (0, t * R) if t < NT - 1 else (1, 0)
                    last = mm_(bank[b_][0:R, c0:c0 + R], left[0:D, t * R:(t + 1) * R], right[0:D, t * R:(t + 1) * R])
                last.then_inc(s["at_ps"], 1)
                pe.wait_ge(s["at_sb"], 2 * (k + 1))

            attention(smT, qsT, 0)
            for t in range(NT):
                mm_(bank[5][0:R, t * D:(t + 1) * D], att[:, t, :], v0[:, t, :], True, False)
                last = mm_(bank[5][0:R, t * D:(t + 1) * D], q0T[:, t * R:(t + 1) * R],
                           bnc[:, 0:1].to_broadcast([D, D]), False, True)
            last.then_inc(s["ao_ps"], 1)
            layernorm(1)

            for hd in range(H):
                for i in range(2):
                    n = 2 * hd + i
                    if n >= 4:
                        before = hd - 2
                        pe.wait_ge(s["t1_odd"] if before % 2 else s["t1_even"], before // 2 * 2 + i + 1)
                    mm_(bank[n % 4][0:A, 0:HALF], gram[:, hd, :], xT[:, i * HALF:(i + 1) * HALF]).then_inc(s["t1_ps"], 1)
            pe.wait_ge(s["t1_even"], H)
            pe.wait_ge(s["t1_odd"], H)

            def slots(t):
                return slice(t * R, t * R + rows[t])

            def slice_logits(t):
                if t >= 1:
                    pe.wait_ge(s["s_sub"], t)
                if t >= 4:
                    pe.wait_ge(s["vo_sb2"], t - 3)
                mm_(bank[0][0:rows[t], :], xT[:, slots(t)], ws[:, :]).then_inc(s["s_ps"], 1)

            def norms(t):
                rt = rows[t]
                pe.wait_ge(s["s_w"], t + 1)
                if t >= 3:
                    pe.wait_ge(s["o_sb"], t - 2)
                mm_(bank[4][0:rt, :], same[0:rt, 0:rt], sw[0:rt, t % 4].rearrange("p h g -> p (h g)")).then_inc(s["n_ps"], 1)

            def token_products(t):
                rt = rows[t]
                if t >= 3:
                    pe.wait_ge(s["p_sb"], 2 * (t - 2))
                elif t >= 1:
                    pe.wait_ge(s["m_sb"], 2 * t)
                for hd in range(H):
                    c0 = hd // 2 * R
                    last = mm_(bank[1 + hd % 2][0:rt, c0:c0 + rt], t1[:, hd, slots(t)], xT[:, slots(t)])
                last.then_inc(s["m_ps"], 1)

            def z(t):
                rt = rows[t]
                pe.wait_ge(s["s_n"], t + 1)
                pe.wait_ge(s["m_sb"], 2 * (t + 1))
                if t >= 1:
                    pe.wait_ge(s["z_sb"], sum(imgs[0:t]))
                for hd in range(H):
                    last = mm_(bank[7][0:rt, hd * S:(hd + 1) * S], mm[0:rt, t % 2, hd, 0:rt], sn[0:rt, t % 4, hd, :])
                last.then_inc(s["z_ps"], 1)

            def slices_T(t):
                rt = rows[t]
                if t >= 1:
                    pe.wait_ge(s["r_sb"], t)
                for k in range(HH):
                    last = tr(bank[3][:, k * R:k * R + rt], sn[0:rt, t % 4, 2 * k:2 * k + 2, :].rearrange("p h g -> p (h g)"), rt)
                last.then_inc(s["snT_ps"], 1)

            def logits(t, p):
                if 0 <= t < NT and p < pairs[t]:
                    rt = rows[t]
                    pe.wait_ge(s["z_sb"], sum(imgs[0:t + 1]))
                    u = sum(pairs[0:t]) + p
                    if u >= 2:
                        pe.wait_ge(s["u_sub"], u - 1)
                    for hd in range(H):
                        for j in range(2):
                            last = mm_(bank[5 + u % 2][j * S:(j + 1) * S, hd * S:(hd + 1) * S],
                                       zx[0:rt, t % 2, 2 * p + j, hd * S:(hd + 1) * S], sn[0:rt, t % 4, hd, :])
                    last.then_inc(s["l_ps"], 1)

            def weights_T(t):
                rt = rows[t]
                pe.wait_ge(s["m_sb"], 2 * min(t + 3, NT))
                for k in range(HH):
                    last = tr(bank[1][:, k * R:k * R + rt], sw[0:rt, t % 4, 2 * k:2 * k + 2, :].rearrange("p h g -> p (h g)"), rt)
                last.then_inc(s["et_ps"], 1)

            def project_values(t):
                if t + 3 < NT:
                    pe.wait_ge(s["s_sub"], t + 4)
                else:
                    pe.wait_ge(s["s_sub"], NT)
                if t >= 1:
                    pe.wait_ge(s["vo_sb2"], t)
                mm_(bank[0][0:rows[t], :], xT[:, slots(t)], vo[:, :]).then_inc(s["vo_ps2"], 1)

            def r(t):
                pe.wait_ge(s["et_sb"], 4 * (t + 1))
                pe.wait_ge(s["u_exp"], sum(pairs[0:t + 1]))
                pe.wait_ge(s["snT_sb"], t + 1)
                for p in range(pairs[t]):
                    for hd, (k, half) in enumerate(heads):
                        c0 = k * R + p * 2 * N
                        last = mm_(bank[3][half, c0:c0 + 2 * N], fe[:, t % 2, p, hd, :], etx[:, t % 2, hd, p * 2 * N:(p + 1) * 2 * N])
                last.then_inc(s["r_ps"], 1)

            def products_back(t):
                rt = rows[t]
                pe.wait_ge(s["r_sb"], t + 1)
                for hd, (k, half) in enumerate(heads):
                    c0 = k * R
                    last = mm_(bank[1 + hd % 2][0:rt, c0:c0 + rt], snT[half, t % 2, k, 0:rt], rT[half, t % 2, k, 0:rt])
                last.then_inc(s["p_ps"], 1)

            def output(t):
                rt = rows[t]
                pe.wait_ge(s["p_sb"], 2 * (t + 1))
                pe.wait_ge(s["vo_sb2"], t + 1)
                pe.wait_ge(s["n_eps"], min(t + 3, NT))
                for hd in range(H):
                    last = mm_(bank[4][0:D, 0:rt], vox[0:rt, t % 2, hd, :], pT[0:rt, t % 2, hd, 0:rt], hd == 0, hd == H - 1)
                last.then_inc(s["o_ps"], 1)

            for i in range(NT + 3):
                if 0 <= i - 1 < NT:
                    norms(i - 1)
                if i < NT:
                    slice_logits(i)
                if i >= 3:
                    weights_T(i - 3)
                    slices_T(i - 3)
                logits(i - 2, 0)
                if i >= 3:
                    project_values(i - 3)
                    r(i - 3)
                logits(i - 2, 1)
                if 0 <= i - 1 < NT:
                    z(i - 1)
                if i >= 3:
                    products_back(i - 3)
                logits(i - 2, 2)
                if i >= 3:
                    output(i - 3)
                if i < NT:
                    token_products(i)
            pe.wait_ge(s["o_sb"], NT)
            for t in range(NT):
                last = tr(bank[5][0:R, t * D:(t + 1) * D], hT0[:, t * R:(t + 1) * R], D)
            last.then_inc(s["ot_ps"], 1)
            layernorm(2)

            for i in range(2):
                mm_(bank[i][0:D, 0:HALF], g1[:, :], xT[0:D, i * HALF:(i + 1) * HALF]).then_inc(s["t_ps"], 1)
            for t in range(NT):
                last = mm_(bank[4][0:R, t * D:(t + 1) * D], xT[0:D, t * R:(t + 1) * R], vo1[:, :])
            last.then_inc(s["v_ps"], 1)
            pe.wait_ge(s["t_sb"], 2)
            attention(xT, qsT, 1)
            pe.wait_ge(s["v_sb"], 2)
            for t in range(NT):
                last = mm_(bank[5][0:R, t * D:(t + 1) * D], att[:, t, :], vt1[:, t, :])
            last.then_inc(s["ao_ps"], 1)
            layernorm(3)

            for t in range(NT):
                last = mm_(bank[3][0:R, t * E:(t + 1) * E], xT[:, t * R:(t + 1) * R], gate_a[:, :])
            last.then_inc(s["g_ps"], 1)
            pe.wait_ge(s["moe_in"], 5 * 16)
            pe.wait_ge(s["g_disp"], 1)
            for t in range(NT):
                b_, c0 = (4, t * R) if t < NT - 1 else (5, 0)
                last = tr(bank[b_][0:E, c0:c0 + R], gw[:, t, :], R)
            last.then_inc(s["d_ps"], 1)
            pe.wait_ge(s["rt"], 3)
            pe.wait_ge(s["w_lo"], 2)
            pe.wait_ge(s["x_lo"], 2)

            def down(n):
                e, i = divmod(n, 2)
                pe.wait_ge(s["e_w"], n + 1)
                mm_(bank[6 + i][0:D, 0:HALF], w3[:, e, :], hidw[:, n % 2, :], e == 0, e == E - 1).then_inc(s["e_out"], 1)

            for n in range(2 * E):
                e, i = divmod(n, 2)
                cols = slice(i * HALF, (i + 1) * HALF)
                if n >= 2:
                    pe.wait_ge(s["e_silu"], n - 1)
                    pe.wait_ge(s["e_hid"], n - 1)
                mm_(bank[n % 2][:, 0:HALF], w1h[:, e, :], xS[:, cols], True, False)
                mm_(bank[n % 2][:, 0:HALF], w1l[:, e, :], xS[:, cols], False, True).then_inc(s["e1_ps"], 1)
                mm_(bank[2 + n % 2][:, 0:HALF], w2h[:, e, :], xS[:, cols], True, False)
                mm_(bank[2 + n % 2][:, 0:HALF], w2l[:, e, :], xS[:, cols], False, True).then_inc(s["e2_ps"], 1)
                if n == 0:
                    pe.wait_ge(s["d_lo"], 2)
                if n >= 2:
                    pe.wait_ge(s["e_w"], n - 1)
                mm_(bank[4 + n % 2][:, 0:HALF], pick[:, e:e + 1].to_broadcast([LOW + E, HID]), dispT[:, cols]).then_inc(s["db_ps"], 1)
                if n >= 1:
                    down(n - 1)
            down(2 * E - 1)
            pe.wait_ge(s["e_outT"], 2)
            for t in range(NT):
                last = tr(bank[0][0:R, t * D:(t + 1) * D], hT0[:, t * R:(t + 1) * R], D)
            last.then_inc(s["e_fin"], 1)


_INS = ['x', 'cls_tok', 'L0_tok_W', 'L0_tok_b', 'L0_attn_W_qk', 'L0_attn_b_qk', 'L0_attn_W_v', 'L0_attn_b_v',
        'L0_attn_gamma', 'L0_attn_beta', 'L0_ffn_W_fx', 'L0_ffn_b_fx', 'L0_ffn_W_x', 'L0_ffn_b_x', 'L0_ffn_W_slice',
        'L0_ffn_b_slice', 'L0_ffn_W_q', 'L0_ffn_W_k', 'L0_ffn_W_v', 'L0_ffn_W_out', 'L0_ffn_b_out',
        'L0_ffn_temperature', 'L1_attn_Wq', 'L1_attn_Wk', 'L1_attn_Wv', 'L1_attn_Wo', 'L1_ffn_gate_w',
        'L1_ffn_gate_b', 'L1_ffn_w1', 'L1_ffn_w2', 'L1_ffn_w3']
_OUTS = [((32, 17, 64), 'float32')]


def kernel(**inputs):
    import numpy as _np
    import concourse.bacc as _bacc
    from concourse import mybir as _mybir
    from concourse.bass_utils import run_bass_kernel_spmd as _run

    nc = _bacc.Bacc("TRN2", target_bir_lowering=False, num_devices=1)
    arrays, args = {}, []
    for name in _INS:
        a = _np.ascontiguousarray(inputs[name])
        arrays[f"in_{name}_dram"] = a
        args.append(nc.dram_tensor(f"in_{name}_dram", a.shape, _mybir.dt.from_np(a.dtype), kind="ExternalInput").ap())
    for i, (shape, dtype) in enumerate(_OUTS):
        dt = _mybir.dt.from_np(_np.dtype(dtype))
        args.append(nc.dram_tensor(f"out_{i}_dram", shape, dt, kind="ExternalOutput").ap())
    vit_tower_kernel(nc, *args)
    r = _run(nc, [arrays], core_ids=[0])
    got = tuple(r.results[0][f"out_{i}_dram"] for i in range(len(_OUTS)))
    return got[0]
```

```python
from contextlib import ExitStack

import concourse.bass as bass
from concourse import mybir

F32 = mybir.dt.float32
F32R = mybir.dt.float32r
ALU = mybir.AluOpType
ACT = mybir.ActivationFunctionType
AX_X = mybir.AxisListType.X

EPS = 1e-5


def vit_tower_kernel(nc, x, cls_tok, tok_W, tok_b, a0_W_qk, a0_b_qk, a0_W_v, a0_b_v, a0_gamma, a0_beta,
                     f0_W_fx, f0_b_fx, f0_W_x, f0_b_x, f0_W_slice, f0_b_slice, f0_W_q, f0_W_k, f0_W_v,
                     f0_W_out, f0_b_out, f0_temperature, a1_Wq, a1_Wk, a1_Wv, a1_Wo,
                     f1_gate_w, f1_gate_b, f1_w1, f1_w2, f1_w3, out):
    B, C, IMG, _ = x.shape
    D = cls_tok.shape[2]
    PATCH = 16
    HP = IMG // PATCH
    N = HP * HP + 1
    G = 6
    R = G * N
    NT = -(-B // G)
    TP = NT * R
    T = B * N
    H = f0_temperature.shape[1]
    HH = H // 2
    S = f0_W_slice.shape[1]
    E, _, HID = f1_w1.shape
    A = D + 1
    HALF = T // 2
    XC = HALF // N
    FIRST = (512 // R) * R
    IH = 8
    NCH = C * PATCH // IH
    assert D == 64 and S == 64 and B * HP == 128 and R <= 128 and HID == 128 and C == 3
    LOW = 32
    rows = [min(G, B - t * G) * N for t in range(NT)]
    imgs = [min(G, B - t * G) for t in range(NT)]
    pairs = [n // 2 for n in imgs]

    with ExitStack() as ctx:
        def sb(name, shape, dt=F32):
            return ctx.enter_context(nc.sbuf_tensor(name, shape, dt))

        def sem(name):
            return ctx.enter_context(nc.semaphore(name))

        bank = [ctx.enter_context(nc.psum_tensor(f"bank{i}", [128, 512], F32)) for i in range(8)]

        region = sb("region", [128, 2 * G * H * S])
        XIN, PIX = C * PATCH * IMG, 2 * 512
        CH = HP * 128
        xin = region[:, 0:XIN].rearrange("p (c n) -> p c n", c=C)
        pixT = region[:, XIN:XIN + PIX].rearrange("p (k n) -> p k n", k=2)
        tokw = region[0:D, XIN + PIX:XIN + PIX + C * PATCH * PATCH]
        silu, hid, hidw = (region[0:HID, i * 2 * HALF:(i + 1) * 2 * HALF].rearrange("p (a n) -> p a n", a=2) for i in range(3))
        zx = region[0:R, :].rearrange("p (a i n) -> p a i n", a=2, i=G)
        tokb = sb("tokb", [D, 1])
        cls = sb("cls", [D, 1])
        wk_a = sb("wk_a", [A, D])
        wq_a = sb("wq_a", [A, D])
        wv_a = sb("wv_a", [A, D])
        gamma = sb("gamma", [D, 1])
        beta = sb("beta", [D, 1])
        wfx_a = sb("wfx_a", [A, H * D])
        wx_a = sb("wx_a", [A, H * D])
        wslice = sb("wslice", [128, S])
        bslice = sb("bslice", [D + 1, S])
        wq2 = sb("wq2", [128, D])
        wk2 = sb("wk2", [128, D])
        wv2 = sb("wv2", [D, 2, D])
        wout = sb("wout", [128, HH, D])
        bout = sb("bout", [D, 1])
        temp = sb("temp", [128, H])
        l1q = sb("l1q", [D, D])
        l1k = sb("l1k", [D, D])
        l1v = sb("l1v", [D, D])
        l1o = sb("l1o", [D, D])
        gate_a = sb("gate_a", [A, E])
        w3 = sb("w3", [HID, E, D])

        ident = sb("ident", [128, 128])
        EPSC = sb("eps_col", [128, 1])
        imgmask = sb("imgmask", [R, G])
        same = sb("same", [R, R])
        causal = sb("causal", [R, R])
        fold = sb("fold", [A, D])
        pickb = sb("pickb", [A, 2 * D])
        ONE = sb("one_col", [128, 1])
        rev = sb("rev", [R, E])
        pick = sb("pick", [LOW + E, E], F32R)

        tokwT = sb("tokwT", [128, NCH, D])
        wfxT = sb("wfxT", [128, HH, 2, D])
        wxT = sb("wxT", [128, HH, 2, D])
        wvT = sb("wvT", [128, D])
        rtemp = sb("rtemp", [128, H])
        ws = sb("ws", [128, H, S])
        wsh, wsl = (sb(n, [128, H, S], F32R) for n in ("wsh", "wsl"))
        qT = sb("qT", [128, HH, 2, D])
        kT = sb("kT", [128, HH, 2, D])
        gramh, graml = (sb(n, [128, H, 2 * D], F32R) for n in ("gramh", "graml"))
        wvo = sb("wvo", [128, HH, D])
        voh, vol = (sb(n, [128, H, D], F32R) for n in ("voh", "vol"))
        g1 = sb("g1", [D, D])
        l1oT = sb("l1oT", [D, D])
        vo1 = sb("vo1", [D, D])

        hT0 = sb("hT0", [D, TP])
        h = sb("h", [R, NT, D])
        musum = sb("musum", [R, NT])
        xc = sb("xc", [R, NT, D])
        sq = sb("sq", [R, NT, D])
        vsum = sb("vsum", [R, NT])
        std = sb("std", [R, NT])
        spare = sb("spare", [1, 16])
        rstd = sb("rstd", [R, NT])
        xn = sb("xn", [R, NT, D])
        xT = sb("xT", [A, TP])
        xS = sb("xS", [2 * D, TP], F32R)

        kmax = sb("kmax", [D, B])
        ksum = sb("ksum", [D, B])
        krec = sb("krec", [D, B])
        smT = sb("smT", [D, TP])
        q0T = sb("q0T", [D, TP])
        qsT = sb("qsT", [D, TP])
        v0 = sb("v0", [R, NT, D])
        stats = sb("stats", [D, NT, 6])
        mv = sb("mv", [D, 2])
        bnl = sb("bnl", [D, 1])
        bnr = sb("bnr", [D, 1])
        bna = sb("bna", [D, 1])
        bnm = sb("bnm", [D, 1])
        bnc = sb("bnc", [D, 1])
        att = sb("att", [R, NT, R])
        vt1 = sb("vt1", [R, NT, D])

        smax = sb("smax", [R, NT, H])
        ssum = sb("ssum", [R, NT, H])
        srec = sb("srec", [R, NT, H])
        sexp = sb("sexp", [R, 2, H, S])
        sw = sb("sw", [R, 2, H, S])
        nsum = sb("nsum", [128, 2, HH, G])
        nrec = sb("nrec", [128, 2, HH, G])
        snT = sb("snT", [128, 3, HH, R])
        sn = sb("sn", [R, 2, H, S])
        mm = sb("mm", [R, 2, H, R])
        lg = sb("lg", [128, 2, H, S])
        umax = sb("umax", [128, NT, G // 2, H])
        usum = sb("usum", [128, 2, G // 2, H])
        urec = sb("urec", [128, 2, G // 2, H])
        etx = sb("etx", [128, 3, H, R])
        rT = sb("rT", [128, 2, HH, R])
        pT = sb("pT", [R, 2, H, R])
        vox = sb("vox", [R, 2, H, D])

        gmax = sb("gmax", [R, NT])
        gd = sb("gd", [R, NT, E])
        ge = sb("ge", [R, NT, E])
        gc = sb("gc", [R, NT, E])
        gr = sb("gr", [R, NT])
        gs1 = sb("gs1", [R, NT, E])
        gd2 = sb("gd2", [R, NT, E])
        gs2 = sb("gs2", [R, NT, E])
        gw = sb("gw", [R, NT, E])
        dispT = sb("dispT", [LOW + E, TP], F32R)

        with ExitStack() as early:
            xre = early.enter_context(nc.sbuf_tensor("xre", [128, 2, CH], F32))
            kexp = early.enter_context(nc.sbuf_tensor("kexp", [D, T], F32))
            sm = early.enter_context(nc.sbuf_tensor("sm", [R, NT, D], F32))
            vexp = early.enter_context(nc.sbuf_tensor("vexp", [R, 2, G, D], F32))
        fe = sb("fe", [128, 2, G // 2, H, S])
        with ExitStack() as early:
            t1h, t1l = (early.enter_context(nc.sbuf_tensor(n, [2 * D, H, T], F32R)) for n in ("t1h", "t1l"))
        with ExitStack() as early:
            w1, w2 = (early.enter_context(nc.sbuf_tensor(n, [2 * D, E, HID], F32)) for n in ("w1", "w2"))
        w1l, w2l, w1h, w2h = (sb(n, [2 * D, E, HID], F32R) for n in ("w1l", "w2l", "w1h", "w2h"))

        names = """x_in0 x_in1 x_in2 tokw_in a0_in f0_in l1_in moe_in w12_in small_in fx_in ident const late
            tokwT_ps tokwT_sb re_even re_odd pix_ps pix_even pix_odd tok_ps tok_sb htm_ps h_upd
            wT_ps wT_sb ab_ps ab_sb pick gram_ps gram_hi gram_sb ws_ps ws_sb ws_hi ws_lo rt wvo_ps wvo_sb vo_ps vo_hi vo_sb l1_ps l1_sb l1b_ps l1b_sb
            ln_sum ln_cen ln_sq ln_var ln_std ln_rstd ln_xn ln_ps ln_xT
            k_ps q_ps v_ps k_max k_sub k_exp k_sum k_rec k_sm q_sb v_sb sm_ps sm_sb vexp_d vexp_p lam_ps bn_st bn_mv bn_std
            bn_rstd bn_a bn_m bn_c q_scaled at_ps at_sb ao_ps
            t1_ps t1_hi t1_lo s_ps s_max s_sub s_exp s_sum s_rec s_w n_sum n_eps n_rec s_n m_ps m_sb z_ps z_sb sn_ps snT_sb
            l_ps u_max u_sub u_exp u_sum u_rec u_w et_ps et_sb r_ps r_sb p_ps p_sb vo_ps2 vo_sb2 o_ps o_sb ot_ps
            t_ps t_sb
            w_hi w_lo x_pad x_hi x_hi_last x_lo g_ps g_max g_sub g_exp g_step g_disp d_zero d_ps d_sb d_lo e1_ps e2_ps db_ps e_silu e_hid e_w e_out e_outT e_fin
            e_res stored""".split()
        s = {n: sem(n) for n in names}

        CONSTS = 20
        LATE = 3 + N + E

        block = ctx.enter_context(nc.Block())

        def row(v):
            return v.rearrange("(a n) -> a n", a=1)

        def col(v):
            return v.rearrange("(n a) -> n a", a=1)

        @block.sync
        def _(sp):
            xv = x.rearrange("b c (hp i) w -> c b hp (i w)", hp=HP)
            sp.dma_start(tokw[:, :], tok_W).then_inc(s["tokw_in"], 16)
            for c in range(C):
                for b0 in range(0, B, B // 4):
                    sp.dma_start(xin[b0 * HP:(b0 + B // 4) * HP, c, :], xv[c, b0:b0 + B // 4]).then_inc(s[f"x_in{c}"], 16)
            for group, loads in (
                    ("small_in", ((tokb[:, :], col(tok_b)), (cls[:, :], col(cls_tok.rearrange("a b d -> (a b d)"))),
                                  (bout[:, :], col(f0_b_out)), (gamma[:, :], col(a0_gamma)), (beta[:, :], col(a0_beta)))),
                    ("fx_in", ((wfx_a[0:D, :], f0_W_fx), (wfx_a[D:A, :], row(f0_b_fx)),
                               (wx_a[0:D, :], f0_W_x), (wx_a[D:A, :], row(f0_b_x)),
                               (wv2[:, 0, :], f0_W_v), (wv2[:, 1, :], f0_W_v))),
                    ("a0_in", ((wk_a[0:D, :], a0_W_qk[1]), (wk_a[D:A, :], a0_b_qk[1:2, :]),
                               (wq_a[0:D, :], a0_W_qk[0]), (wq_a[D:A, :], a0_b_qk[0:1, :]),
                               (wv_a[0:D, :], a0_W_v), (wv_a[D:A, :], row(a0_b_v)))),
                    ("f0_in", ((wq2[0:D, :], f0_W_q), (wq2[D:128, :], f0_W_q), (wk2[0:D, :], f0_W_k), (wk2[D:128, :], f0_W_k),
                               (wout[:, :, :], f0_W_out.rearrange("(a p) d -> p a d", p=128)),
                               (wslice[0:D, :], f0_W_slice), (wslice[D:128, :], f0_W_slice),
                               (bslice[0:1, :], row(f0_b_slice)), (bslice[D:D + 1, :], row(f0_b_slice)),
                               (temp[:, :], f0_temperature.rearrange("a h b c -> a (h b c)").to_broadcast([128, H])))),
                    ("l1_in", ((l1q[:, :], a1_Wq), (l1k[:, :], a1_Wk), (l1v[:, :], a1_Wv), (l1o[:, :], a1_Wo),
                               (gate_a[0:D, :], f1_gate_w), (gate_a[D:A, :], row(f1_gate_b)))),
                    ("moe_in", ((w3[:, :, :], f1_w3.rearrange("e f d -> f e d")),))):
                for dst, src in loads:
                    sp.dma_start(dst, src).then_inc(s[group], 16)
            sp.wait_ge(s["m_ps"], NT)
            for half in (slice(0, D), slice(D, 2 * D)):
                sp.dma_start(w1[half, :, :], f1_w1.rearrange("e d f -> d e f")).then_inc(s["w12_in"], 16)
                sp.dma_start(w2[half, :, :], f1_w2.rearrange("e d f -> d e f")).then_inc(s["w12_in"], 16)
            sp.wait_ge(s["e_res"], 1)
            ov = out.rearrange("b n d -> (b n) d")
            full = NT - 1
            sp.dma_start(ov[0:full * R, :].rearrange("(t p) d -> p t d", p=R), xn[:, 0:full, :]).then_inc(s["stored"], 16)
            sp.dma_start(ov[full * R:T, :], xn[0:rows[full], full, :]).then_inc(s["stored"], 16)
            sp.wait_ge(s["stored"], 32)

        def reorder(k, engine, copy, done):
            c, ih = divmod(k, PATCH // IH)
            engine.wait_ge(s[f"x_in{c}"], 4 * 16)
            if k >= 2:
                engine.wait_ge(s["pix_ps"], k - 1)
            v = xin[:, c, :].rearrange("p (i w j) -> p w i j", i=PATCH, w=HP)
            copy(xre[:, k % 2, :].rearrange("p (w i j) -> p w i j", w=HP, i=IH),
                 v[:, :, ih * IH:(ih + 1) * IH, :]).then_inc(done, 1)

        @block.scalar
        def _(act):
            def evac(dst, src):
                return nc.scalar.activation(dst, src, ACT.Copy)

            act.wait_ge(s["tokwT_ps"], 1)
            evac(tokwT[:, :, :], bank[0][:, 0:NCH * D].rearrange("p (k d) -> p k d", k=NCH)).then_inc(s["tokwT_sb"], 1)
            for k in range(0, NCH, 2):
                reorder(k, act, evac, s["re_even"])
                act.wait_ge(s["pix_ps"], k + 1)
                if k >= 2:
                    act.wait_ge(s["tok_ps"], k - 1)
                evac(pixT[:, 0, :], bank[0][:, :]).then_inc(s["pix_even"], 1)
            act.wait_ge(s["small_in"], 5 * 16)
            act.wait_ge(s["tok_ps"], NCH)
            for j in range(HP):
                nc.scalar.activation(
                    hT0[:, 0:T].rearrange("p (b n) -> p b n", n=N)[:, :, 1 + j::HP],
                    bank[2][0:D, j * B * HP:(j + 1) * B * HP].rearrange("p (b a) -> p b a", a=HP),
                    ACT.Identity, bias=tokb[:, 0:1]).then_inc(s["tok_sb"], 1)

            loads = [0]

            def tables(function):
                nc.scalar.activation(spare[:, loads[0]:loads[0] + 1], EPSC[0:1, 0:1], function)
                loads[0] += 1

            def layernorm(k, while_waiting=lambda: None):
                tables(ACT.Sqrt)
                act.wait_ge(s["ln_cen"], k + 1)
                nc.scalar.activation(sq[:, :, :], xc[:, :, :], ACT.Square).then_inc(s["ln_sq"], 1)
                act.wait_ge(s["ln_var"], k + 1)
                nc.scalar.activation(std[:, :], vsum[:, :], ACT.Sqrt, bias=EPSC[0:R, 0:1], scale=1.0 / D).then_inc(s["ln_std"], 1)
                tables(ACT.Exp)
                while_waiting()
                act.wait_ge(s["ln_ps"], k + 1)
                evac(xT[0:D, 0:FIRST], bank[6][0:D, 0:FIRST]).then_inc(s["ln_xT"], 1)

            def twice(ps):
                return ps[:, 0:HH * D].rearrange("p (k d) -> p k d", k=HH).unsqueeze(2).to_broadcast([128, HH, 2, D])

            def folded_first():
                act.wait_ge(s["wT_ps"], 1)
                evac(wfxT[:, :, :, :], twice(bank[0])).then_inc(s["wT_sb"], 1)
                act.wait_ge(s["wT_ps"], 2)
                evac(wxT[:, :, :, :], twice(bank[1])).then_inc(s["wT_sb"], 1)
                act.wait_ge(s["wT_ps"], 3)
                evac(wvT[:, :], bank[2][:, 0:D]).then_inc(s["wT_sb"], 1)

            def folded_second():
                act.wait_ge(s["ab_ps"], 1)
                nc.scalar.activation(qT[:, :, :, :], twice(bank[6]), ACT.Copy, scale=float(D) ** -0.5).then_inc(s["ab_sb"], 1)
                act.wait_ge(s["ab_ps"], 2)
                evac(kT[:, :, :, :], twice(bank[7])).then_inc(s["ab_sb"], 1)
                act.wait_ge(s["wvo_ps"], 1)
                evac(wvo[:, :, :], bank[5][:, 0:HH * D].rearrange("p (k d) -> p k d", k=HH)).then_inc(s["wvo_sb"], 1)

            def folded_third():
                act.wait_ge(s["gram_ps"], 1)
                for i in range(2):
                    evac(gramh[:, i::2, :], bank[i][:, :].rearrange("p (k d) -> p k d", k=HH)).then_inc(s["gram_hi"], 1)

            def folded_fourth():
                act.wait_ge(s["vo_ps"], 1)
                for i in range(2):
                    evac(voh[:, i::2, :], bank[2 + i][:, 0:HH * D].rearrange("p (k d) -> p k d", k=HH)).then_inc(s["vo_hi"], 1)

            layernorm(0, folded_first)

            for i in range(2):
                act.wait_ge(s["q_ps"], i + 1)
                evac(q0T[:, i * HALF:(i + 1) * HALF], bank[2 + i][0:D, 0:HALF]).then_inc(s["q_sb"], 1)
            act.wait_ge(s["v_ps"], 1)
            evac(v0[:, :, :], bank[4][0:R, 0:NT * D].rearrange("p (t d) -> p t d", t=NT)).then_inc(s["v_sb"], 1)
            act.wait_ge(s["k_sub"], 2)
            nc.scalar.activation(kexp[:, :], kexp[:, :], ACT.Exp).then_inc(s["k_exp"], 1)
            folded_second()
            act.wait_ge(s["sm_ps"], 1)
            evac(sm[:, :, :], bank[5][0:R, 0:NT * D].rearrange("p (t d) -> p t d", t=NT)).then_inc(s["sm_sb"], 1)
            tables(ACT.Sqrt)
            act.wait_ge(s["bn_mv"], 1)
            nc.scalar.activation(bnl[:, :], mv[:, 1:2], ACT.Sqrt, bias=EPSC[0:D, 0:1]).then_inc(s["bn_std"], 1)

            layernorm(1, folded_third)

            act.wait_ge(s["x_pad"], 2)
            evac(xS[0:D - 1, 0:FIRST], bank[6][0:D - 1, 0:FIRST]).then_inc(s["x_hi"], 1)
            folded_fourth()

            def product_parts(n):
                i, hd = divmod(n, H)
                act.wait_ge(s["t1_ps"], n + 1)
                evac(t1h[:, hd, i * HALF:(i + 1) * HALF], bank[3 + n % 4][:, 0:HALF]).then_inc(s["t1_hi"], 1)

            act.wait_ge(s["l1_ps"], 1)
            evac(g1[:, :], bank[4][0:D, 0:D]).then_inc(s["l1_sb"], 1)
            evac(l1oT[:, :], bank[4][0:D, D:2 * D]).then_inc(s["l1_sb"], 1)
            act.wait_ge(s["l1b_ps"], 1)
            evac(vo1[:, :], bank[5][0:D, 0:D]).then_inc(s["l1b_sb"], 1)

            def slice_exp(t):
                act.wait_ge(s["s_sub"], t + 1)
                if t >= 2:
                    act.wait_ge(s["s_w"], t - 1)
                nc.scalar.activation(sexp[0:rows[t], t % 2], sexp[0:rows[t], t % 2], ACT.Exp).then_inc(s["s_exp"], 1)

            def blocks(t):
                act.wait_ge(s["snT_sb"], t + 1)
                if t >= 3:
                    act.wait_ge(s["r_ps"], t - 2)
                np_ = pairs[t]
                for i in range(2):
                    for j in range(2):
                        src, dst = (slice(a * S, (a + 1) * S) for a in (i, j))

                        def view(a):
                            return a.rearrange("p k (q i n) -> p k q i n", q=G // 2, i=2)[:, :, 0:np_, j, :]

                        evac(view(etx[dst, t % 3, i::2, :]),
                             view(bank[3][src, 0:HH * R].rearrange("p (k r) -> p k r", k=HH))).then_inc(s["et_sb"], 1)

            def spread_z(t, p):
                if not (0 <= t < NT and p < pairs[t]):
                    return
                act.wait_ge(s["z_ps"], t + 1)
                if t >= 2:
                    act.wait_ge(s["l_ps"], sum(pairs[0:t - 1]))
                for i in (2 * p, 2 * p + 1):
                    nc.scalar.activation(zx[0:rows[t], t % 2, i, :], bank[7][0:rows[t], :], ACT.Copy,
                                         scale=imgmask[0:rows[t], i:i + 1]).then_inc(s["z_sb"], 1)

            def slices(t):
                act.wait_ge(s["sn_ps"], t + 1)
                if t >= 2:
                    act.wait_ge(s["l_ps"], sum(pairs[0:t - 1]))
                evac(sn[0:rows[t], t % 2], bank[4][0:rows[t], :].rearrange("p (h g) -> p h g", h=H)).then_inc(s["s_n"], 1)

            def values(t):
                act.wait_ge(s["vo_ps2"], t + 1)
                if t >= 2:
                    act.wait_ge(s["o_ps"], t - 1)
                evac(vox[0:rows[t], t % 2], bank[0][0:rows[t], :].rearrange("p (h d) -> p h d", h=H)).then_inc(s["vo_sb2"], 1)

            def slice_attention_exp(t, p):
                if 0 <= t < NT and p < pairs[t]:
                    u = sum(pairs[0:t]) + p
                    act.wait_ge(s["u_sub"], u + 1)
                    if t >= 2:
                        act.wait_ge(s["r_ps"], t - 1)
                    nc.scalar.activation(fe[:, t % 2, p], lg[:, u % 2], ACT.Exp).then_inc(s["u_exp"], 1)

            def r_out(t):
                act.wait_ge(s["r_ps"], t + 1)
                if t >= 2:
                    act.wait_ge(s["p_ps"], t - 1)
                evac(rT[:, t % 2, :, 0:rows[t]],
                     bank[3][:, 0:HH * R].rearrange("p (k r) -> p k r", k=HH)[:, :, 0:rows[t]]).then_inc(s["r_sb"], 1)

            def o_out(t):
                act.wait_ge(s["o_ps"], t + 1)
                nc.scalar.activation(hT0[:, t * R:t * R + rows[t]], bank[4][0:D, 0:rows[t]], ACT.Identity,
                                     bias=bout[:, 0:1]).then_inc(s["o_sb"], 1)

            for i in range(NT + 3):
                if 0 <= i - 1 < NT:
                    slices(i - 1)
                if i < NT:
                    slice_exp(i)
                if i == 0:
                    for n in range(2 * H):
                        product_parts(n)
                slice_attention_exp(i - 2, 0)
                spread_z(i - 1, 0)
                if i >= 3:
                    r_out(i - 3)
                slice_attention_exp(i - 2, 1)
                spread_z(i - 1, 1)
                if i >= 3:
                    values(i - 3)
                slice_attention_exp(i - 2, 2)
                spread_z(i - 1, 2)
                if i < NT:
                    blocks(i)
                if i >= 3:
                    o_out(i - 3)

            layernorm(2)

            for i in range(2):
                act.wait_ge(s["t_ps"], i + 1)
                evac(qsT[:, i * HALF:(i + 1) * HALF], bank[i][0:D, 0:HALF]).then_inc(s["t_sb"], 1)
            act.wait_ge(s["v_ps"], 2)
            evac(vt1[:, :, :], bank[4][0:R, 0:NT * D].rearrange("p (t d) -> p t d", t=NT)).then_inc(s["v_sb"], 1)

            layernorm(3)

            evac(xS[0:D, 0:FIRST], bank[6][0:D, 0:FIRST]).then_inc(s["x_hi"], 1)
            act.wait_ge(s["g_sub"], 1)
            nc.scalar.activation(ge[:, :, :], gd[:, :, :], ACT.Exp).then_inc(s["g_exp"], 1)
            tables(ACT.Silu)
            act.wait_ge(s["d_zero"], 1)
            act.wait_ge(s["d_ps"], 1)
            evac(dispT[0:E, 0:FIRST], bank[4][0:E, 0:FIRST]).then_inc(s["d_sb"], 1)
            evac(dispT[0:E, FIRST:TP], bank[5][0:E, 0:TP - FIRST]).then_inc(s["d_sb"], 1)
            for n in range(2 * E):
                act.wait_ge(s["e1_ps"], n + 1)
                if n >= 2:
                    act.wait_ge(s["e_hid"], n - 1)
                nc.scalar.activation(silu[:, n % 2, :], bank[n % 2][:, 0:HALF], ACT.Silu).then_inc(s["e_silu"], 1)
            act.wait_ge(s["e_out"], 2 * E)
            for i in range(2):
                evac(hT0[:, i * HALF:(i + 1) * HALF], bank[6 + i][0:D, 0:HALF]).then_inc(s["e_outT"], 1)

        @block.gpsimd
        def _(pool):
            made = {"ident": 0, "const": 0, "late": 0}

            def link(ins, what):
                made[what] += 1
                ins.then_inc(s[what], 1)
                pool.wait_ge(s[what], made[what])

            def fill(t, value, what="const"):
                link(nc.gpsimd.memset(t, value), what)

            def select(t, pattern, base, mult, op, value, what="const"):
                link(nc.gpsimd.affine_select(out=t, in_=t, pattern=pattern, base=base, channel_multiplier=mult,
                                             compare_op=op, fill=value), what)

            fill(ident[:, :], 0.0, "ident")
            select(ident[:, :], [[-1, 128]], 0, 1, ALU.not_equal, 1.0, "ident")
            fill(fold[:, :], 0.0)
            select(fold[:, :], [[-1, D]], 0, 1, ALU.not_equal, 1.0)
            select(fold[:, :], [[0, D]], 1 - D, 1, ALU.not_equal, -1.0)
            fill(fold[:, D - 1:D], 0.0)
            fill(fold[D:A, D - 1:D], 1.0)
            fill(pickb[:, :], 0.0)
            fill(pickb[:, D - 1::D], 1.0)
            fill(ONE[:, :], 1.0)
            fill(EPSC[:, :], EPS)
            fill(xT[D:A, :], 1.0)
            for pad in (hT0, smT, q0T, qsT):
                fill(pad[:, T:TP], 0.0)
            fill(imgmask[:, :], 1.0)
            select(imgmask[:, :], [[-N, G]], 0, 1, ALU.is_ge, 0.0)
            select(imgmask[:, :], [[N, G]], N - 1, -1, ALU.is_ge, 0.0)
            same3 = same[:, :].rearrange("p (i n) -> p i n", i=G)
            fill(same[:, :], 1.0)
            select(same3, [[-N, G], [0, N]], 0, 1, ALU.is_ge, 0.0)
            select(same3, [[N, G], [0, N]], N - 1, -1, ALU.is_ge, 0.0)
            assert made["const"] == CONSTS
            fill(etx[:, :, :, :], 0.0, "late")
            causal3 = causal[:, :].rearrange("p (i n) -> p i n", i=G)
            for l in range(N):
                fill(causal3[:, :, l:l + 1], 1.0 / max(l, 1), "late")
            select(causal3, [[-N, G], [0, N]], 0, 1, ALU.is_ge, 0.0, "late")
            select(causal3, [[N, G], [1, N]], 0, -1, ALU.is_ge, 0.0, "late")
            for e in range(E):
                fill(rev[:, e:e + 1], float(E - e), "late")
            assert made["late"] == LATE

            for t in range(0, NT, 2):
                pool.wait_ge(s["v_sb"], 1)
                if t >= 2:
                    pool.wait_ge(s["lam_ps"], t - 1)
                nc.gpsimd.tensor_tensor(vexp[:, 0], v0[:, t:t + 1, :].to_broadcast([R, G, D]),
                                        imgmask[:, :].unsqueeze(2).to_broadcast([R, G, D]), ALU.mult).then_inc(s["vexp_p"], 1)

            def weights(t):
                pool.wait_ge(s["s_rec"], t + 1)
                if t >= 2:
                    pool.wait_ge(s["et_ps"], t - 1)
                rt = rows[t]
                nc.gpsimd.tensor_tensor(sw[0:rt, t % 2], sexp[0:rt, t % 2],
                                        srec[0:rt, t, :].unsqueeze(2).to_broadcast([rt, H, S]), ALU.mult).then_inc(s["s_w"], 1)

            def scaled(t):
                for p in range(pairs[t]):
                    pool.wait_ge(s["u_rec"], sum(pairs[0:t]) + p + 1)
                    nc.gpsimd.tensor_tensor(fe[:, t % 2, p], fe[:, t % 2, p],
                                            urec[:, t % 2, p, :].unsqueeze(2).to_broadcast([128, H, S]), ALU.mult).then_inc(s["u_w"], 1)

            for i in range(NT + 2):
                if i < NT:
                    weights(i)
                if i >= 2:
                    scaled(i - 2)

            pool.wait_ge(s["m_ps"], NT)
            pool.wait_ge(s["w12_in"], 4 * 16)
            for wi, hi in ((w1, w1h), (w2, w2h)):
                nc.gpsimd.tensor_copy(hi[:, :, :], wi[:, :, :]).then_inc(s["w_hi"], 1)
            for j, (wi, hi, lo) in enumerate(((w1, w1h, w1l), (w2, w2h, w2l))):
                pool.wait_ge(s["w_hi"], j + 1)
                nc.gpsimd.tensor_tensor(lo[:, :, :], wi[:, :, :], hi[:, :, :].bitcast(F32), ALU.subtract).then_inc(s["w_lo"], 1)

        @block.vector
        def _(dve):
            def cp(dst, src):
                return nc.vector.tensor_copy(dst, src)

            dve.wait_ge(s["const"], CONSTS)
            dve.wait_ge(s["ident"], 2)
            nc.vector.tensor_tensor(pick[:, :], ident[0:LOW + E, 0:E], ident[0:LOW + E, LOW:LOW + E], ALU.add).then_inc(s["pick"], 1)
            nc.vector.tensor_copy(dispT[0:LOW, :], ident[0:LOW, LOW:LOW + 1].to_broadcast([LOW, TP])).then_inc(s["d_zero"], 1)
            nc.vector.tensor_copy(xS[D // 2:D, :], ONE[D // 2:D, 0:1].to_broadcast([D // 2, TP])).then_inc(s["x_pad"], 1)
            nc.vector.tensor_copy(xS[D + D // 2:2 * D, :], ident[D + D // 2:2 * D, 0:1].to_broadcast([D // 2, TP])).then_inc(s["x_pad"], 1)
            for k in range(1, NCH, 2):
                reorder(k, dve, cp, s["re_odd"])
                dve.wait_ge(s["pix_ps"], k + 1)
                if k >= 2:
                    dve.wait_ge(s["tok_ps"], k - 1)
                cp(pixT[:, 1, :], bank[1][:, :]).then_inc(s["pix_odd"], 1)
            dve.wait_ge(s["small_in"], 5 * 16)
            cp(hT0[:, 0:T].rearrange("p (b n) -> p b n", n=N)[:, :, 0:1],
               cls[:, 0:1].unsqueeze(1).to_broadcast([D, B, 1])).then_inc(s["tok_sb"], 1)
            dve.wait_ge(s["htm_ps"], 1)
            cp(h[:, :, :], bank[3][0:R, 0:NT * D].rearrange("p (t d) -> p t d", t=NT)).then_inc(s["h_upd"], 1)

            def layernorm(k, while_waiting=lambda: None):
                dve.wait_ge(s["h_upd"], k + 1)
                nc.vector.tensor_reduce(musum[:, :], h[:, :, :], AX_X, ALU.add).then_inc(s["ln_sum"], 1)
                dve.wait_ge(s["ln_sum"], k + 1)
                nc.vector.scalar_tensor_tensor(out=xc[:, :, :], in0=musum[:, :].unsqueeze(2).to_broadcast([R, NT, D]),
                                               scalar=-1.0 / D, in1=h[:, :, :], op0=ALU.mult, op1=ALU.add).then_inc(s["ln_cen"], 1)
                dve.wait_ge(s["ln_sq"], k + 1)
                nc.vector.tensor_reduce(vsum[:, :], sq[:, :, :], AX_X, ALU.add).then_inc(s["ln_var"], 1)
                dve.wait_ge(s["ln_std"], k + 1)
                nc.vector.reciprocal(rstd[:, :], std[:, :]).then_inc(s["ln_rstd"], 1)
                dve.wait_ge(s["ln_rstd"], k + 1)
                nc.vector.tensor_tensor(xn[:, :, :], xc[:, :, :], rstd[:, :].unsqueeze(2).to_broadcast([R, NT, D]),
                                        ALU.mult).then_inc(s["ln_xn"], 1)
                while_waiting()
                dve.wait_ge(s["ln_ps"], k + 1)
                cp(xT[0:D, FIRST:TP], bank[7][0:D, 0:TP - FIRST]).then_inc(s["ln_xT"], 1)

            layernorm(0)

            for i in range(2):
                dve.wait_ge(s["k_ps"], i + 1)
                nc.vector.tensor_reduce(kmax[:, i * XC:(i + 1) * XC], bank[i][0:D, 0:HALF].rearrange("p (b n) -> p b n", n=N),
                                        AX_X, ALU.max).then_inc(s["k_max"], 1)
                dve.wait_ge(s["k_max"], i + 1)
                nc.vector.tensor_tensor(kexp[:, i * HALF:(i + 1) * HALF].rearrange("p (b n) -> p b n", n=N),
                                        bank[i][0:D, 0:HALF].rearrange("p (b n) -> p b n", n=N),
                                        kmax[:, i * XC:(i + 1) * XC].unsqueeze(2).to_broadcast([D, XC, N]),
                                        ALU.subtract).then_inc(s["k_sub"], 1)
            dve.wait_ge(s["k_exp"], 1)
            kv = kexp[:, :].rearrange("p (b n) -> p b n", n=N)
            nc.vector.tensor_reduce(ksum[:, :], kv, AX_X, ALU.add).then_inc(s["k_sum"], 1)
            dve.wait_ge(s["k_sum"], 1)
            nc.vector.reciprocal(krec[:, :], ksum[:, :]).then_inc(s["k_rec"], 1)
            dve.wait_ge(s["k_rec"], 1)
            nc.vector.tensor_tensor(smT[:, 0:T].rearrange("p (b n) -> p b n", n=N), kv,
                                    krec[:, :].unsqueeze(2).to_broadcast([D, B, N]), ALU.mult).then_inc(s["k_sm"], 1)
            for t in range(NT + 1):
                if t < NT and t % 2:
                    dve.wait_ge(s["v_sb"], 1)
                    if t >= 2:
                        dve.wait_ge(s["lam_ps"], t - 1)
                    nc.vector.tensor_tensor(vexp[:, 1], v0[:, t:t + 1, :].to_broadcast([R, G, D]),
                                            imgmask[:, :].unsqueeze(2).to_broadcast([R, G, D]), ALU.mult).then_inc(s["vexp_d"], 1)
                if t >= 1:
                    dve.wait_ge(s["lam_ps"], t)
                    nc.vector.bn_stats(stats[:, t - 1, :], bank[(t - 1) % 4][0:D, 0:imgs[t - 1] * D]).then_inc(s["bn_st"], 1)
            dve.wait_ge(s["bn_st"], NT)
            nc.vector.bn_aggr(mv[:, :], stats[:, :, :].rearrange("p t s -> p (t s)")).then_inc(s["bn_mv"], 1)
            dve.wait_ge(s["bn_std"], 1)
            nc.vector.reciprocal(bnr[:, :], bnl[:, :]).then_inc(s["bn_rstd"], 1)
            dve.wait_ge(s["bn_rstd"], 1)
            nc.vector.tensor_tensor(bna[:, :], gamma[:, :], bnr[:, :], ALU.mult).then_inc(s["bn_a"], 1)
            dve.wait_ge(s["bn_a"], 1)
            nc.vector.tensor_tensor(bnm[:, :], mv[:, 0:1], bna[:, :], ALU.mult).then_inc(s["bn_m"], 1)
            dve.wait_ge(s["bn_m"], 1)
            nc.vector.tensor_tensor(bnc[:, :], beta[:, :], bnm[:, :], ALU.subtract).then_inc(s["bn_c"], 1)
            dve.wait_ge(s["q_sb"], 2)
            nc.vector.tensor_scalar(qsT[:, 0:T], q0T[:, 0:T], bna[:, 0:1], None, ALU.mult).then_inc(s["q_scaled"], 1)

            def split_tokens(j, feats):
                dve.wait_ge(s["ln_ps"], 2 * j + 2)
                cp(xS[0:feats, FIRST:TP], bank[7][0:feats, 0:TP - FIRST]).then_inc(s["x_hi_last"], 1)
                dve.wait_ge(s["x_hi_last"], j + 1)
                nc.vector.tensor_tensor(xS[D:D + feats, FIRST:TP], bank[7][0:feats, 0:TP - FIRST],
                                        xS[0:feats, FIRST:TP].bitcast(F32), ALU.subtract).then_inc(s["x_lo"], 1)
                dve.wait_ge(s["x_hi"], j + 1)
                nc.vector.tensor_tensor(xS[D:D + feats, 0:FIRST], bank[6][0:feats, 0:FIRST],
                                        xS[0:feats, 0:FIRST].bitcast(F32), ALU.subtract).then_inc(s["x_lo"], 1)

            def mask_attention(k, op_scalar):
                dve.wait_ge(s["at_ps"], k + 1)
                for b_, t0, t1_ in ((0, 0, NT - 1), (1, NT - 1, NT)):
                    src = bank[b_][0:R, 0:(t1_ - t0) * R].rearrange("p (t r) -> p t r", r=R)
                    m = (same if k == 0 else causal)[:, :].unsqueeze(1).to_broadcast([R, t1_ - t0, R])
                    if k == 0:
                        i_ = nc.vector.tensor_tensor(att[:, t0:t1_, :], src, m, ALU.mult)
                    else:
                        i_ = nc.vector.scalar_tensor_tensor(out=att[:, t0:t1_, :], in0=src, scalar=0.0, in1=m,
                                                            op0=ALU.max, op1=ALU.mult)
                    i_.then_inc(s["at_sb"], 1)

            def residual(k, ps):
                nc.vector.tensor_tensor(h[:, :, :], h[:, :, :], ps[0:R, 0:NT * D].rearrange("p (t d) -> p t d", t=NT),
                                        ALU.add).then_inc(s["h_upd"], 1)

            dve.wait_ge(s["f0_in"], 10 * 16)
            nc.vector.tensor_scalar(rtemp[:, :], temp[:, :], 0.1, 5.0, ALU.max, ALU.min).then_inc(s["rt"], 1)
            dve.wait_ge(s["rt"], 1)
            nc.vector.reciprocal(rtemp[:, :], rtemp[:, :]).then_inc(s["rt"], 1)
            dve.wait_ge(s["rt"], 2)
            dve.wait_ge(s["ws_ps"], 1)
            for i in range(2):
                nc.vector.tensor_tensor(ws[:, i::2, :], bank[6 + i][:, 0:HH * S].rearrange("p (k g) -> p k g", k=HH),
                                        rtemp[:, i::2].unsqueeze(2).to_broadcast([128, HH, S]), ALU.mult).then_inc(s["ws_sb"], 1)
            mask_attention(0, None)
            dve.wait_ge(s["ws_sb"], 2)
            cp(wsh[:, :, :], ws[:, :, :]).then_inc(s["ws_hi"], 1)
            dve.wait_ge(s["ws_hi"], 1)
            nc.vector.tensor_tensor(wsl[:, :, :], ws[:, :, :], wsh[:, :, :].bitcast(F32), ALU.subtract).then_inc(s["ws_lo"], 1)

            def folded_low():
                for i in range(2):
                    dve.wait_ge(s["gram_hi"], i + 1)
                    nc.vector.tensor_tensor(graml[:, i::2, :], bank[i][:, :].rearrange("p (k d) -> p k d", k=HH),
                                            gramh[:, i::2, :].bitcast(F32), ALU.subtract).then_inc(s["gram_sb"], 1)

            def values_low():
                for i in range(2):
                    dve.wait_ge(s["vo_hi"], i + 1)
                    nc.vector.tensor_tensor(vol[:, i::2, :], bank[2 + i][:, 0:HH * D].rearrange("p (k d) -> p k d", k=HH),
                                            voh[:, i::2, :].bitcast(F32), ALU.subtract).then_inc(s["vo_sb"], 1)

            dve.wait_ge(s["ao_ps"], 1)
            residual(0, bank[5])
            layernorm(1, folded_low)

            split_tokens(0, D - 1)
            values_low()

            def product_parts(n):
                i, hd = divmod(n, H)
                dve.wait_ge(s["t1_hi"], n + 1)
                nc.vector.tensor_tensor(t1l[:, hd, i * HALF:(i + 1) * HALF], bank[3 + n % 4][:, 0:HALF],
                                        t1h[:, hd, i * HALF:(i + 1) * HALF].bitcast(F32), ALU.subtract).then_inc(s["t1_lo"], 1)

            def slice_softmax(t):
                rt = rows[t]
                ps = bank[0][0:rt, :].rearrange("p (h g) -> p h g", h=H)
                dve.wait_ge(s["s_ps"], t + 1)
                nc.vector.tensor_reduce(smax[0:rt, t, :], ps, AX_X, ALU.max).then_inc(s["s_max"], 1)
                dve.wait_ge(s["s_max"], t + 1)
                if t >= 2:
                    dve.wait_ge(s["s_w"], t - 1)
                nc.vector.tensor_tensor(sexp[0:rt, t % 2], ps, smax[0:rt, t, :].unsqueeze(2).to_broadcast([rt, H, S]),
                                        ALU.subtract).then_inc(s["s_sub"], 1)

            def slice_sum(t):
                rt = rows[t]
                dve.wait_ge(s["s_exp"], t + 1)
                nc.vector.tensor_reduce(ssum[0:rt, t, :], sexp[0:rt, t % 2], AX_X, ALU.add).then_inc(s["s_sum"], 1)
                dve.wait_ge(s["s_sum"], t + 1)
                nc.vector.reciprocal(srec[0:rt, t, :], ssum[0:rt, t, :]).then_inc(s["s_rec"], 1)

            def norms(t):
                rt, im = rows[t], imgs[t]
                ps = bank[3][:, 0:HH * R].rearrange("p (k i n) -> p k i n", k=HH, i=G)[:, :, 0:im, :]
                dve.wait_ge(s["et_ps"], t + 1)
                nc.vector.tensor_reduce(nsum[:, t % 2, :, 0:im], ps, AX_X, ALU.add).then_inc(s["n_sum"], 1)
                dve.wait_ge(s["n_sum"], t + 1)
                nc.vector.tensor_scalar(nsum[:, t % 2, :, 0:im], nsum[:, t % 2, :, 0:im], EPS, None, ALU.add).then_inc(s["n_eps"], 1)
                dve.wait_ge(s["n_eps"], t + 1)
                nc.vector.reciprocal(nrec[:, t % 2, :, 0:im], nsum[:, t % 2, :, 0:im]).then_inc(s["n_rec"], 1)
                dve.wait_ge(s["n_rec"], t + 1)
                if t >= 3:
                    dve.wait_ge(s["p_ps"], t - 2)
                nc.vector.tensor_tensor(snT[:, t % 3, :, 0:rt].rearrange("p k (i n) -> p k i n", n=N), ps,
                                        nrec[:, t % 2, :, 0:im].unsqueeze(3).to_broadcast([128, HH, im, N]), ALU.mult).then_inc(s["snT_sb"], 1)

            def mask_pairs(ps_sem, dst, heads_of, sb_sem, t, used):
                rt = rows[t]
                dve.wait_ge(ps_sem, t + 1)
                if t >= 2:
                    dve.wait_ge(used, t - 1)
                for i in range(2):
                    nc.vector.tensor_tensor(
                        dst[0:rt, t % 2, heads_of[i], 0:rt],
                        bank[1 + i][0:rt, 0:HH * R].rearrange("p (k r) -> p k r", k=HH)[:, :, 0:rt],
                        same[0:rt, 0:rt].unsqueeze(1).to_broadcast([rt, HH, rt]), ALU.mult).then_inc(sb_sem, 1)

            def slice_attention_softmax(t, p):
                if 0 <= t < NT and p < pairs[t]:
                    u = sum(pairs[0:t]) + p
                    ps = bank[5 + u % 2][:, :].rearrange("p (h g) -> p h g", h=H)
                    dve.wait_ge(s["l_ps"], u + 1)
                    nc.vector.tensor_reduce(umax[:, t, p, :], ps, AX_X, ALU.max).then_inc(s["u_max"], 1)
                    dve.wait_ge(s["u_max"], u + 1)
                    if u >= 2:
                        dve.wait_ge(s["u_exp"], u - 1)
                    nc.vector.tensor_tensor(lg[:, u % 2], ps, umax[:, t, p, :].unsqueeze(2).to_broadcast([128, H, S]),
                                            ALU.subtract).then_inc(s["u_sub"], 1)

            def slice_attention_sum(t, p):
                if 0 <= t < NT and p < pairs[t]:
                    u = sum(pairs[0:t]) + p
                    dve.wait_ge(s["u_exp"], u + 1)
                    nc.vector.tensor_reduce(usum[:, t % 2, p, :], fe[:, t % 2, p], AX_X, ALU.add).then_inc(s["u_sum"], 1)
                    dve.wait_ge(s["u_sum"], u + 1)
                    nc.vector.reciprocal(urec[:, t % 2, p, :], usum[:, t % 2, p, :]).then_inc(s["u_rec"], 1)

            for i in range(NT + 3):
                if i < NT:
                    slice_softmax(i)
                if i == 0:
                    product_parts(0)
                    product_parts(1)
                slice_attention_softmax(i - 2, 0)
                if i < NT:
                    slice_sum(i)
                if i == 0:
                    for n in range(2, 2 * H):
                        product_parts(n)
                slice_attention_softmax(i - 2, 1)
                slice_attention_sum(i - 2, 0)
                if i >= 3:
                    mask_pairs(s["p_ps"], pT, (slice(0, H, 2), slice(1, H, 2)), s["p_sb"], i - 3, s["o_ps"])
                slice_attention_softmax(i - 2, 2)
                slice_attention_sum(i - 2, 1)
                if i < 3:
                    mask_pairs(s["m_ps"], mm, (slice(0, HH), slice(HH, H)), s["m_sb"], i, s["z_ps"])
                if i < NT:
                    norms(i)
                slice_attention_sum(i - 2, 2)
                if 3 <= i < NT:
                    mask_pairs(s["m_ps"], mm, (slice(0, HH), slice(HH, H)), s["m_sb"], i, s["z_ps"])
            dve.wait_ge(s["ot_ps"], 1)
            residual(1, bank[5])
            layernorm(2)

            dve.wait_ge(s["late"], LATE)
            mask_attention(1, None)
            dve.wait_ge(s["ao_ps"], 2)
            residual(2, bank[5])
            layernorm(3)

            split_tokens(1, D)

            steps = [0]

            def step(ins):
                steps[0] += 1
                ins.then_inc(s["g_step"], 1)
                dve.wait_ge(s["g_step"], steps[0])

            gps = bank[3][0:R, 0:NT * E].rearrange("p (t e) -> p t e", t=NT)

            def over(a):
                return a[:, :].unsqueeze(2).to_broadcast([R, NT, E])

            ranks = rev[:, :].unsqueeze(1).to_broadcast([R, NT, E])
            dve.wait_ge(s["g_ps"], 1)
            step(nc.vector.tensor_reduce(gmax[:, :], gps, AX_X, ALU.max))
            nc.vector.tensor_tensor(gd[:, :, :], gps, over(gmax), ALU.subtract).then_inc(s["g_sub"], 1)
            dve.wait_ge(s["g_sub"], 1)
            step(nc.vector.scalar_tensor_tensor(out=gc[:, :, :], in0=gd[:, :, :], scalar=0.0, in1=ranks, op0=ALU.is_ge, op1=ALU.mult))
            step(nc.vector.tensor_reduce(gr[:, :], gc[:, :, :], AX_X, ALU.max))
            step(nc.vector.tensor_tensor(gs1[:, :, :], gc[:, :, :], over(gr), ALU.is_equal))
            step(nc.vector.scalar_tensor_tensor(out=gd2[:, :, :], in0=gs1[:, :, :], scalar=-1e30, in1=gd[:, :, :], op0=ALU.mult, op1=ALU.add))
            step(nc.vector.tensor_reduce(gr[:, :], gd2[:, :, :], AX_X, ALU.max))
            step(nc.vector.tensor_tensor(gs2[:, :, :], gd2[:, :, :], over(gr), ALU.is_equal))
            step(nc.vector.tensor_tensor(gc[:, :, :], gs2[:, :, :], ranks, ALU.mult))
            step(nc.vector.tensor_reduce(gr[:, :], gc[:, :, :], AX_X, ALU.max))
            step(nc.vector.tensor_tensor(gs2[:, :, :], gc[:, :, :], over(gr), ALU.is_equal))
            step(nc.vector.tensor_tensor(gs2[:, :, :], gs1[:, :, :], gs2[:, :, :], ALU.add))
            dve.wait_ge(s["g_exp"], 1)
            step(nc.vector.tensor_tensor(gw[:, :, :], gs2[:, :, :], ge[:, :, :], ALU.mult))
            step(nc.vector.tensor_reduce(gr[:, :], gw[:, :, :], AX_X, ALU.add))
            step(nc.vector.reciprocal(gr[:, :], gr[:, :]))
            nc.vector.tensor_tensor(gw[:, :, :], gw[:, :, :], over(gr), ALU.mult).then_inc(s["g_disp"], 1)
            dve.wait_ge(s["d_sb"], 2)
            nc.vector.tensor_tensor(dispT[LOW:LOW + E, 0:FIRST], bank[4][0:E, 0:FIRST], dispT[0:E, 0:FIRST].bitcast(F32), ALU.subtract).then_inc(s["d_lo"], 1)
            nc.vector.tensor_tensor(dispT[LOW:LOW + E, FIRST:TP], bank[5][0:E, 0:TP - FIRST], dispT[0:E, FIRST:TP].bitcast(F32), ALU.subtract).then_inc(s["d_lo"], 1)
            for n in range(2 * E):
                dve.wait_ge(s["e_silu"], n + 1)
                dve.wait_ge(s["e2_ps"], n + 1)
                nc.vector.tensor_tensor(hid[:, n % 2, :], silu[:, n % 2, :], bank[2 + n % 2][:, 0:HALF], ALU.mult).then_inc(s["e_hid"], 1)
                dve.wait_ge(s["e_hid"], n + 1)
                dve.wait_ge(s["db_ps"], n + 1)
                if n >= 2:
                    dve.wait_ge(s["e_out"], n - 1)
                nc.vector.tensor_tensor(hidw[:, n % 2, :], hid[:, n % 2, :], bank[4 + n % 2][:, 0:HALF], ALU.mult).then_inc(s["e_w"], 1)
            dve.wait_ge(s["e_fin"], 1)
            nc.vector.tensor_tensor(xn[:, :, :], h[:, :, :], bank[0][0:R, 0:NT * D].rearrange("p (t d) -> p t d", t=NT),
                                    ALU.add).then_inc(s["e_res"], 1)

        @block.tensor
        def _(pe):
            def mm_(o, l, r, start=True, stop=True):
                return nc.tensor.matmul(o, l, r, start=start, stop=stop)

            def tr(o, i, n):
                return nc.tensor.transpose(o, i, ident[0:n, 0:n])

            pe.wait_ge(s["ident"], 2)
            pe.wait_ge(s["tokw_in"], 16)
            for k in range(NCH):
                last = tr(bank[0][:, k * D:(k + 1) * D], tokw[:, k * 128:(k + 1) * 128], D)
            last.then_inc(s["tokwT_ps"], 1)
            heads = [(hd // 2, slice((hd % 2) * D, (hd % 2 + 1) * D)) for hd in range(H)]

            def once(w):
                return w.rearrange("p a d -> p (a d)")

            def fold_first():
                pe.wait_ge(s["fx_in"], 6 * 16)
                pe.wait_ge(s["const"], CONSTS)
                for b_, w in ((0, wfx_a), (1, wx_a)):
                    for k in range(HH):
                        last = mm_(bank[b_][:, k * D:(k + 1) * D], w[:, k * 128:(k + 1) * 128], fold[:, :])
                    last.then_inc(s["wT_ps"], 1)
                tr(bank[2][:, 0:D], wv2[:, :, :].rearrange("p a d -> p (a d)"), D).then_inc(s["wT_ps"], 1)

            def fold_second():
                pe.wait_ge(s["f0_in"], 10 * 16)
                for b_, w in ((6, wq2), (7, wk2)):
                    for k, half in heads:
                        last = mm_(bank[b_][half, k * D:(k + 1) * D], w[half, :], wfxT[half, k, 0, :])
                    last.then_inc(s["ab_ps"], 1)
                for k, half in heads:
                    last = mm_(bank[5][half, k * D:(k + 1) * D], wvT[half, :], wout[half, k, :])
                last.then_inc(s["wvo_ps"], 1)

            def fold_logits():
                pe.wait_ge(s["ab_sb"], 2)
                for i in range(2):
                    half = slice(i * D, (i + 1) * D)
                    mm_(bank[6 + i][:, 0:HH * S], pickb[i * D:i * D + 1, :],
                        bslice[i * D:i * D + 1, :].unsqueeze(1).to_broadcast([1, HH, S]), True, False)
                    for k in range(HH):
                        last = mm_(bank[6 + i][:, k * S:(k + 1) * S], once(wxT[half, k, :, :]), wslice[half, :], False, k == HH - 1)
                last.then_inc(s["ws_ps"], 1)

            def fold_grams():
                for hd, (k, half) in enumerate(heads):
                    last = mm_(bank[hd % 2][:, k * 2 * D:(k + 1) * 2 * D], once(kT[half, k, :, :]), once(qT[half, k, :, :]))
                last.then_inc(s["gram_ps"], 1)

            def fold_values():
                pe.wait_ge(s["wvo_sb"], 1)
                for hd, (k, half) in enumerate(heads):
                    last = mm_(bank[2 + hd % 2][:, k * D:(k + 1) * D], once(wfxT[half, k, :, :]), wvo[half, k, :])
                last.then_inc(s["vo_ps"], 1)

            def fold_layer1():
                pe.wait_ge(s["l1_in"], 6 * 16)
                mm_(bank[4][0:D, 0:D], l1q[:, :], l1k[:, :])
                tr(bank[4][0:D, D:2 * D], l1o[:, :], D).then_inc(s["l1_ps"], 1)
                pe.wait_ge(s["l1_sb"], 2)
                mm_(bank[5][0:D, 0:D], l1v[:, :], l1oT[:, :]).then_inc(s["l1b_ps"], 1)

            pe.wait_ge(s["tokwT_sb"], 1)
            def pixels(k):
                return s["pix_odd"] if k % 2 else s["pix_even"]

            for k in range(NCH + 1):
                if k < NCH:
                    pe.wait_ge(s["re_odd"] if k % 2 else s["re_even"], k // 2 + 1)
                    if k >= 2:
                        pe.wait_ge(pixels(k - 2), (k - 2) // 2 + 1)
                    for w in range(HP):
                        last = tr(bank[k % 2][:, w * 128:(w + 1) * 128], xre[:, k % 2, w * 128:(w + 1) * 128], 128)
                    last.then_inc(s["pix_ps"], 1)
                if k >= 1:
                    pe.wait_ge(pixels(k - 1), (k - 1) // 2 + 1)
                    mm_(bank[2][0:D, :], tokwT[:, k - 1, :], pixT[:, (k - 1) % 2, :], k == 1, k == NCH).then_inc(s["tok_ps"], 1)
            pe.wait_ge(s["tok_sb"], HP + 1)
            for t in range(NT):
                last = tr(bank[3][0:R, t * D:(t + 1) * D], hT0[:, t * R:(t + 1) * R], D)
            last.then_inc(s["htm_ps"], 1)

            def layernorm(k):
                pe.wait_ge(s["ln_xn"], k + 1)
                for t in range(NT):
                    b_, c0 = (6, t * R) if t < NT - 1 else (7, 0)
                    last = tr(bank[b_][0:D, c0:c0 + R], xn[:, t, :], R)
                last.then_inc(s["ln_ps"], 1)
                pe.wait_ge(s["ln_xT"], 2 * (k + 1))

            fold_first()
            layernorm(0)

            pe.wait_ge(s["a0_in"], 6 * 16)
            pe.wait_ge(s["wT_sb"], 3)
            for i in range(2):
                mm_(bank[i][0:D, 0:HALF], wk_a[:, :], xT[:, i * HALF:(i + 1) * HALF]).then_inc(s["k_ps"], 1)
            for t in range(NT):
                last = mm_(bank[4][0:R, t * D:(t + 1) * D], xT[:, t * R:(t + 1) * R], wv_a[:, :])
            last.then_inc(s["v_ps"], 1)
            for i in range(2):
                mm_(bank[2 + i][0:D, 0:HALF], wq_a[:, :], xT[:, i * HALF:(i + 1) * HALF]).then_inc(s["q_ps"], 1)
            fold_second()
            pe.wait_ge(s["k_sm"], 1)
            pe.wait_ge(s["wvo_sb"], 1)
            for t in range(NT):
                last = tr(bank[5][0:R, t * D:(t + 1) * D], smT[:, t * R:(t + 1) * R], D)
            last.then_inc(s["sm_ps"], 1)
            pe.wait_ge(s["sm_sb"], 1)
            pe.wait_ge(s["q_sb"], 2)
            for t in range(NT):
                if t % 2:
                    pe.wait_ge(s["vexp_d"], t // 2 + 1)
                else:
                    pe.wait_ge(s["vexp_p"], t // 2 + 1)
                if t >= 4:
                    pe.wait_ge(s["bn_st"], t - 3)
                mm_(bank[t % 4][0:D, 0:imgs[t] * D], sm[:, t, :],
                    vexp[:, t % 2, 0:imgs[t], :]).then_inc(s["lam_ps"], 1)
            fold_logits()
            pe.wait_ge(s["bn_st"], NT)
            pe.wait_ge(s["q_scaled"], 1)

            def attention(left, right, k):
                for t in range(NT):
                    b_, c0 = (0, t * R) if t < NT - 1 else (1, 0)
                    last = mm_(bank[b_][0:R, c0:c0 + R], left[0:D, t * R:(t + 1) * R], right[0:D, t * R:(t + 1) * R])
                last.then_inc(s["at_ps"], 1)
                pe.wait_ge(s["at_sb"], 2 * (k + 1))

            attention(smT, qsT, 0)
            for t in range(NT):
                mm_(bank[5][0:R, t * D:(t + 1) * D], att[:, t, :], v0[:, t, :], True, False)
                last = mm_(bank[5][0:R, t * D:(t + 1) * D], q0T[:, t * R:(t + 1) * R],
                           bnc[:, 0:1].to_broadcast([D, D]), False, True)
            last.then_inc(s["ao_ps"], 1)
            fold_grams()
            pe.wait_ge(s["ws_sb"], 2)
            layernorm(1)
            fold_values()
            pe.wait_ge(s["h_upd"], 2)
            fold_layer1()

            def flat(w):
                return w[:, :, :].rearrange("p h d -> p (h d)")

            def token_product_operands():
                for n in range(2 * H):
                    i, hd = divmod(n, H)
                    if n >= 4:
                        pe.wait_ge(s["t1_lo"], n - 3)
                    cols = slice(i * HALF, (i + 1) * HALF)
                    mm_(bank[3 + n % 4][:, 0:HALF], gramh[:, hd, :], xS[:, cols], True, False)
                    mm_(bank[3 + n % 4][:, 0:HALF], graml[:, hd, :], xS[:, cols], False, True).then_inc(s["t1_ps"], 1)
                pe.wait_ge(s["t1_lo"], 2 * H)

            pe.wait_ge(s["x_lo"], 2)
            pe.wait_ge(s["ws_lo"], 1)
            pe.wait_ge(s["vo_sb"], 2)
            pe.wait_ge(s["l1b_sb"], 1)

            def slots(t):
                return slice(t * R, t * R + rows[t])

            def slice_logits(t):
                if t >= 1:
                    pe.wait_ge(s["s_sub"], t)
                if t >= 4:
                    pe.wait_ge(s["vo_sb2"], t - 3)
                mm_(bank[0][0:rows[t], :], xS[:, slots(t)], flat(wsh), True, False)
                mm_(bank[0][0:rows[t], :], xS[:, slots(t)], flat(wsl), False, True).then_inc(s["s_ps"], 1)

            def weights_T(t):
                rt = rows[t]
                pe.wait_ge(s["s_w"], t + 1)
                if t >= 3:
                    pe.wait_ge(s["r_sb"], t - 2)
                elif t >= 1:
                    pe.wait_ge(s["et_sb"], 4 * t)
                for k in range(HH):
                    last = tr(bank[3][:, k * R:k * R + rt], sw[0:rt, t % 2, 2 * k:2 * k + 2, :].rearrange("p h g -> p (h g)"), rt)
                last.then_inc(s["et_ps"], 1)

            def token_products(t):
                rt = rows[t]
                if t >= 3:
                    pe.wait_ge(s["p_sb"], 2 * (t - 2))
                elif t >= 1:
                    pe.wait_ge(s["m_sb"], 2 * t)
                for i in range(2):
                    o = bank[1 + i][0:rt, 0:HH * R].rearrange("p (k r) -> p k r", k=HH)[:, :, 0:rt]
                    mm_(o, xS[:, slots(t)], t1h[:, i * HH:(i + 1) * HH, slots(t)], True, False)
                    last = mm_(o, xS[:, slots(t)], t1l[:, i * HH:(i + 1) * HH, slots(t)], False, True)
                last.then_inc(s["m_ps"], 1)

            def z(t):
                rt = rows[t]
                pe.wait_ge(s["s_n"], t + 1)
                pe.wait_ge(s["m_sb"], 2 * (t + 1))
                if t >= 1:
                    pe.wait_ge(s["z_sb"], sum(imgs[0:t]))
                for hd in range(H):
                    last = mm_(bank[7][0:rt, hd * S:(hd + 1) * S], mm[0:rt, t % 2, hd, 0:rt], sn[0:rt, t % 2, hd, :])
                last.then_inc(s["z_ps"], 1)

            def slices(t):
                rt = rows[t]
                pe.wait_ge(s["snT_sb"], t + 1)
                if t >= 3:
                    pe.wait_ge(s["o_sb"], t - 2)
                elif t >= 1:
                    pe.wait_ge(s["s_n"], t)
                for k in range(HH):
                    last = tr(bank[4][0:rt, k * 2 * S:(k + 1) * 2 * S], snT[:, t % 3, k, 0:rt], 128)
                last.then_inc(s["sn_ps"], 1)

            def logits(t, p):
                if 0 <= t < NT and p < pairs[t]:
                    rt = rows[t]
                    pe.wait_ge(s["z_sb"], sum(imgs[0:t]) + 2 * p + 2)
                    u = sum(pairs[0:t]) + p
                    if u >= 2:
                        pe.wait_ge(s["u_sub"], u - 1)
                    for hd in range(H):
                        for j in range(2):
                            last = mm_(bank[5 + u % 2][j * S:(j + 1) * S, hd * S:(hd + 1) * S],
                                       zx[0:rt, t % 2, 2 * p + j, hd * S:(hd + 1) * S], sn[0:rt, t % 2, hd, :])
                    last.then_inc(s["l_ps"], 1)

            def project_values(t):
                if t + 3 < NT:
                    pe.wait_ge(s["s_sub"], t + 4)
                else:
                    pe.wait_ge(s["s_sub"], NT)
                if t >= 1:
                    pe.wait_ge(s["vo_sb2"], t)
                mm_(bank[0][0:rows[t], :], xS[:, slots(t)], flat(voh), True, False)
                mm_(bank[0][0:rows[t], :], xS[:, slots(t)], flat(vol), False, True).then_inc(s["vo_ps2"], 1)

            def r(t):
                pe.wait_ge(s["u_w"], sum(pairs[0:t + 1]))
                pe.wait_ge(s["et_sb"], 4 * min(t + 3, NT))
                for p in range(pairs[t]):
                    for hd, (k, half) in enumerate(heads):
                        c0 = k * R + p * 2 * N
                        last = mm_(bank[3][half, c0:c0 + 2 * N], fe[:, t % 2, p, hd, :], etx[:, t % 3, hd, p * 2 * N:(p + 1) * 2 * N])
                last.then_inc(s["r_ps"], 1)

            def products_back(t):
                rt = rows[t]
                pe.wait_ge(s["r_sb"], t + 1)
                pe.wait_ge(s["m_sb"], 2 * min(t + 3, NT))
                for hd, (k, half) in enumerate(heads):
                    c0 = k * R
                    last = mm_(bank[1 + hd % 2][0:rt, c0:c0 + rt], snT[half, t % 3, k, 0:rt], rT[half, t % 2, k, 0:rt])
                last.then_inc(s["p_ps"], 1)

            def output(t):
                rt = rows[t]
                pe.wait_ge(s["p_sb"], 2 * (t + 1))
                pe.wait_ge(s["vo_sb2"], t + 1)
                pe.wait_ge(s["s_n"], min(t + 3, NT))
                for hd in range(H):
                    last = mm_(bank[4][0:D, 0:rt], vox[0:rt, t % 2, hd, :], pT[0:rt, t % 2, hd, 0:rt], hd == 0, hd == H - 1)
                last.then_inc(s["o_ps"], 1)

            for i in range(NT + 3):
                if i < NT:
                    slice_logits(i)
                if i == 0:
                    token_product_operands()
                logits(i - 2, 0)
                if 0 <= i - 1 < NT:
                    slices(i - 1)
                if 0 <= i - 1 < NT:
                    z(i - 1)
                if i >= 3:
                    r(i - 3)
                logits(i - 2, 1)
                if i >= 3:
                    products_back(i - 3)
                    project_values(i - 3)
                logits(i - 2, 2)
                if i < 3:
                    token_products(i)
                if i < NT:
                    weights_T(i)
                if i >= 3:
                    output(i - 3)
                if 3 <= i < NT:
                    token_products(i)
            pe.wait_ge(s["o_sb"], NT)
            for t in range(NT):
                last = tr(bank[5][0:R, t * D:(t + 1) * D], hT0[:, t * R:(t + 1) * R], D)
            last.then_inc(s["ot_ps"], 1)
            layernorm(2)

            for i in range(2):
                mm_(bank[i][0:D, 0:HALF], g1[:, :], xT[0:D, i * HALF:(i + 1) * HALF]).then_inc(s["t_ps"], 1)
            for t in range(NT):
                last = mm_(bank[4][0:R, t * D:(t + 1) * D], xT[0:D, t * R:(t + 1) * R], vo1[:, :])
            last.then_inc(s["v_ps"], 1)
            pe.wait_ge(s["t_sb"], 2)
            attention(xT, qsT, 1)
            pe.wait_ge(s["v_sb"], 2)
            for t in range(NT):
                last = mm_(bank[5][0:R, t * D:(t + 1) * D], att[:, t, :], vt1[:, t, :])
            last.then_inc(s["ao_ps"], 1)
            layernorm(3)

            for t in range(NT):
                last = mm_(bank[3][0:R, t * E:(t + 1) * E], xT[:, t * R:(t + 1) * R], gate_a[:, :])
            last.then_inc(s["g_ps"], 1)
            pe.wait_ge(s["moe_in"], 16)
            pe.wait_ge(s["g_disp"], 1)
            for t in range(NT):
                b_, c0 = (4, t * R) if t < NT - 1 else (5, 0)
                last = tr(bank[b_][0:E, c0:c0 + R], gw[:, t, :], R)
            last.then_inc(s["d_ps"], 1)
            pe.wait_ge(s["pick"], 1)
            pe.wait_ge(s["w_lo"], 2)
            pe.wait_ge(s["x_lo"], 4)

            def down(n):
                e, i = divmod(n, 2)
                pe.wait_ge(s["e_w"], n + 1)
                mm_(bank[6 + i][0:D, 0:HALF], w3[:, e, :], hidw[:, n % 2, :], e == 0, e == E - 1).then_inc(s["e_out"], 1)

            for n in range(2 * E):
                e, i = divmod(n, 2)
                cols = slice(i * HALF, (i + 1) * HALF)
                if n >= 2:
                    pe.wait_ge(s["e_silu"], n - 1)
                    pe.wait_ge(s["e_hid"], n - 1)
                mm_(bank[n % 2][:, 0:HALF], w1h[:, e, :], xS[:, cols], True, False)
                mm_(bank[n % 2][:, 0:HALF], w1l[:, e, :], xS[:, cols], False, True).then_inc(s["e1_ps"], 1)
                mm_(bank[2 + n % 2][:, 0:HALF], w2h[:, e, :], xS[:, cols], True, False)
                mm_(bank[2 + n % 2][:, 0:HALF], w2l[:, e, :], xS[:, cols], False, True).then_inc(s["e2_ps"], 1)
                if n == 0:
                    pe.wait_ge(s["d_lo"], 2)
                if n >= 2:
                    pe.wait_ge(s["e_w"], n - 1)
                mm_(bank[4 + n % 2][:, 0:HALF], pick[:, e:e + 1].to_broadcast([LOW + E, HID]), dispT[:, cols]).then_inc(s["db_ps"], 1)
                if n >= 1:
                    down(n - 1)
            down(2 * E - 1)
            pe.wait_ge(s["e_outT"], 2)
            for t in range(NT):
                last = tr(bank[0][0:R, t * D:(t + 1) * D], hT0[:, t * R:(t + 1) * R], D)
            last.then_inc(s["e_fin"], 1)


_INS = ['x', 'cls_tok', 'L0_tok_W', 'L0_tok_b', 'L0_attn_W_qk', 'L0_attn_b_qk', 'L0_attn_W_v', 'L0_attn_b_v',
        'L0_attn_gamma', 'L0_attn_beta', 'L0_ffn_W_fx', 'L0_ffn_b_fx', 'L0_ffn_W_x', 'L0_ffn_b_x', 'L0_ffn_W_slice',
        'L0_ffn_b_slice', 'L0_ffn_W_q', 'L0_ffn_W_k', 'L0_ffn_W_v', 'L0_ffn_W_out', 'L0_ffn_b_out',
        'L0_ffn_temperature', 'L1_attn_Wq', 'L1_attn_Wk', 'L1_attn_Wv', 'L1_attn_Wo', 'L1_ffn_gate_w',
        'L1_ffn_gate_b', 'L1_ffn_w1', 'L1_ffn_w2', 'L1_ffn_w3']
_OUTS = [((32, 17, 64), 'float32')]


def kernel(**inputs):
    import numpy as _np
    import concourse.bacc as _bacc
    from concourse import mybir as _mybir
    from concourse.bass_utils import run_bass_kernel_spmd as _run

    nc = _bacc.Bacc("TRN2", target_bir_lowering=False, num_devices=1)
    arrays, args = {}, []
    for name in _INS:
        a = _np.ascontiguousarray(inputs[name])
        arrays[f"in_{name}_dram"] = a
        args.append(nc.dram_tensor(f"in_{name}_dram", a.shape, _mybir.dt.from_np(a.dtype), kind="ExternalInput").ap())
    for i, (shape, dtype) in enumerate(_OUTS):
        dt = _mybir.dt.from_np(_np.dtype(dtype))
        args.append(nc.dram_tensor(f"out_{i}_dram", shape, dt, kind="ExternalOutput").ap())
    vit_tower_kernel(nc, *args)
    r = _run(nc, [arrays], core_ids=[0])
    got = tuple(r.results[0][f"out_{i}_dram"] for i in range(len(_OUTS)))
    return got[0]
```

```python
from contextlib import ExitStack

import concourse.bass as bass
from concourse import mybir

F32 = mybir.dt.float32
F32R = mybir.dt.float32r
ALU = mybir.AluOpType
ACT = mybir.ActivationFunctionType
AX_X = mybir.AxisListType.X

EPS = 1e-5


def vit_tower_kernel(nc, x, cls_tok, tok_W, tok_b, a0_W_qk, a0_b_qk, a0_W_v, a0_b_v, a0_gamma, a0_beta,
                     f0_W_fx, f0_b_fx, f0_W_x, f0_b_x, f0_W_slice, f0_b_slice, f0_W_q, f0_W_k, f0_W_v,
                     f0_W_out, f0_b_out, f0_temperature, a1_Wq, a1_Wk, a1_Wv, a1_Wo,
                     f1_gate_w, f1_gate_b, f1_w1, f1_w2, f1_w3, out):
    B, C, IMG, _ = x.shape
    D = cls_tok.shape[2]
    PATCH = 16
    HP = IMG // PATCH
    N = HP * HP + 1
    G = 6
    R = G * N
    NT = -(-B // G)
    TP = NT * R
    T = B * N
    H = f0_temperature.shape[1]
    HH = H // 2
    S = f0_W_slice.shape[1]
    E, _, HID = f1_w1.shape
    A = D + 1
    HALF = T // 2
    XC = HALF // N
    FIRST = (512 // R) * R
    IH = 8
    NCH = C * PATCH // IH
    assert D == 64 and S == 64 and B * HP == 128 and R <= 128 and HID == 128 and C == 3
    LOW = 32
    NORM_FILL, SLICES_FILL, SOFTMAX_FILL = (6, 10, 6, 6), (6, 6, 6, 0), (8, 0, 0, 0, 8, 4)
    NG = NT // 2
    rows = [min(G, B - t * G) * N for t in range(NT)]
    imgs = [min(G, B - t * G) for t in range(NT)]
    pairs = [n // 2 for n in imgs]

    with ExitStack() as ctx:
        def sb(name, shape, dt=F32):
            return ctx.enter_context(nc.sbuf_tensor(name, shape, dt))

        def sem(name):
            return ctx.enter_context(nc.semaphore(name))

        bank = [ctx.enter_context(nc.psum_tensor(f"bank{i}", [128, 512], F32)) for i in range(8)]

        region = sb("region", [128, 2 * G * H * S])
        XIN, PIX = C * PATCH * IMG, 2 * 512
        CH = HP * 128
        xin = region[:, 0:XIN].rearrange("p (c n) -> p c n", c=C)
        pixT = region[:, XIN:XIN + PIX].rearrange("p (k n) -> p k n", k=2)
        tokw = region[0:D, XIN + PIX:XIN + PIX + C * PATCH * PATCH]
        AHEAD = 3
        RING = 5
        silu, hid, hidw = (region[0:HID, i * RING * HALF:(i + 1) * RING * HALF].rearrange("p (a n) -> p a n", a=RING) for i in range(3))
        zx = region[0:R, :].rearrange("p (a i n) -> p a i n", a=2, i=G)
        tokb = sb("tokb", [D, 1])
        cls = sb("cls", [D, 1])
        wk_a = sb("wk_a", [A, D])
        wq_a = sb("wq_a", [A, D])
        wv_a = sb("wv_a", [A, D])
        gamma = sb("gamma", [D, 1])
        beta = sb("beta", [D, 1])
        wfx_a = sb("wfx_a", [A, H * D])
        wx_a = sb("wx_a", [A, H * D])
        wslice = sb("wslice", [128, S])
        bslice = sb("bslice", [D + 1, S])
        wq2 = sb("wq2", [128, D])
        wk2 = sb("wk2", [128, D])
        wv2 = sb("wv2", [D, 2, D])
        wout = sb("wout", [128, HH, D])
        bout = sb("bout", [D, 1])
        temp = sb("temp", [128, H])
        l1q = sb("l1q", [D, D])
        l1k = sb("l1k", [D, D])
        l1v = sb("l1v", [D, D])
        l1o = sb("l1o", [D, D])
        gate_a = sb("gate_a", [A, E])
        w3 = sb("w3", [HID, E, D])

        ident = sb("ident", [128, 128])
        EPSC = sb("eps_col", [128, 1])
        imgmask = sb("imgmask", [R, G])
        same = sb("same", [R, R])
        causal = sb("causal", [R, R])
        fold = sb("fold", [A, D])
        pickb = sb("pickb", [A, 2 * D])
        ONE = sb("one_col", [128, 1])
        rev = sb("rev", [R, E])
        pick = sb("pick", [LOW + E, E], F32R)

        tokwT = sb("tokwT", [128, NCH, D])
        wfxT = sb("wfxT", [128, HH, 2, D])
        wxT = sb("wxT", [128, HH, 2, D])
        wvT = sb("wvT", [128, D])
        rtemp = sb("rtemp", [128, H])
        ws = sb("ws", [128, H, S])
        wsh, wsl = (sb(n, [128, H, S], F32R) for n in ("wsh", "wsl"))
        qT = sb("qT", [128, HH, 2, D])
        kT = sb("kT", [128, HH, 2, D])
        gramh, graml = (sb(n, [128, H, 2 * D], F32R) for n in ("gramh", "graml"))
        wvo = sb("wvo", [128, HH, D])
        voh, vol = (sb(n, [128, H, D], F32R) for n in ("voh", "vol"))
        g1 = sb("g1", [D, D])
        l1oT = sb("l1oT", [D, D])
        vo1 = sb("vo1", [D, D])

        hT0 = sb("hT0", [D, TP])
        h = sb("h", [R, NT, D])
        xc = sb("xc", [R, NT, D])
        lstats = sb("lstats", [R, NT, 6])
        lmv = sb("lmv", [R, NT, 2])
        std = sb("std", [R, NT])
        spare = sb("spare", [1, 16])
        rstd = sb("rstd", [R, NT])
        xn = sb("xn", [R, NT, D])
        xT = sb("xT", [A, TP])
        xS = sb("xS", [2 * D, TP], F32R)

        kmax = sb("kmax", [D, B])
        ksum = sb("ksum", [D, B])
        krec = sb("krec", [D, B])
        smT = sb("smT", [D, TP])
        q0T = sb("q0T", [D, TP])
        qsT = sb("qsT", [D, TP])
        v0 = sb("v0", [R, NT, D])
        stats = sb("stats", [D, NT, 6])
        mv = sb("mv", [D, 2])
        bnl = sb("bnl", [D, 1])
        bnr = sb("bnr", [D, 1])
        bna = sb("bna", [D, 1])
        bnm = sb("bnm", [D, 1])
        bnc = sb("bnc", [D, 1])
        att = sb("att", [R, NT, R])
        vt1 = sb("vt1", [R, NT, D])

        smax = sb("smax", [R, NT, H])
        ssum = sb("ssum", [R, NT, H])
        srec = sb("srec", [R, NT, H])
        sexp = sb("sexp", [R, 2, H, S])
        sw = sb("sw", [R, 2, H, S])
        nsum = sb("nsum", [128, 2, HH, G])
        nrec = sb("nrec", [128, 2, HH, G])
        snT = sb("snT", [128, 3, HH, R])
        sn = sb("sn", [R, 2, H, S])
        mm = sb("mm", [R, 2, H, R])
        lg = sb("lg", [128, 2, H, S])
        umax = sb("umax", [128, NT, G // 2, H])
        usum = sb("usum", [128, 2, G // 2, H])
        urec = sb("urec", [128, 2, G // 2, H])
        etx = sb("etx", [128, 3, H, R])
        rT = sb("rT", [128, 2, HH, R])
        pT = sb("pT", [R, 2, H, R])
        vox = sb("vox", [R, 2, H, D])

        gmax = sb("gmax", [R, NT])
        gd = sb("gd", [R, NT, E])
        ge = sb("ge", [R, NT, E])
        gc = sb("gc", [R, NT, E])
        gr = sb("gr", [R, NT])
        gs1 = sb("gs1", [R, NT, E])
        gd2 = sb("gd2", [R, NT, E])
        gs2 = sb("gs2", [R, NT, E])
        gw = sb("gw", [R, NT, E])
        dispT = sb("dispT", [LOW + E, TP], F32R)

        with ExitStack() as early:
            xre = early.enter_context(nc.sbuf_tensor("xre", [128, 2, CH], F32))
            kexp = early.enter_context(nc.sbuf_tensor("kexp", [D, T], F32))
            sm = early.enter_context(nc.sbuf_tensor("sm", [R, NT, D], F32))
            vexp = early.enter_context(nc.sbuf_tensor("vexp", [R, 2, G, D], F32))
        fe = sb("fe", [128, 2, G // 2, H, S])
        with ExitStack() as early:
            t1h, t1l = (early.enter_context(nc.sbuf_tensor(n, [2 * D, H, T], F32R)) for n in ("t1h", "t1l"))
        with ExitStack() as early:
            w1, w2 = (early.enter_context(nc.sbuf_tensor(n, [2 * D, E, HID], F32)) for n in ("w1", "w2"))
        w1l, w2l, w1h, w2h = (sb(n, [2 * D, E, HID], F32R) for n in ("w1l", "w2l", "w1h", "w2h"))

        names = """x_in0 x_in1 x_in2 tokw_in a0_in f0_in l1_in moe_in w12_in small_in norm_in fx_in ab_in ident const late
            tokwT_ps tokwT_sb re_even re_odd pix_ps pix_even pix_odd tok_ps tok_sb htm_ps h_upd
            wT_ps wT_sb ab_ps ab_sb pick gram_ps gram_hi gram_sb ws_ps ws_sb ws_hi ws_lo rt wvo_ps wvo_sb vo_ps vo_hi vo_sb l1_ps l1_sb l1b_ps l1b_sb
            ln_st ln_mv ln_cen ln_std ln_rstd ln_xn ln_ps ln_xT
            k_ps q_ps v_ps k_max k_sub k_exp k_sum k_rec k_sm q_sb v_sb sm_ps sm_sb vexp_d vexp_p lam_ps bn_st bn_mv bn_std
            bn_rstd bn_a bn_m bn_c q_scaled at_ps at_sb ao_ps
            t1_ps t1_hi t1_lo s_ps s_max s_sub s_exp s_sum s_rec s_w n_sum n_eps n_rec s_n m_ps m_sb z_ps z_sb sn_ps snT_sb
            l_ps u_max u_sub u_exp u_sum u_rec u_w et_ps et_sb r_ps r_sb p_ps p_sb vo_ps2 vo_sb2 o_ps o_sb ot_ps
            t_ps t_sb
            w_hi w_lo x_pad x_hi x_hi_last x_lo g_ps g_max g_sub g_exp g_step g_disp d_zero d_ps d_sb d_lo e1_ps e2_ps db_ps e_silu e_hid e_w e_out e_outT e_fin
            e_res stored""".split()
        s = {n: sem(n) for n in names}

        CONSTS = 20
        LATE = 3 + N + E

        block = ctx.enter_context(nc.Block())

        def row(v):
            return v.rearrange("(a n) -> a n", a=1)

        def col(v):
            return v.rearrange("(n a) -> n a", a=1)

        @block.sync
        def _(sp):
            xv = x.rearrange("b c (hp i) w -> c b hp (i w)", hp=HP)
            sp.dma_start(tokw[:, :], tok_W).then_inc(s["tokw_in"], 16)
            for c in range(C):
                for b0 in range(0, B, B // 4):
                    sp.dma_start(xin[b0 * HP:(b0 + B // 4) * HP, c, :], xv[c, b0:b0 + B // 4]).then_inc(s[f"x_in{c}"], 16)
            for group, loads in (
                    ("small_in", ((tokb[:, :], col(tok_b)), (cls[:, :], col(cls_tok.rearrange("a b d -> (a b d)"))))),
                    ("fx_in", ((wfx_a[0:D, :], f0_W_fx), (wfx_a[D:A, :], row(f0_b_fx)),
                               (wx_a[0:D, :], f0_W_x), (wx_a[D:A, :], row(f0_b_x)),
                               (wv2[:, 0, :], f0_W_v), (wv2[:, 1, :], f0_W_v))),
                    ("ab_in", ((wq2[0:D, :], f0_W_q), (wq2[D:128, :], f0_W_q), (wk2[0:D, :], f0_W_k), (wk2[D:128, :], f0_W_k),
                               (wout[:, :, :], f0_W_out.rearrange("(a p) d -> p a d", p=128)))),
                    ("a0_in", ((wk_a[0:D, :], a0_W_qk[1]), (wk_a[D:A, :], a0_b_qk[1:2, :]),
                               (wq_a[0:D, :], a0_W_qk[0]), (wq_a[D:A, :], a0_b_qk[0:1, :]),
                               (wv_a[0:D, :], a0_W_v), (wv_a[D:A, :], row(a0_b_v)))),
                    ("norm_in", ((gamma[:, :], col(a0_gamma)), (beta[:, :], col(a0_beta)), (bout[:, :], col(f0_b_out)))),
                    ("f0_in", ((wslice[0:D, :], f0_W_slice), (wslice[D:128, :], f0_W_slice),
                               (bslice[0:1, :], row(f0_b_slice)), (bslice[D:D + 1, :], row(f0_b_slice)),
                               (temp[:, :], f0_temperature.rearrange("a h b c -> a (h b c)").to_broadcast([128, H])))),
                    ("l1_in", ((l1q[:, :], a1_Wq), (l1k[:, :], a1_Wk), (l1v[:, :], a1_Wv), (l1o[:, :], a1_Wo),
                               (gate_a[0:D, :], f1_gate_w), (gate_a[D:A, :], row(f1_gate_b)))),
                    ("moe_in", ((w3[:, :, :], f1_w3.rearrange("e f d -> f e d")),))):
                for dst, src in loads:
                    sp.dma_start(dst, src).then_inc(s[group], 16)
            sp.wait_ge(s["m_ps"], 2 * NT)
            for half in (slice(0, D), slice(D, 2 * D)):
                sp.dma_start(w1[half, :, :], f1_w1.rearrange("e d f -> d e f")).then_inc(s["w12_in"], 16)
                sp.dma_start(w2[half, :, :], f1_w2.rearrange("e d f -> d e f")).then_inc(s["w12_in"], 16)
            sp.wait_ge(s["e_res"], 1)
            ov = out.rearrange("b n d -> (b n) d")
            full = NT - 1
            sp.dma_start(ov[0:full * R, :].rearrange("(t p) d -> p t d", p=R), xn[:, 0:full, :]).then_inc(s["stored"], 16)
            sp.dma_start(ov[full * R:T, :], xn[0:rows[full], full, :]).then_inc(s["stored"], 16)
            sp.wait_ge(s["stored"], 32)

        def reorder(k, engine, copy, done):
            c, ih = divmod(k, PATCH // IH)
            engine.wait_ge(s[f"x_in{c}"], 4 * 16)
            if k >= 2:
                engine.wait_ge(s["pix_ps"], k - 1)
            v = xin[:, c, :].rearrange("p (i w j) -> p w i j", i=PATCH, w=HP)
            copy(xre[:, k % 2, :].rearrange("p (w i j) -> p w i j", w=HP, i=IH),
                 v[:, :, ih * IH:(ih + 1) * IH, :]).then_inc(done, 1)

        @block.scalar
        def _(act):
            def evac(dst, src):
                return nc.scalar.activation(dst, src, ACT.Copy)

            act.wait_ge(s["tokwT_ps"], 1)
            evac(tokwT[:, :, :], bank[0][:, 0:NCH * D].rearrange("p (k d) -> p k d", k=NCH)).then_inc(s["tokwT_sb"], 1)
            for k in range(0, NCH, 2):
                reorder(k, act, evac, s["re_even"])
                act.wait_ge(s["pix_ps"], k + 1)
                if k >= 2:
                    act.wait_ge(s["tok_ps"], k - 1)
                evac(pixT[:, 0, :], bank[0][:, :]).then_inc(s["pix_even"], 1)
            act.wait_ge(s["small_in"], 2 * 16)
            act.wait_ge(s["tok_ps"], NCH)
            for j in range(HP):
                nc.scalar.activation(
                    hT0[:, 0:T].rearrange("p (b n) -> p b n", n=N)[:, :, 1 + j::HP],
                    bank[2][0:D, j * B * HP:(j + 1) * B * HP].rearrange("p (b a) -> p b a", a=HP),
                    ACT.Identity, bias=tokb[:, 0:1]).then_inc(s["tok_sb"], 1)

            loads = [0]

            def tables(function):
                nc.scalar.activation(spare[:, loads[0]:loads[0] + 1], EPSC[0:1, 0:1], function)
                loads[0] += 1

            def layernorm(k, while_waiting=lambda: None):
                tables(ACT.Sqrt)
                act.wait_ge(s["ln_mv"], (k + 1) * NT)
                nc.scalar.activation(std[:, :].unsqueeze(2), lmv[:, :, 1:2], ACT.Sqrt, bias=EPSC[0:R, 0:1]).then_inc(s["ln_std"], 1)
                tables(ACT.Exp)
                while_waiting()
                act.wait_ge(s["ln_ps"], k + 1)
                evac(xT[0:D, 0:FIRST], bank[6][0:D, 0:FIRST]).then_inc(s["ln_xT"], 1)

            def twice(ps):
                return ps[:, 0:HH * D].rearrange("p (k d) -> p k d", k=HH).unsqueeze(2).to_broadcast([128, HH, 2, D])

            def folded_first():
                act.wait_ge(s["wT_ps"], 1)
                evac(wfxT[:, :, :, :], twice(bank[4])).then_inc(s["wT_sb"], 1)
                act.wait_ge(s["wT_ps"], 2)
                evac(wxT[:, :, :, :], twice(bank[5])).then_inc(s["wT_sb"], 1)
                act.wait_ge(s["wT_ps"], 3)
                evac(wvT[:, :], bank[0][:, 0:D]).then_inc(s["wT_sb"], 1)

            def folded_second():
                act.wait_ge(s["ab_ps"], 1)
                nc.scalar.activation(qT[:, :, :, :], twice(bank[4]), ACT.Copy, scale=float(D) ** -0.5).then_inc(s["ab_sb"], 1)
                act.wait_ge(s["ab_ps"], 2)
                evac(kT[:, :, :, :], twice(bank[5])).then_inc(s["ab_sb"], 1)
                act.wait_ge(s["wvo_ps"], 1)
                evac(wvo[:, :, :], bank[3][:, 0:HH * D].rearrange("p (k d) -> p k d", k=HH)).then_inc(s["wvo_sb"], 1)

            def folded_third():
                act.wait_ge(s["gram_ps"], 1)
                for i in range(2):
                    evac(gramh[:, i::2, :], bank[i][:, :].rearrange("p (k d) -> p k d", k=HH)).then_inc(s["gram_hi"], 1)

            def folded_fourth():
                act.wait_ge(s["vo_ps"], 1)
                for i in range(2):
                    evac(voh[:, i::2, :], bank[5 + i][:, 0:HH * D].rearrange("p (k d) -> p k d", k=HH)).then_inc(s["vo_hi"], 1)

            folded_first()
            layernorm(0)
            folded_second()

            act.wait_ge(s["k_sub"], 2)
            nc.scalar.activation(kexp[:, :], kexp[:, :], ACT.Exp).then_inc(s["k_exp"], 1)
            act.wait_ge(s["v_ps"], 1)
            evac(v0[:, :, :], bank[4][0:R, 0:NT * D].rearrange("p (t d) -> p t d", t=NT)).then_inc(s["v_sb"], 1)
            for i in range(2):
                act.wait_ge(s["q_ps"], i + 1)
                evac(q0T[:, i * HALF:(i + 1) * HALF], bank[2 + i][0:D, 0:HALF]).then_inc(s["q_sb"], 1)
            act.wait_ge(s["sm_ps"], 1)
            evac(sm[:, :, :], bank[5][0:R, 0:NT * D].rearrange("p (t d) -> p t d", t=NT)).then_inc(s["sm_sb"], 1)
            tables(ACT.Sqrt)
            act.wait_ge(s["bn_mv"], 1)
            nc.scalar.activation(bnl[:, :], mv[:, 1:2], ACT.Sqrt, bias=EPSC[0:D, 0:1]).then_inc(s["bn_std"], 1)

            layernorm(1, folded_third)

            act.wait_ge(s["x_pad"], 2)
            evac(xS[0:D - 1, 0:FIRST], bank[6][0:D - 1, 0:FIRST]).then_inc(s["x_hi"], 1)

            def product_parts(n):
                i, hd = divmod(n, H)
                act.wait_ge(s["t1_ps"], n + 1)
                evac(t1h[:, hd, i * HALF:(i + 1) * HALF], bank[3 + n % 4][:, 0:HALF]).then_inc(s["t1_hi"], 1)

            def folded_layer1():
                act.wait_ge(s["l1_ps"], 1)
                evac(g1[:, :], bank[5][0:D, 0:D]).then_inc(s["l1_sb"], 1)
                evac(l1oT[:, :], bank[5][0:D, D:2 * D]).then_inc(s["l1_sb"], 1)

            def slice_exp(t):
                act.wait_ge(s["s_sub"], t + 1)
                if t >= 2:
                    act.wait_ge(s["s_w"], t - 1)
                nc.scalar.activation(sexp[0:rows[t], t % 2], sexp[0:rows[t], t % 2], ACT.Exp).then_inc(s["s_exp"], 1)

            def blocks(t):
                act.wait_ge(s["snT_sb"], t + 1)
                if t >= 3:
                    act.wait_ge(s["r_ps"], t - 2)
                np_ = pairs[t]
                for i in range(2):
                    for j in range(2):
                        src, dst = (slice(a * S, (a + 1) * S) for a in (i, j))

                        def view(a):
                            return a.rearrange("p k (q i n) -> p k q i n", q=G // 2, i=2)[:, :, 0:np_, j, :]

                        evac(view(etx[dst, t % 3, i::2, :]),
                             view(bank[3][src, 0:HH * R].rearrange("p (k r) -> p k r", k=HH))).then_inc(s["et_sb"], 1)

            def spread_z(t, p):
                if not (0 <= t < NT and p < pairs[t]):
                    return
                act.wait_ge(s["z_ps"], t + 1)
                if t >= 2:
                    act.wait_ge(s["l_ps"], sum(pairs[0:t - 1]))
                for i in (2 * p, 2 * p + 1):
                    nc.scalar.activation(zx[0:rows[t], t % 2, i, :], bank[7][0:rows[t], :], ACT.Copy,
                                         scale=imgmask[0:rows[t], i:i + 1]).then_inc(s["z_sb"], 1)

            def slices(t):
                act.wait_ge(s["sn_ps"], t + 1)
                if t >= 2:
                    act.wait_ge(s["l_ps"], sum(pairs[0:t - 1]))
                evac(sn[0:rows[t], t % 2], bank[4][0:rows[t], :].rearrange("p (h g) -> p h g", h=H)).then_inc(s["s_n"], 1)

            def values(t):
                act.wait_ge(s["vo_ps2"], t + 1)
                if t >= 2:
                    act.wait_ge(s["o_ps"], t - 1)
                evac(vox[0:rows[t], t % 2], bank[0][0:rows[t], :].rearrange("p (h d) -> p h d", h=H)).then_inc(s["vo_sb2"], 1)

            def slice_attention_exp(t, p):
                if 0 <= t < NT and p < pairs[t]:
                    u = sum(pairs[0:t]) + p
                    act.wait_ge(s["u_sub"], u + 1)
                    if t >= 2:
                        act.wait_ge(s["r_ps"], t - 1)
                    nc.scalar.activation(fe[:, t % 2, p], lg[:, u % 2], ACT.Exp).then_inc(s["u_exp"], 1)

            def r_out(t):
                act.wait_ge(s["r_ps"], t + 1)
                if t >= 2:
                    act.wait_ge(s["p_ps"], 2 * (t - 1))
                evac(rT[:, t % 2, :, 0:rows[t]],
                     bank[3][:, 0:HH * R].rearrange("p (k r) -> p k r", k=HH)[:, :, 0:rows[t]]).then_inc(s["r_sb"], 1)

            def o_out(t):
                act.wait_ge(s["o_ps"], t + 1)
                nc.scalar.activation(hT0[:, t * R:t * R + rows[t]], bank[4][0:D, 0:rows[t]], ACT.Identity,
                                     bias=bout[:, 0:1]).then_inc(s["o_sb"], 1)

            for i in range(NT + 3):
                if 0 <= i - 1 < NT:
                    slices(i - 1)
                if i == 0:
                    product_parts(0)
                    product_parts(1)
                if i < NT:
                    slice_exp(i)
                if i == 0:
                    for n in range(2, 2 * H):
                        product_parts(n)
                slice_attention_exp(i - 2, 0)
                if i < 3:
                    spread_z(i - 1, 0)
                else:
                    r_out(i - 3)
                slice_attention_exp(i - 2, 1)
                if i >= 3:
                    spread_z(i - 1, 0)
                spread_z(i - 1, 1)
                if i == 1:
                    folded_fourth()
                if i == NT + 2:
                    folded_layer1()
                if i >= 3:
                    values(i - 3)
                slice_attention_exp(i - 2, 2)
                spread_z(i - 1, 2)
                if i < NT:
                    blocks(i)
                if i >= 3:
                    o_out(i - 3)

            layernorm(2)

            act.wait_ge(s["l1b_ps"], 1)
            evac(vo1[:, :], bank[5][0:D, 0:D]).then_inc(s["l1b_sb"], 1)
            for i in range(2):
                act.wait_ge(s["t_ps"], i + 1)
                evac(qsT[:, i * HALF:(i + 1) * HALF], bank[i][0:D, 0:HALF]).then_inc(s["t_sb"], 1)
            act.wait_ge(s["v_ps"], 2)
            evac(vt1[:, :, :], bank[4][0:R, 0:NT * D].rearrange("p (t d) -> p t d", t=NT)).then_inc(s["v_sb"], 1)

            layernorm(3)

            evac(xS[0:D, 0:FIRST], bank[6][0:D, 0:FIRST]).then_inc(s["x_hi"], 1)
            act.wait_ge(s["g_sub"], 1)
            nc.scalar.activation(ge[:, :, :], gd[:, :, :], ACT.Exp).then_inc(s["g_exp"], 1)
            tables(ACT.Silu)

            def silu_step(n):
                act.wait_ge(s["e1_ps"], n + 1)
                if n >= RING:
                    act.wait_ge(s["e_hid"], n - RING + 1)
                nc.scalar.activation(silu[:, n % RING, :], bank[n % 2][:, 0:HALF], ACT.Silu).then_inc(s["e_silu"], 1)

            for n in range(AHEAD):
                silu_step(n)
            act.wait_ge(s["d_zero"], 1)
            act.wait_ge(s["d_ps"], 1)
            evac(dispT[0:E, 0:FIRST], bank[4][0:E, 0:FIRST]).then_inc(s["d_sb"], 1)
            evac(dispT[0:E, FIRST:TP], bank[5][0:E, 0:TP - FIRST]).then_inc(s["d_sb"], 1)
            for n in range(AHEAD, 2 * E):
                silu_step(n)
            act.wait_ge(s["e_out"], 2 * E)
            for i in range(2):
                evac(hT0[:, i * HALF:(i + 1) * HALF], bank[6 + i][0:D, 0:HALF]).then_inc(s["e_outT"], 1)

        @block.gpsimd
        def _(pool):
            made = {"ident": 0, "const": 0, "late": 0}

            def link(ins, what):
                made[what] += 1
                ins.then_inc(s[what], 1)
                pool.wait_ge(s[what], made[what])

            def fill(t, value, what="const"):
                link(nc.gpsimd.memset(t, value), what)

            def select(t, pattern, base, mult, op, value, what="const"):
                link(nc.gpsimd.affine_select(out=t, in_=t, pattern=pattern, base=base, channel_multiplier=mult,
                                             compare_op=op, fill=value), what)

            fill(ident[:, :], 0.0, "ident")
            select(ident[:, :], [[-1, 128]], 0, 1, ALU.not_equal, 1.0, "ident")
            fill(fold[:, :], 0.0)
            select(fold[:, :], [[-1, D]], 0, 1, ALU.not_equal, 1.0)
            select(fold[:, :], [[0, D]], 1 - D, 1, ALU.not_equal, -1.0)
            fill(fold[:, D - 1:D], 0.0)
            fill(fold[D:A, D - 1:D], 1.0)
            fill(pickb[:, :], 0.0)
            fill(pickb[:, D - 1::D], 1.0)
            fill(ONE[:, :], 1.0)
            fill(EPSC[:, :], EPS)
            fill(xT[D:A, :], 1.0)
            for pad in (hT0, smT, q0T, qsT):
                fill(pad[:, T:TP], 0.0)
            fill(imgmask[:, :], 1.0)
            select(imgmask[:, :], [[-N, G]], 0, 1, ALU.is_ge, 0.0)
            select(imgmask[:, :], [[N, G]], N - 1, -1, ALU.is_ge, 0.0)
            same3 = same[:, :].rearrange("p (i n) -> p i n", i=G)
            fill(same[:, :], 1.0)
            select(same3, [[-N, G], [0, N]], 0, 1, ALU.is_ge, 0.0)
            select(same3, [[N, G], [0, N]], N - 1, -1, ALU.is_ge, 0.0)
            assert made["const"] == CONSTS
            fill(etx[:, :, :, :], 0.0, "late")
            causal3 = causal[:, :].rearrange("p (i n) -> p i n", i=G)
            for l in range(N):
                fill(causal3[:, :, l:l + 1], 1.0 / max(l, 1), "late")
            select(causal3, [[-N, G], [0, N]], 0, 1, ALU.is_ge, 0.0, "late")
            select(causal3, [[N, G], [1, N]], 0, -1, ALU.is_ge, 0.0, "late")
            for e in range(E):
                fill(rev[:, e:e + 1], float(E - e), "late")
            assert made["late"] == LATE

            for t in range(0, NT, 2):
                pool.wait_ge(s["v_sb"], 1)
                if t >= 2:
                    pool.wait_ge(s["lam_ps"], t - 1)
                nc.gpsimd.tensor_tensor(vexp[:, 0], v0[:, t:t + 1, :].to_broadcast([R, G, D]),
                                        imgmask[:, :].unsqueeze(2).to_broadcast([R, G, D]), ALU.mult).then_inc(s["vexp_p"], 1)

            def weights(t):
                pool.wait_ge(s["s_rec"], t + 1)
                if t >= 2:
                    pool.wait_ge(s["et_ps"], t - 1)
                rt = rows[t]
                nc.gpsimd.tensor_tensor(sw[0:rt, t % 2], sexp[0:rt, t % 2],
                                        srec[0:rt, t, :].unsqueeze(2).to_broadcast([rt, H, S]), ALU.mult).then_inc(s["s_w"], 1)

            def scaled(t):
                for p in range(pairs[t]):
                    pool.wait_ge(s["u_rec"], sum(pairs[0:t]) + p + 1)
                    nc.gpsimd.tensor_tensor(fe[:, t % 2, p], fe[:, t % 2, p],
                                            urec[:, t % 2, p, :].unsqueeze(2).to_broadcast([128, H, S]), ALU.mult).then_inc(s["u_w"], 1)

            for i in range(NT + 2):
                if i < NT:
                    weights(i)
                if i >= 2:
                    scaled(i - 2)

            pool.wait_ge(s["m_ps"], 2 * NT)
            pool.wait_ge(s["w12_in"], 4 * 16)
            for wi, hi in ((w1, w1h), (w2, w2h)):
                nc.gpsimd.tensor_copy(hi[:, :, :], wi[:, :, :]).then_inc(s["w_hi"], 1)
            for j, (wi, hi, lo) in enumerate(((w1, w1h, w1l), (w2, w2h, w2l))):
                pool.wait_ge(s["w_hi"], j + 1)
                nc.gpsimd.tensor_tensor(lo[:, :, :], wi[:, :, :], hi[:, :, :].bitcast(F32), ALU.subtract).then_inc(s["w_lo"], 1)

        @block.vector
        def _(dve):
            def cp(dst, src):
                return nc.vector.tensor_copy(dst, src)

            dve.wait_ge(s["const"], CONSTS)
            dve.wait_ge(s["ident"], 2)
            nc.vector.tensor_tensor(pick[:, :], ident[0:LOW + E, 0:E], ident[0:LOW + E, LOW:LOW + E], ALU.add).then_inc(s["pick"], 1)
            nc.vector.tensor_copy(dispT[0:LOW, :], ident[0:LOW, LOW:LOW + 1].to_broadcast([LOW, TP])).then_inc(s["d_zero"], 1)
            nc.vector.tensor_copy(xS[D // 2:D, :], ONE[D // 2:D, 0:1].to_broadcast([D // 2, TP])).then_inc(s["x_pad"], 1)
            nc.vector.tensor_copy(xS[D + D // 2:2 * D, :], ident[D + D // 2:2 * D, 0:1].to_broadcast([D // 2, TP])).then_inc(s["x_pad"], 1)
            for k in range(1, NCH, 2):
                reorder(k, dve, cp, s["re_odd"])
                dve.wait_ge(s["pix_ps"], k + 1)
                if k >= 2:
                    dve.wait_ge(s["tok_ps"], k - 1)
                cp(pixT[:, 1, :], bank[1][:, :]).then_inc(s["pix_odd"], 1)
            dve.wait_ge(s["small_in"], 2 * 16)
            cp(hT0[:, 0:T].rearrange("p (b n) -> p b n", n=N)[:, :, 0:1],
               cls[:, 0:1].unsqueeze(1).to_broadcast([D, B, 1])).then_inc(s["tok_sb"], 1)
            dve.wait_ge(s["htm_ps"], 1)
            cp(h[:, :, :], bank[3][0:R, 0:NT * D].rearrange("p (t d) -> p t d", t=NT)).then_inc(s["h_upd"], 1)

            def layernorm(k, while_waiting=lambda: None):
                dve.wait_ge(s["h_upd"], k + 1)
                for t in range(NT):
                    nc.vector.bn_stats(lstats[:, t, :], h[:, t, :]).then_inc(s["ln_st"], 1)
                for t in range(NT):
                    dve.wait_ge(s["ln_st"], k * NT + t + 1)
                    nc.vector.bn_aggr(lmv[:, t, :], lstats[:, t, :]).then_inc(s["ln_mv"], 1)
                dve.wait_ge(s["ln_mv"], (k + 1) * NT)
                nc.vector.tensor_tensor(xc[:, :, :], h[:, :, :], lmv[:, :, 0:1].to_broadcast([R, NT, D]),
                                        ALU.subtract).then_inc(s["ln_cen"], 1)
                dve.wait_ge(s["ln_std"], k + 1)
                nc.vector.reciprocal(rstd[:, :], std[:, :]).then_inc(s["ln_rstd"], 1)
                dve.wait_ge(s["ln_rstd"], k + 1)
                dve.wait_ge(s["ln_cen"], k + 1)
                nc.vector.tensor_tensor(xn[:, :, :], xc[:, :, :], rstd[:, :].unsqueeze(2).to_broadcast([R, NT, D]),
                                        ALU.mult).then_inc(s["ln_xn"], 1)
                while_waiting()
                dve.wait_ge(s["ln_ps"], k + 1)
                cp(xT[0:D, FIRST:TP], bank[7][0:D, 0:TP - FIRST]).then_inc(s["ln_xT"], 1)

            layernorm(0)

            for i in range(2):
                dve.wait_ge(s["k_ps"], i + 1)
                nc.vector.tensor_reduce(kmax[:, i * XC:(i + 1) * XC], bank[i][0:D, 0:HALF].rearrange("p (b n) -> p b n", n=N),
                                        AX_X, ALU.max).then_inc(s["k_max"], 1)
                dve.wait_ge(s["k_max"], i + 1)
                nc.vector.tensor_tensor(kexp[:, i * HALF:(i + 1) * HALF].rearrange("p (b n) -> p b n", n=N),
                                        bank[i][0:D, 0:HALF].rearrange("p (b n) -> p b n", n=N),
                                        kmax[:, i * XC:(i + 1) * XC].unsqueeze(2).to_broadcast([D, XC, N]),
                                        ALU.subtract).then_inc(s["k_sub"], 1)
            dve.wait_ge(s["k_exp"], 1)
            kv = kexp[:, :].rearrange("p (b n) -> p b n", n=N)
            nc.vector.tensor_reduce(ksum[:, :], kv, AX_X, ALU.add).then_inc(s["k_sum"], 1)
            dve.wait_ge(s["k_sum"], 1)
            nc.vector.reciprocal(krec[:, :], ksum[:, :]).then_inc(s["k_rec"], 1)
            dve.wait_ge(s["k_rec"], 1)
            nc.vector.tensor_tensor(smT[:, 0:T].rearrange("p (b n) -> p b n", n=N), kv,
                                    krec[:, :].unsqueeze(2).to_broadcast([D, B, N]), ALU.mult).then_inc(s["k_sm"], 1)
            for t in range(NT + 1):
                if t < NT and t % 2:
                    dve.wait_ge(s["v_sb"], 1)
                    if t >= 2:
                        dve.wait_ge(s["lam_ps"], t - 1)
                    nc.vector.tensor_tensor(vexp[:, 1], v0[:, t:t + 1, :].to_broadcast([R, G, D]),
                                            imgmask[:, :].unsqueeze(2).to_broadcast([R, G, D]), ALU.mult).then_inc(s["vexp_d"], 1)
                if t >= 1:
                    dve.wait_ge(s["lam_ps"], t)
                    nc.vector.bn_stats(stats[:, t - 1, :], bank[(t - 1) % 4][0:D, 0:imgs[t - 1] * D]).then_inc(s["bn_st"], 1)
            dve.wait_ge(s["bn_st"], NT)
            nc.vector.bn_aggr(mv[:, :], stats[:, :, :].rearrange("p t s -> p (t s)")).then_inc(s["bn_mv"], 1)
            dve.wait_ge(s["bn_std"], 1)
            nc.vector.reciprocal(bnr[:, :], bnl[:, :]).then_inc(s["bn_rstd"], 1)
            dve.wait_ge(s["bn_rstd"], 1)
            dve.wait_ge(s["norm_in"], 3 * 16)
            nc.vector.tensor_tensor(bna[:, :], gamma[:, :], bnr[:, :], ALU.mult).then_inc(s["bn_a"], 1)
            dve.wait_ge(s["bn_a"], 1)
            nc.vector.tensor_tensor(bnm[:, :], mv[:, 0:1], bna[:, :], ALU.mult).then_inc(s["bn_m"], 1)
            dve.wait_ge(s["bn_m"], 1)
            nc.vector.tensor_tensor(bnc[:, :], beta[:, :], bnm[:, :], ALU.subtract).then_inc(s["bn_c"], 1)
            dve.wait_ge(s["q_sb"], 2)
            nc.vector.tensor_scalar(qsT[:, 0:T], q0T[:, 0:T], bna[:, 0:1], None, ALU.mult).then_inc(s["q_scaled"], 1)

            def split_tokens(j, feats):
                dve.wait_ge(s["ln_ps"], 2 * j + 2)
                cp(xS[0:feats, FIRST:TP], bank[7][0:feats, 0:TP - FIRST]).then_inc(s["x_hi_last"], 1)
                dve.wait_ge(s["x_hi_last"], j + 1)
                nc.vector.tensor_tensor(xS[D:D + feats, FIRST:TP], bank[7][0:feats, 0:TP - FIRST],
                                        xS[0:feats, FIRST:TP].bitcast(F32), ALU.subtract).then_inc(s["x_lo"], 1)
                dve.wait_ge(s["x_hi"], j + 1)
                nc.vector.tensor_tensor(xS[D:D + feats, 0:FIRST], bank[6][0:feats, 0:FIRST],
                                        xS[0:feats, 0:FIRST].bitcast(F32), ALU.subtract).then_inc(s["x_lo"], 1)

            def mask_attention(k):
                for g in range(NG):
                    dve.wait_ge(s["at_ps"], k * NG + g + 1)
                    src = bank[g][0:R, 0:2 * R].rearrange("p (t r) -> p t r", t=2)
                    dst = att[:, 2 * g:2 * g + 2, :]
                    m = (causal if k else same)[:, :].unsqueeze(1).to_broadcast([R, 2, R])
                    if k == 0:
                        i_ = nc.vector.tensor_tensor(dst, src, m, ALU.mult)
                    else:
                        i_ = nc.vector.scalar_tensor_tensor(out=dst, in0=src, scalar=0.0, in1=m, op0=ALU.max, op1=ALU.mult)
                    i_.then_inc(s["at_sb"], 1)

            def residual(k, ps):
                nc.vector.tensor_tensor(h[:, :, :], h[:, :, :], ps[0:R, 0:NT * D].rearrange("p (t d) -> p t d", t=NT),
                                        ALU.add).then_inc(s["h_upd"], 1)

            dve.wait_ge(s["f0_in"], 5 * 16)
            nc.vector.tensor_scalar(rtemp[:, :], temp[:, :], 0.1, 5.0, ALU.max, ALU.min).then_inc(s["rt"], 1)
            dve.wait_ge(s["rt"], 1)
            nc.vector.reciprocal(rtemp[:, :], rtemp[:, :]).then_inc(s["rt"], 1)
            dve.wait_ge(s["rt"], 2)
            dve.wait_ge(s["ws_ps"], 1)
            for i in range(2):
                nc.vector.tensor_tensor(ws[:, i::2, :], bank[6 + i][:, 0:HH * S].rearrange("p (k g) -> p k g", k=HH),
                                        rtemp[:, i::2].unsqueeze(2).to_broadcast([128, HH, S]), ALU.mult).then_inc(s["ws_sb"], 1)
            mask_attention(0)
            dve.wait_ge(s["ws_sb"], 2)
            cp(wsh[:, :, :], ws[:, :, :]).then_inc(s["ws_hi"], 1)
            dve.wait_ge(s["ws_hi"], 1)
            nc.vector.tensor_tensor(wsl[:, :, :], ws[:, :, :], wsh[:, :, :].bitcast(F32), ALU.subtract).then_inc(s["ws_lo"], 1)

            def folded_low():
                for i in range(2):
                    dve.wait_ge(s["gram_hi"], i + 1)
                    nc.vector.tensor_tensor(graml[:, i::2, :], bank[i][:, :].rearrange("p (k d) -> p k d", k=HH),
                                            gramh[:, i::2, :].bitcast(F32), ALU.subtract).then_inc(s["gram_sb"], 1)

            def values_low():
                for i in range(2):
                    dve.wait_ge(s["vo_hi"], i + 1)
                    nc.vector.tensor_tensor(vol[:, i::2, :], bank[5 + i][:, 0:HH * D].rearrange("p (k d) -> p k d", k=HH),
                                            voh[:, i::2, :].bitcast(F32), ALU.subtract).then_inc(s["vo_sb"], 1)

            dve.wait_ge(s["ao_ps"], 1)
            residual(0, bank[5])
            layernorm(1, folded_low)

            split_tokens(0, D - 1)

            def product_parts(n):
                i, hd = divmod(n, H)
                dve.wait_ge(s["t1_hi"], n + 1)
                nc.vector.tensor_tensor(t1l[:, hd, i * HALF:(i + 1) * HALF], bank[3 + n % 4][:, 0:HALF],
                                        t1h[:, hd, i * HALF:(i + 1) * HALF].bitcast(F32), ALU.subtract).then_inc(s["t1_lo"], 1)

            def slice_softmax(t):
                rt = rows[t]
                ps = bank[0][0:rt, :].rearrange("p (h g) -> p h g", h=H)
                dve.wait_ge(s["s_ps"], t + 1)
                nc.vector.tensor_reduce(smax[0:rt, t, :], ps, AX_X, ALU.max).then_inc(s["s_max"], 1)
                dve.wait_ge(s["s_max"], t + 1)
                if t >= 2:
                    dve.wait_ge(s["s_w"], t - 1)
                nc.vector.tensor_tensor(sexp[0:rt, t % 2], ps, smax[0:rt, t, :].unsqueeze(2).to_broadcast([rt, H, S]),
                                        ALU.subtract).then_inc(s["s_sub"], 1)

            def slice_sum(t):
                rt = rows[t]
                dve.wait_ge(s["s_exp"], t + 1)
                nc.vector.tensor_reduce(ssum[0:rt, t, :], sexp[0:rt, t % 2], AX_X, ALU.add).then_inc(s["s_sum"], 1)
                dve.wait_ge(s["s_sum"], t + 1)
                nc.vector.reciprocal(srec[0:rt, t, :], ssum[0:rt, t, :]).then_inc(s["s_rec"], 1)

            def norms(t):
                rt, im = rows[t], imgs[t]
                ps = bank[3][:, 0:HH * R].rearrange("p (k i n) -> p k i n", k=HH, i=G)[:, :, 0:im, :]
                dve.wait_ge(s["et_ps"], t + 1)
                nc.vector.tensor_reduce(nsum[:, t % 2, :, 0:im], ps, AX_X, ALU.add).then_inc(s["n_sum"], 1)
                dve.wait_ge(s["n_sum"], t + 1)
                nc.vector.tensor_scalar(nsum[:, t % 2, :, 0:im], nsum[:, t % 2, :, 0:im], EPS, None, ALU.add).then_inc(s["n_eps"], 1)
                dve.wait_ge(s["n_eps"], t + 1)
                nc.vector.reciprocal(nrec[:, t % 2, :, 0:im], nsum[:, t % 2, :, 0:im]).then_inc(s["n_rec"], 1)
                dve.wait_ge(s["n_rec"], t + 1)
                if t >= 3:
                    dve.wait_ge(s["p_ps"], 2 * (t - 2))
                nc.vector.tensor_tensor(snT[:, t % 3, :, 0:rt].rearrange("p k (i n) -> p k i n", n=N), ps,
                                        nrec[:, t % 2, :, 0:im].unsqueeze(3).to_broadcast([128, HH, im, N]), ALU.mult).then_inc(s["snT_sb"], 1)

            def mask_pairs(ps_sem, dst, heads_of, sb_sem, t, used):
                rt = rows[t]
                if t >= 2:
                    dve.wait_ge(used, t - 1)
                for i in range(2):
                    dve.wait_ge(ps_sem, 2 * t + i + 1)
                    nc.vector.tensor_tensor(
                        dst[0:rt, t % 2, heads_of[i], 0:rt],
                        bank[1 + i][0:rt, 0:HH * R].rearrange("p (k r) -> p k r", k=HH)[:, :, 0:rt],
                        same[0:rt, 0:rt].unsqueeze(1).to_broadcast([rt, HH, rt]), ALU.mult).then_inc(sb_sem, 1)

            def slice_attention_softmax(t, p):
                if 0 <= t < NT and p < pairs[t]:
                    u = sum(pairs[0:t]) + p
                    ps = bank[5 + u % 2][:, :].rearrange("p (h g) -> p h g", h=H)
                    dve.wait_ge(s["l_ps"], u + 1)
                    nc.vector.tensor_reduce(umax[:, t, p, :], ps, AX_X, ALU.max).then_inc(s["u_max"], 1)
                    dve.wait_ge(s["u_max"], u + 1)
                    if u >= 2:
                        dve.wait_ge(s["u_exp"], u - 1)
                    nc.vector.tensor_tensor(lg[:, u % 2], ps, umax[:, t, p, :].unsqueeze(2).to_broadcast([128, H, S]),
                                            ALU.subtract).then_inc(s["u_sub"], 1)

            def slice_attention_sum(t, p):
                if 0 <= t < NT and p < pairs[t]:
                    u = sum(pairs[0:t]) + p
                    dve.wait_ge(s["u_exp"], u + 1)
                    nc.vector.tensor_reduce(usum[:, t % 2, p, :], fe[:, t % 2, p], AX_X, ALU.add).then_inc(s["u_sum"], 1)
                    dve.wait_ge(s["u_sum"], u + 1)
                    nc.vector.reciprocal(urec[:, t % 2, p, :], usum[:, t % 2, p, :]).then_inc(s["u_rec"], 1)

            for i in range(NT + 3):
                if i < NT:
                    slice_softmax(i)
                if i == 0:
                    product_parts(0)
                    product_parts(1)
                slice_attention_softmax(i - 2, 0)
                if i < NT:
                    slice_sum(i)
                if i == 0:
                    for n in range(2, 2 * H):
                        product_parts(n)
                slice_attention_softmax(i - 2, 1)
                slice_attention_sum(i - 2, 0)
                if i >= 3:
                    mask_pairs(s["p_ps"], pT, (slice(0, H, 2), slice(1, H, 2)), s["p_sb"], i - 3, s["o_ps"])
                slice_attention_softmax(i - 2, 2)
                if i == 1:
                    values_low()
                if i < 3:
                    mask_pairs(s["m_ps"], mm, (slice(0, HH), slice(HH, H)), s["m_sb"], i, s["z_ps"])
                    norms(i)
                slice_attention_sum(i - 2, 1)
                if 3 <= i < NT:
                    norms(i)
                slice_attention_sum(i - 2, 2)
                if 3 <= i < NT:
                    mask_pairs(s["m_ps"], mm, (slice(0, HH), slice(HH, H)), s["m_sb"], i, s["z_ps"])
            dve.wait_ge(s["ot_ps"], 1)
            residual(1, bank[5])
            layernorm(2)

            dve.wait_ge(s["late"], LATE)
            mask_attention(1)
            dve.wait_ge(s["ao_ps"], 2)
            residual(2, bank[5])
            layernorm(3)

            split_tokens(1, D)

            def hidden(n):
                dve.wait_ge(s["e_silu"], n + 1)
                dve.wait_ge(s["e2_ps"], n + 1)
                nc.vector.tensor_tensor(hid[:, n % RING, :], silu[:, n % RING, :], bank[2 + n % 2][:, 0:HALF], ALU.mult).then_inc(s["e_hid"], 1)

            steps = [0]

            def step(ins):
                steps[0] += 1
                ins.then_inc(s["g_step"], 1)
                dve.wait_ge(s["g_step"], steps[0])

            gps = bank[3][0:R, 0:NT * E].rearrange("p (t e) -> p t e", t=NT)

            def over(a):
                return a[:, :].unsqueeze(2).to_broadcast([R, NT, E])

            ranks = rev[:, :].unsqueeze(1).to_broadcast([R, NT, E])
            dve.wait_ge(s["g_ps"], 1)
            step(nc.vector.tensor_reduce(gmax[:, :], gps, AX_X, ALU.max))
            nc.vector.tensor_tensor(gd[:, :, :], gps, over(gmax), ALU.subtract).then_inc(s["g_sub"], 1)
            dve.wait_ge(s["g_sub"], 1)
            step(nc.vector.scalar_tensor_tensor(out=gc[:, :, :], in0=gd[:, :, :], scalar=0.0, in1=ranks, op0=ALU.is_ge, op1=ALU.mult))
            step(nc.vector.tensor_reduce(gr[:, :], gc[:, :, :], AX_X, ALU.max))
            step(nc.vector.tensor_tensor(gs1[:, :, :], gc[:, :, :], over(gr), ALU.is_equal))
            step(nc.vector.scalar_tensor_tensor(out=gd2[:, :, :], in0=gs1[:, :, :], scalar=-1e30, in1=gd[:, :, :], op0=ALU.mult, op1=ALU.add))
            step(nc.vector.tensor_reduce(gr[:, :], gd2[:, :, :], AX_X, ALU.max))
            step(nc.vector.tensor_tensor(gs2[:, :, :], gd2[:, :, :], over(gr), ALU.is_equal))
            hidden(0)
            step(nc.vector.tensor_tensor(gc[:, :, :], gs2[:, :, :], ranks, ALU.mult))
            step(nc.vector.tensor_reduce(gr[:, :], gc[:, :, :], AX_X, ALU.max))
            step(nc.vector.tensor_tensor(gs2[:, :, :], gc[:, :, :], over(gr), ALU.is_equal))
            step(nc.vector.tensor_tensor(gs2[:, :, :], gs1[:, :, :], gs2[:, :, :], ALU.add))
            hidden(1)
            dve.wait_ge(s["g_exp"], 1)
            step(nc.vector.tensor_tensor(gw[:, :, :], gs2[:, :, :], ge[:, :, :], ALU.mult))
            step(nc.vector.tensor_reduce(gr[:, :], gw[:, :, :], AX_X, ALU.add))
            step(nc.vector.reciprocal(gr[:, :], gr[:, :]))
            nc.vector.tensor_tensor(gw[:, :, :], gw[:, :, :], over(gr), ALU.mult).then_inc(s["g_disp"], 1)

            def weighted(n):
                dve.wait_ge(s["e_hid"], n + 1)
                dve.wait_ge(s["db_ps"], n + 1)
                if n >= RING:
                    dve.wait_ge(s["e_out"], n - RING + 1)
                nc.vector.tensor_tensor(hidw[:, n % RING, :], hid[:, n % RING, :], bank[4 + n % 2][:, 0:HALF], ALU.mult).then_inc(s["e_w"], 1)

            hidden(2)
            dve.wait_ge(s["d_sb"], 2)
            nc.vector.tensor_tensor(dispT[LOW:LOW + E, 0:FIRST], bank[4][0:E, 0:FIRST], dispT[0:E, 0:FIRST].bitcast(F32), ALU.subtract).then_inc(s["d_lo"], 1)
            nc.vector.tensor_tensor(dispT[LOW:LOW + E, FIRST:TP], bank[5][0:E, 0:TP - FIRST], dispT[0:E, FIRST:TP].bitcast(F32), ALU.subtract).then_inc(s["d_lo"], 1)
            for n in range(2 * E):
                weighted(n)
                if n + AHEAD < 2 * E:
                    hidden(n + AHEAD)
            dve.wait_ge(s["e_fin"], 1)
            nc.vector.tensor_tensor(xn[:, :, :], h[:, :, :], bank[0][0:R, 0:NT * D].rearrange("p (t d) -> p t d", t=NT),
                                    ALU.add).then_inc(s["e_res"], 1)

        @block.tensor
        def _(pe):
            def mm_(o, l, r, start=True, stop=True):
                return nc.tensor.matmul(o, l, r, start=start, stop=stop)

            def tr(o, i, n):
                return nc.tensor.transpose(o, i, ident[0:n, 0:n])

            def keep_clock(b_, n):
                for _ in range(n):
                    mm_(bank[b_][:, 0:128], ident[:, :], ident[:, :])

            pe.wait_ge(s["ident"], 2)
            keep_clock(3, 5)
            pe.wait_ge(s["tokw_in"], 16)
            for k in range(NCH):
                last = tr(bank[0][:, k * D:(k + 1) * D], tokw[:, k * 128:(k + 1) * 128], D)
            last.then_inc(s["tokwT_ps"], 1)
            heads = [(hd // 2, slice((hd % 2) * D, (hd % 2 + 1) * D)) for hd in range(H)]

            def once(w):
                return w.rearrange("p a d -> p (a d)")

            def fold_first():
                pe.wait_ge(s["fx_in"], 6 * 16)
                pe.wait_ge(s["const"], CONSTS)
                for b_, w in ((4, wfx_a), (5, wx_a)):
                    for k in range(HH):
                        last = mm_(bank[b_][:, k * D:(k + 1) * D], w[:, k * 128:(k + 1) * 128], fold[:, :])
                    last.then_inc(s["wT_ps"], 1)
                tr(bank[0][:, 0:D], wv2[:, :, :].rearrange("p a d -> p (a d)"), D).then_inc(s["wT_ps"], 1)

            def fold_second():
                pe.wait_ge(s["ab_in"], 5 * 16)
                pe.wait_ge(s["wT_sb"], 3)
                for b_, w in ((4, wq2), (5, wk2)):
                    for k, half in heads:
                        last = mm_(bank[b_][half, k * D:(k + 1) * D], w[half, :], wfxT[half, k, 0, :])
                    last.then_inc(s["ab_ps"], 1)

            def fold_out():
                pe.wait_ge(s["h_upd"], 1)
                for k, half in heads:
                    last = mm_(bank[3][half, k * D:(k + 1) * D], wvT[half, :], wout[half, k, :])
                last.then_inc(s["wvo_ps"], 1)

            def fold_logits():
                pe.wait_ge(s["f0_in"], 5 * 16)
                for i in range(2):
                    half = slice(i * D, (i + 1) * D)
                    mm_(bank[6 + i][:, 0:HH * S], pickb[i * D:i * D + 1, :],
                        bslice[i * D:i * D + 1, :].unsqueeze(1).to_broadcast([1, HH, S]), True, False)
                    for k in range(HH):
                        last = mm_(bank[6 + i][:, k * S:(k + 1) * S], once(wxT[half, k, :, :]), wslice[half, :], False, k == HH - 1)
                last.then_inc(s["ws_ps"], 1)

            def fold_grams():
                for hd, (k, half) in enumerate(heads):
                    last = mm_(bank[hd % 2][:, k * 2 * D:(k + 1) * 2 * D], once(kT[half, k, :, :]), once(qT[half, k, :, :]))
                last.then_inc(s["gram_ps"], 1)

            def fold_values():
                pe.wait_ge(s["wvo_sb"], 1)
                for hd, (k, half) in enumerate(heads):
                    last = mm_(bank[5 + hd % 2][:, k * D:(k + 1) * D], once(wfxT[half, k, :, :]), wvo[half, k, :])
                last.then_inc(s["vo_ps"], 1)

            def fold_layer1():
                pe.wait_ge(s["l1_in"], 6 * 16)
                pe.wait_ge(s["u_sub"], sum(pairs))
                mm_(bank[5][0:D, 0:D], l1q[:, :], l1k[:, :])
                tr(bank[5][0:D, D:2 * D], l1o[:, :], D).then_inc(s["l1_ps"], 1)

            def fold_layer1_values():
                pe.wait_ge(s["l1_sb"], 2)
                pe.wait_ge(s["h_upd"], 3)
                mm_(bank[5][0:D, 0:D], l1v[:, :], l1oT[:, :]).then_inc(s["l1b_ps"], 1)

            keep_clock(3, 5)
            pe.wait_ge(s["tokwT_sb"], 1)
            def pixels(k):
                return s["pix_odd"] if k % 2 else s["pix_even"]

            for k in range(NCH + 1):
                if k < NCH:
                    pe.wait_ge(s["re_odd"] if k % 2 else s["re_even"], k // 2 + 1)
                    if k >= 2:
                        pe.wait_ge(pixels(k - 2), (k - 2) // 2 + 1)
                    for w in range(HP):
                        last = tr(bank[k % 2][:, w * 128:(w + 1) * 128], xre[:, k % 2, w * 128:(w + 1) * 128], 128)
                    last.then_inc(s["pix_ps"], 1)
                if k >= 1:
                    pe.wait_ge(pixels(k - 1), (k - 1) // 2 + 1)
                    mm_(bank[2][0:D, :], tokwT[:, k - 1, :], pixT[:, (k - 1) % 2, :], k == 1, k == NCH).then_inc(s["tok_ps"], 1)
            pe.wait_ge(s["pix_even"], NCH // 2)
            fold_first()
            pe.wait_ge(s["tok_sb"], HP + 1)
            for t in range(NT):
                last = tr(bank[3][0:R, t * D:(t + 1) * D], hT0[:, t * R:(t + 1) * R], D)
            last.then_inc(s["htm_ps"], 1)

            def layernorm(k):
                keep_clock(7, NORM_FILL[k])
                pe.wait_ge(s["ln_xn"], k + 1)
                for t in range(NT):
                    b_, c0 = (6, t * R) if t < NT - 1 else (7, 0)
                    last = tr(bank[b_][0:D, c0:c0 + R], xn[:, t, :], R)
                last.then_inc(s["ln_ps"], 1)
                pe.wait_ge(s["ln_xT"], 2 * (k + 1))

            fold_second()
            layernorm(0)
            fold_out()

            pe.wait_ge(s["a0_in"], 6 * 16)
            for i in range(2):
                mm_(bank[i][0:D, 0:HALF], wk_a[:, :], xT[:, i * HALF:(i + 1) * HALF]).then_inc(s["k_ps"], 1)
            pe.wait_ge(s["ab_sb"], 2)
            for t in range(NT):
                last = mm_(bank[4][0:R, t * D:(t + 1) * D], xT[:, t * R:(t + 1) * R], wv_a[:, :])
            last.then_inc(s["v_ps"], 1)
            pe.wait_ge(s["wvo_sb"], 1)
            for i in range(2):
                mm_(bank[2 + i][0:D, 0:HALF], wq_a[:, :], xT[:, i * HALF:(i + 1) * HALF]).then_inc(s["q_ps"], 1)
            pe.wait_ge(s["k_sm"], 1)
            for t in range(NT):
                last = tr(bank[5][0:R, t * D:(t + 1) * D], smT[:, t * R:(t + 1) * R], D)
            last.then_inc(s["sm_ps"], 1)
            pe.wait_ge(s["sm_sb"], 1)
            pe.wait_ge(s["q_sb"], 2)
            for t in range(NT):
                if t % 2:
                    pe.wait_ge(s["vexp_d"], t // 2 + 1)
                else:
                    pe.wait_ge(s["vexp_p"], t // 2 + 1)
                if t >= 4:
                    pe.wait_ge(s["bn_st"], t - 3)
                mm_(bank[t % 4][0:D, 0:imgs[t] * D], sm[:, t, :],
                    vexp[:, t % 2, 0:imgs[t], :]).then_inc(s["lam_ps"], 1)
            fold_logits()
            pe.wait_ge(s["bn_st"], NT)
            pe.wait_ge(s["q_scaled"], 1)

            def attention(left, right):
                for t in range(NT):
                    last = mm_(bank[t // 2][0:R, t % 2 * R:(t % 2 + 1) * R], left[0:D, t * R:(t + 1) * R], right[0:D, t * R:(t + 1) * R])
                    if t % 2:
                        last.then_inc(s["at_ps"], 1)

            attention(smT, qsT)
            for t in range(NT):
                mm_(bank[5][0:R, t * D:(t + 1) * D], q0T[:, t * R:(t + 1) * R], bnc[:, 0:1].to_broadcast([D, D]), t == 0, False)
            for t in range(NT):
                pe.wait_ge(s["at_sb"], t // 2 + 1)
                last = mm_(bank[5][0:R, t * D:(t + 1) * D], att[:, t, :], v0[:, t, :], False, t == NT - 1)
            last.then_inc(s["ao_ps"], 1)
            fold_grams()
            pe.wait_ge(s["ws_sb"], 2)
            layernorm(1)

            def flat(w):
                return w[:, :, :].rearrange("p h d -> p (h d)")

            def token_product_operands():
                for n in range(2 * H):
                    i, hd = divmod(n, H)
                    if n >= 4:
                        pe.wait_ge(s["t1_lo"], n - 3)
                    cols = slice(i * HALF, (i + 1) * HALF)
                    mm_(bank[3 + n % 4][:, 0:HALF], gramh[:, hd, :], xS[:, cols], True, False)
                    mm_(bank[3 + n % 4][:, 0:HALF], graml[:, hd, :], xS[:, cols], False, True).then_inc(s["t1_ps"], 1)
                pe.wait_ge(s["t1_lo"], 2 * H)

            pe.wait_ge(s["x_lo"], 2)
            pe.wait_ge(s["ws_lo"], 1)

            def slots(t):
                return slice(t * R, t * R + rows[t])

            def slice_logits(t):
                if t >= 1:
                    pe.wait_ge(s["s_sub"], t)
                if t >= 4:
                    pe.wait_ge(s["vo_sb2"], t - 3)
                mm_(bank[0][0:rows[t], :], xS[:, slots(t)], flat(wsh), True, False)
                mm_(bank[0][0:rows[t], :], xS[:, slots(t)], flat(wsl), False, True).then_inc(s["s_ps"], 1)

            def weights_T(t):
                rt = rows[t]
                pe.wait_ge(s["s_w"], t + 1)
                if t >= 3:
                    pe.wait_ge(s["r_sb"], t - 2)
                elif t >= 1:
                    pe.wait_ge(s["et_sb"], 4 * t)
                for k in range(HH):
                    last = tr(bank[3][:, k * R:k * R + rt], sw[0:rt, t % 2, 2 * k:2 * k + 2, :].rearrange("p h g -> p (h g)"), rt)
                last.then_inc(s["et_ps"], 1)

            def token_products(t):
                rt = rows[t]
                if t >= 3:
                    pe.wait_ge(s["p_sb"], 2 * (t - 2))
                elif t >= 1:
                    pe.wait_ge(s["m_sb"], 2 * t)
                for i in range(2):
                    o = bank[1 + i][0:rt, 0:HH * R].rearrange("p (k r) -> p k r", k=HH)[:, :, 0:rt]
                    mm_(o, xS[:, slots(t)], t1h[:, i * HH:(i + 1) * HH, slots(t)], True, False)
                    mm_(o, xS[:, slots(t)], t1l[:, i * HH:(i + 1) * HH, slots(t)], False, True).then_inc(s["m_ps"], 1)

            def z(t):
                rt = rows[t]
                pe.wait_ge(s["s_n"], t + 1)
                pe.wait_ge(s["m_sb"], 2 * (t + 1))
                if t >= 1:
                    pe.wait_ge(s["z_sb"], sum(imgs[0:t]))
                for hd in range(H):
                    last = mm_(bank[7][0:rt, hd * S:(hd + 1) * S], mm[0:rt, t % 2, hd, 0:rt], sn[0:rt, t % 2, hd, :])
                last.then_inc(s["z_ps"], 1)

            def slices(t):
                rt = rows[t]
                if t >= 3:
                    pe.wait_ge(s["o_sb"], t - 2)
                elif t >= 1:
                    pe.wait_ge(s["s_n"], t)
                keep_clock(4, SLICES_FILL[min(t, 3)])
                pe.wait_ge(s["snT_sb"], t + 1)
                for k in range(HH):
                    last = tr(bank[4][0:rt, k * 2 * S:(k + 1) * 2 * S], snT[:, t % 3, k, 0:rt], 128)
                last.then_inc(s["sn_ps"], 1)

            def logits(t, p):
                if 0 <= t < NT and p < pairs[t]:
                    rt = rows[t]
                    pe.wait_ge(s["z_sb"], sum(imgs[0:t]) + 2 * p + 2)
                    u = sum(pairs[0:t]) + p
                    if u >= 2:
                        pe.wait_ge(s["u_sub"], u - 1)
                    for hd in range(H):
                        for j in range(2):
                            last = mm_(bank[5 + u % 2][j * S:(j + 1) * S, hd * S:(hd + 1) * S],
                                       zx[0:rt, t % 2, 2 * p + j, hd * S:(hd + 1) * S], sn[0:rt, t % 2, hd, :])
                    last.then_inc(s["l_ps"], 1)

            def project_values(t):
                if t + 3 < NT:
                    pe.wait_ge(s["s_sub"], t + 4)
                else:
                    pe.wait_ge(s["s_sub"], NT)
                if t >= 1:
                    pe.wait_ge(s["vo_sb2"], t)
                mm_(bank[0][0:rows[t], :], xS[:, slots(t)], flat(voh), True, False)
                mm_(bank[0][0:rows[t], :], xS[:, slots(t)], flat(vol), False, True).then_inc(s["vo_ps2"], 1)

            def r(t):
                pe.wait_ge(s["et_sb"], 4 * min(t + 3, NT))
                if t >= 1:
                    pe.wait_ge(s["r_sb"], t)
                keep_clock(3, SOFTMAX_FILL[t])
                pe.wait_ge(s["u_w"], sum(pairs[0:t + 1]))
                for p in range(pairs[t]):
                    for hd, (k, half) in enumerate(heads):
                        c0 = k * R + p * 2 * N
                        last = mm_(bank[3][half, c0:c0 + 2 * N], fe[:, t % 2, p, hd, :], etx[:, t % 3, hd, p * 2 * N:(p + 1) * 2 * N])
                last.then_inc(s["r_ps"], 1)

            def products_back(t):
                rt = rows[t]
                pe.wait_ge(s["m_sb"], 2 * min(t + 3, NT))
                if t >= NT - 2:
                    keep_clock(2, 3)
                pe.wait_ge(s["r_sb"], t + 1)
                for i in range(2):
                    for k, half in heads[i::2]:
                        last = mm_(bank[1 + i][0:rt, k * R:k * R + rt], snT[half, t % 3, k, 0:rt], rT[half, t % 2, k, 0:rt])
                    last.then_inc(s["p_ps"], 1)

            def output(t):
                rt = rows[t]
                pe.wait_ge(s["vo_sb2"], t + 1)
                pe.wait_ge(s["s_n"], min(t + 3, NT))
                if t >= NT - 2:
                    keep_clock(4, 3)
                for i in range(2):
                    pe.wait_ge(s["p_sb"], 2 * t + i + 1)
                    for hd in range(i, H, 2):
                        last = mm_(bank[4][0:D, 0:rt], vox[0:rt, t % 2, hd, :], pT[0:rt, t % 2, hd, 0:rt], hd == 0, hd == H - 1)
                last.then_inc(s["o_ps"], 1)

            for i in range(NT + 3):
                if i < NT:
                    slice_logits(i)
                if i == 0:
                    token_product_operands()
                if i == 2:
                    pe.wait_ge(s["vo_sb"], 2)
                if i == NT + 2:
                    fold_layer1()
                logits(i - 2, 0)
                if 0 <= i - 1 < NT:
                    slices(i - 1)
                if i < 3:
                    if 0 <= i - 1 < NT:
                        z(i - 1)
                    if i == 1:
                        fold_values()
                    logits(i - 2, 1)
                else:
                    logits(i - 2, 1)
                    r(i - 3)
                    if i - 1 < NT:
                        z(i - 1)
                if i >= 3:
                    products_back(i - 3)
                    project_values(i - 3)
                logits(i - 2, 2)
                if i < 3:
                    token_products(i)
                if i < NT:
                    weights_T(i)
                if i >= 3:
                    output(i - 3)
                if 3 <= i < NT:
                    token_products(i)
            pe.wait_ge(s["o_sb"], NT)
            pe.wait_ge(s["l1_sb"], 2)
            for t in range(NT):
                last = tr(bank[5][0:R, t * D:(t + 1) * D], hT0[:, t * R:(t + 1) * R], D)
            last.then_inc(s["ot_ps"], 1)
            fold_layer1_values()
            layernorm(2)

            for i in range(2):
                mm_(bank[i][0:D, 0:HALF], g1[:, :], xT[0:D, i * HALF:(i + 1) * HALF]).then_inc(s["t_ps"], 1)
            pe.wait_ge(s["l1b_sb"], 1)
            for t in range(NT):
                last = mm_(bank[4][0:R, t * D:(t + 1) * D], xT[0:D, t * R:(t + 1) * R], vo1[:, :])
            last.then_inc(s["v_ps"], 1)
            pe.wait_ge(s["t_sb"], 2)
            attention(xT, qsT)
            pe.wait_ge(s["v_sb"], 2)
            for t in range(NT):
                pe.wait_ge(s["at_sb"], NG + t // 2 + 1)
                last = mm_(bank[5][0:R, t * D:(t + 1) * D], att[:, t, :], vt1[:, t, :])
            last.then_inc(s["ao_ps"], 1)
            layernorm(3)

            for t in range(NT):
                last = mm_(bank[3][0:R, t * E:(t + 1) * E], xT[:, t * R:(t + 1) * R], gate_a[:, :])
            last.then_inc(s["g_ps"], 1)
            pe.wait_ge(s["w_lo"], 2)
            pe.wait_ge(s["x_lo"], 4)

            def columns(n):
                return slice(n % 2 * HALF, (n % 2 + 1) * HALF)

            def up(n):
                if n >= 2:
                    pe.wait_ge(s["e_silu"], n - 1)
                    pe.wait_ge(s["e_hid"], n - 1)
                for b_, hi, lo, done in ((n % 2, w1h, w1l, "e1_ps"), (2 + n % 2, w2h, w2l, "e2_ps")):
                    mm_(bank[b_][:, 0:HALF], hi[:, n // 2, :], xS[:, columns(n)], True, False)
                    mm_(bank[b_][:, 0:HALF], lo[:, n // 2, :], xS[:, columns(n)], False, True).then_inc(s[done], 1)

            def dispatch(n):
                if n >= 2:
                    pe.wait_ge(s["e_w"], n - 1)
                e = n // 2
                mm_(bank[4 + n % 2][:, 0:HALF], pick[:, e:e + 1].to_broadcast([LOW + E, HID]), dispT[:, columns(n)]).then_inc(s["db_ps"], 1)

            def down(n):
                e, i = divmod(n, 2)
                pe.wait_ge(s["e_w"], n + 1)
                mm_(bank[6 + i][0:D, 0:HALF], w3[:, e, :], hidw[:, n % RING, :], e == 0, e == E - 1).then_inc(s["e_out"], 1)

            up(0)
            pe.wait_ge(s["g_sub"], 1)
            up(1)
            for n in range(2, AHEAD):
                up(n)
            keep_clock(4, 4)
            pe.wait_ge(s["g_disp"], 1)
            for t in range(NT):
                b_, c0 = (4, t * R) if t < NT - 1 else (5, 0)
                last = tr(bank[b_][0:E, c0:c0 + R], gw[:, t, :], R)
            last.then_inc(s["d_ps"], 1)
            pe.wait_ge(s["moe_in"], 16)
            pe.wait_ge(s["pick"], 1)
            pe.wait_ge(s["d_lo"], 2)
            for n in range(2 * E):
                dispatch(n)
                if n + AHEAD < 2 * E:
                    up(n + AHEAD)
                if n >= 1:
                    down(n - 1)
            down(2 * E - 1)
            pe.wait_ge(s["e_outT"], 2)
            for t in range(NT):
                last = tr(bank[0][0:R, t * D:(t + 1) * D], hT0[:, t * R:(t + 1) * R], D)
            last.then_inc(s["e_fin"], 1)


_INS = ['x', 'cls_tok', 'L0_tok_W', 'L0_tok_b', 'L0_attn_W_qk', 'L0_attn_b_qk', 'L0_attn_W_v', 'L0_attn_b_v',
        'L0_attn_gamma', 'L0_attn_beta', 'L0_ffn_W_fx', 'L0_ffn_b_fx', 'L0_ffn_W_x', 'L0_ffn_b_x', 'L0_ffn_W_slice',
        'L0_ffn_b_slice', 'L0_ffn_W_q', 'L0_ffn_W_k', 'L0_ffn_W_v', 'L0_ffn_W_out', 'L0_ffn_b_out',
        'L0_ffn_temperature', 'L1_attn_Wq', 'L1_attn_Wk', 'L1_attn_Wv', 'L1_attn_Wo', 'L1_ffn_gate_w',
        'L1_ffn_gate_b', 'L1_ffn_w1', 'L1_ffn_w2', 'L1_ffn_w3']
_OUTS = [((32, 17, 64), 'float32')]


def kernel(**inputs):
    import numpy as _np
    import concourse.bacc as _bacc
    from concourse import mybir as _mybir
    from concourse.bass_utils import run_bass_kernel_spmd as _run

    nc = _bacc.Bacc("TRN2", target_bir_lowering=False, num_devices=1)
    arrays, args = {}, []
    for name in _INS:
        a = _np.ascontiguousarray(inputs[name])
        arrays[f"in_{name}_dram"] = a
        args.append(nc.dram_tensor(f"in_{name}_dram", a.shape, _mybir.dt.from_np(a.dtype), kind="ExternalInput").ap())
    for i, (shape, dtype) in enumerate(_OUTS):
        dt = _mybir.dt.from_np(_np.dtype(dtype))
        args.append(nc.dram_tensor(f"out_{i}_dram", shape, dt, kind="ExternalOutput").ap())
    vit_tower_kernel(nc, *args)
    r = _run(nc, [arrays], core_ids=[0])
    got = tuple(r.results[0][f"out_{i}_dram"] for i in range(len(_OUTS)))
    return got[0]
```
